# Optimizing a Trainium2 kernel written in Bass

```python
import numpy as np
import jax
import jax.numpy as jnp

def _softmax(x, axis=-1):
    return jax.nn.softmax(x, axis=axis)

def _gelu(x):
    return jax.nn.gelu(x, approximate=True)

def _silu(x):
    return jax.nn.silu(x)

def _sigmoid(x):
    return jax.nn.sigmoid(x)

def _layernorm(x, axis=-1, eps=1e-05):
    m = jnp.mean(x, axis=axis, keepdims=True)
    v = jnp.var(x, axis=axis, keepdims=True)
    return (x - m) / jnp.sqrt(v + eps)

def _scatter_add(tgt, idx, src, axis=0):
    return tgt.at[idx].add(src)

def _segment_sum(src, seg, n):
    return jax.ops.segment_sum(src, seg, n)
kernel_name = 'mk_flamingo_gated_d4_seqx_r8_d9751e'

def setup_inputs(seed: int=0):
    np.random.seed(seed)
    _w = jnp.asarray

    def _rec_inputs():
        import jax
        import jax.numpy as jnp
        _rk = jax.random.key(seed)
        x = -0.0001661 + 0.9999 * jax.random.normal(jax.random.fold_in(_rk, 1), (16, 64, 256), jnp.float32)
        _lenS = 64 - jax.random.randint(jax.random.fold_in(_rk, 7), (16,), 0, max(1, 64 // 4) + 1, jnp.int32)
        _lenS2 = 64 - jax.random.randint(jax.random.fold_in(_rk, 8), (16,), 0, max(1, 64 // 4) + 1, jnp.int32)
        _ctx_2048P = jax.random.normal(jax.random.fold_in(_rk, 11), (16, 16, 256), jnp.float32)
        _ctx_2048c = jax.random.dirichlet(jax.random.fold_in(_rk, 511), 0.3 * jnp.ones((16,), jnp.float32), (16, 64))
        _ctx_2048t = jnp.einsum('bsk,bkd->bsd', _ctx_2048c, _ctx_2048P)
        _ctx_2048t = _ctx_2048t * jax.lax.rsqrt(jnp.mean(jnp.square(_ctx_2048t)) + 1e-12) * 0.953939
        ctx_2048 = -0.00016346 + 1.00032 * (_ctx_2048t + 0.3 * jax.random.normal(jax.random.fold_in(_rk, 611), (16, 64, 256), jnp.float32))
        _validS = jnp.arange(64)[None, :] < _lenS[:, None]
        _validS2 = jnp.arange(64)[None, :] < _lenS2[:, None]
        _causal = jnp.tril(jnp.ones((64, 64), dtype=bool))
        mask_BxS2_bk0 = jnp.logical_not(jnp.broadcast_to(_validS2[:, :], (16, 64)))
        mask_BxS2_ik0 = jnp.where(jnp.broadcast_to(_validS2[:, :], (16, 64)), 0, 1).astype(jnp.int32)
        _g = jax.random.normal(jax.random.fold_in(_rk, 9001), (2, 4), jnp.float32)
        _g = jnp.sign(_g) * jnp.maximum(jnp.abs(_g), 1.0) + (_g == 0) * 1.0
        g_xattn = _g[0]
        g_ffn = _g[1]
        return (x, ctx_2048, _lenS2, mask_BxS2_bk0, mask_BxS2_ik0, g_xattn, g_ffn)
    x, ctx_2048, _lenS2, mask_BxS2_bk0, mask_BxS2_ik0, g_xattn, g_ffn = _rec_inputs()

    def _L0_xattn_setup():
        import jax, jax.numpy as jnp
        import numpy as np
        DIM = 256
        HEADS = 16
        HEAD_DIM = DIM // HEADS
        EPS = 1e-06
        IMG_TOKENS = 257
        B, L1, L2 = (2, 512, 769)
        SCALE = 1.0 / np.sqrt(HEAD_DIM).astype(np.float32)

        def rms_norm(x, g):
            return x * jax.lax.rsqrt(jnp.mean(x * x, axis=-1, keepdims=True) + EPS) * g

        def attention(q, k, v, kv_mask=None):
            s = jnp.einsum('bqhd,bkhd->bhqk', q, k) * SCALE
            if kv_mask is not None:
                s = jnp.where(kv_mask[:, None, None, :], s, jnp.float32(-1000000000.0))
            p = jax.nn.softmax(s, axis=-1)
            return jnp.einsum('bhqk,bkhd->bqhd', p, v)
        key = jax.random.key(seed)
        ks = jax.random.split(key, 20)
        std = 0.02

        def lin(i):
            return (jax.random.normal(ks[i], (DIM, DIM), jnp.float32) * std, jnp.zeros((DIM,), jnp.float32))
        w_q, b_q = lin(0)
        w_k, b_k = lin(1)
        w_v, b_v = lin(2)
        w_k_img, b_k_img = lin(3)
        w_v_img, b_v_img = lin(4)
        w_o, b_o = lin(5)
        return {'x': jax.random.normal(ks[6], (B, L1, DIM), jnp.float32), 'context': jax.random.normal(ks[7], (B, L2, DIM), jnp.float32), 'context_lens': jax.random.randint(ks[8], (B,), 32, 513, jnp.int64 if jax.config.jax_enable_x64 else jnp.int32), 'w_q': w_q, 'b_q': b_q, 'w_k': w_k, 'b_k': b_k, 'w_v': w_v, 'b_v': b_v, 'w_k_img': w_k_img, 'b_k_img': b_k_img, 'w_v_img': w_v_img, 'b_v_img': b_v_img, 'w_o': w_o, 'b_o': b_o, 'g_q': jnp.ones((DIM,), jnp.float32), 'g_k': jnp.ones((DIM,), jnp.float32), 'g_k_img': jnp.ones((DIM,), jnp.float32)}
    _L0_xattn_all = _L0_xattn_setup()
    _L0_xattn_in = {k: v for k, v in _L0_xattn_all.items() if k in ('w_q', 'b_q', 'w_k', 'b_k', 'w_v', 'b_v', 'w_k_img', 'b_k_img', 'w_v_img', 'b_v_img', 'w_o', 'b_o', 'g_q', 'g_k', 'g_k_img')}
    del _L0_xattn_all

    def _L0_ffn_setup():
        import jax, jax.numpy as jnp
        import numpy as np
        RANK = 64
        SCALING = 1.0 / RANK
        TEMPERATURE = 1.0
        key = jax.random.key(seed)
        k_x, k_a, k_b, k_w = jax.random.split(key, 4)
        B_, S, D = (4, 256, 256)
        E, R, O = (8, RANK, 256)
        x = jax.random.normal(k_x, (B_, S, D), dtype=jnp.float32)
        A = jax.random.normal(k_a, (E, R, D), dtype=jnp.float32) * (1.0 / np.sqrt(D))
        Bw = jax.random.normal(k_b, (E, O, R), dtype=jnp.float32) * 0.02
        Wr = jax.random.normal(k_w, (E, D), dtype=jnp.float32) * (1.0 / np.sqrt(D))
        br = jnp.zeros((E,), dtype=jnp.float32)
        return {'x': x, 'A': A, 'B': Bw, 'Wr': Wr, 'br': br}
    _L0_ffn_all = _L0_ffn_setup()
    _L0_ffn_in = {k: v for k, v in _L0_ffn_all.items() if k in ('A', 'B', 'Wr', 'br')}
    del _L0_ffn_all

    def _L1_xattn_setup():
        import jax, jax.numpy as jnp
        import numpy as np
        key = jax.random.key(seed)
        k1, k2, k3 = jax.random.split(key, 3)
        B, S, D, M = (8, 256, 256, 128)
        hidden_states = jax.random.normal(k1, (B, S, D), dtype=jnp.float32)
        memory_tokens = jax.random.normal(k2, (B, M, D), dtype=jnp.float32)
        memory_mask = jax.random.randint(k3, (B, M), 0, 2).astype(jnp.bool_)
        return {'hidden_states': hidden_states, 'memory_tokens': memory_tokens, 'memory_mask': memory_mask}
    _L1_xattn_all = _L1_xattn_setup()
    _L1_xattn_in = {k: v for k, v in _L1_xattn_all.items() if k in ()}
    del _L1_xattn_all

    def _L1_ffn_setup():
        import jax, jax.numpy as jnp
        import numpy as np
        B, S, H = (4, 128, 256)
        E, K, I, SI = (16, 4, 176, 704)

        def _silu_mul(gu, inter):
            return jax.nn.silu(gu[:, :inter]) * gu[:, inter:]
        key = jax.random.key(seed)
        ks = jax.random.split(key, 7)
        s = 0.02
        return {'hidden_states': jax.random.normal(ks[0], (B, S, H), jnp.float32), 'gate_w': jax.random.normal(ks[1], (E, H), jnp.float32) * s, 'expert_gate_up': jax.random.normal(ks[2], (E, 2 * I, H), jnp.float32) * s, 'expert_down': jax.random.normal(ks[3], (E, H, I), jnp.float32) * s, 'shared_gate_up': jax.random.normal(ks[4], (2 * SI, H), jnp.float32) * s, 'shared_down': jax.random.normal(ks[5], (H, SI), jnp.float32) * s, 'shared_gate_vec': jax.random.normal(ks[6], (1, H), jnp.float32) * s}
    _L1_ffn_all = _L1_ffn_setup()
    _L1_ffn_in = {k: v for k, v in _L1_ffn_all.items() if k in ('gate_w', 'expert_gate_up', 'expert_down', 'shared_gate_up', 'shared_down', 'shared_gate_vec')}
    del _L1_ffn_all

    def _L2_xattn_setup():
        import jax, jax.numpy as jnp
        import numpy as np
        import math
        H = 256
        NH = 16
        HD = H // NH
        EPS_LN = 1e-05
        RES_SCALE_MAX = 0.3

        def _nan_clean(x, lim=10000.0):
            return jnp.nan_to_num(x, nan=0.0, posinf=lim, neginf=-lim)
        key = jax.random.key(seed)
        ks = jax.random.split(key, 12)
        B, S, T = (4, 256, 32)
        std = 1.0 / math.sqrt(H)
        return {'hidden_states': jax.random.normal(ks[0], (B, S, H), jnp.float32), 'audio_tokens': jax.random.normal(ks[1], (B, T, H), jnp.float32), 'attention_mask': jax.random.randint(ks[2], (B, T), 0, 2, jnp.int32), 'Wq': jax.random.normal(ks[3], (H, H), jnp.float32) * std, 'bq': jnp.zeros((H,), jnp.float32), 'Wk': jax.random.normal(ks[4], (H, H), jnp.float32) * std, 'bk': jnp.zeros((H,), jnp.float32), 'Wv': jax.random.normal(ks[5], (H, H), jnp.float32) * std, 'bv': jnp.zeros((H,), jnp.float32), 'Wo': jax.random.normal(ks[6], (H, H), jnp.float32) * std, 'bo': jnp.zeros((H,), jnp.float32), 'ln_gamma': jnp.ones((H,), jnp.float32), 'ln_beta': jnp.zeros((H,), jnp.float32), 'residual_scale': jnp.float32(0.05)}
    _L2_xattn_all = _L2_xattn_setup()
    _L2_xattn_in = {k: v for k, v in _L2_xattn_all.items() if k in ('Wq', 'bq', 'Wk', 'bk', 'Wv', 'bv', 'Wo', 'bo', 'ln_gamma', 'ln_beta', 'residual_scale')}
    del _L2_xattn_all

    def _L2_ffn_setup():
        import jax, jax.numpy as jnp
        import numpy as np
        B, S, D, H = (4, 256, 256, 1024)

        def fwht(x):
            orig_shape = x.shape
            n = orig_shape[-1]
            x = x.reshape(-1, n)
            h = 1
            while h < n:
                xb = x.reshape(-1, n // (2 * h), 2, h)
                a = xb[:, :, 0, :]
                b = xb[:, :, 1, :]
                x = jnp.stack([a + b, a - b], axis=2).reshape(-1, n)
                h *= 2
            scale = jnp.asarray(1.0 / np.sqrt(n), dtype=x.dtype)
            return (x * scale).reshape(orig_shape)
        key = jax.random.key(seed)
        kx, k1, k2, k3 = jax.random.split(key, 4)
        x = jax.random.normal(kx, (B, S, D), dtype=jnp.float32)
        W1 = jax.random.normal(k1, (H, D), dtype=jnp.float32) * (1.0 / np.sqrt(D))
        W2 = jax.random.normal(k2, (D, H), dtype=jnp.float32) * (1.0 / np.sqrt(H))
        W3 = jax.random.normal(k3, (H, D), dtype=jnp.float32) * (1.0 / np.sqrt(D))
        return {'x': x, 'W1': W1, 'W2': W2, 'W3': W3}
    _L2_ffn_all = _L2_ffn_setup()
    _L2_ffn_in = {k: v for k, v in _L2_ffn_all.items() if k in ('W1', 'W2', 'W3')}
    del _L2_ffn_all

    def _L3_xattn_setup():
        import jax, jax.numpy as jnp
        import numpy as np
        DIM = 256
        NHEADS = 32
        HEAD_DIM = DIM // NHEADS
        EPS = 1e-06

        def _rmsnorm(t):
            return t * jax.lax.rsqrt(jnp.mean(t * t, axis=-1, keepdims=True) + EPS)
        key = jax.random.key(seed)
        kx, kc, kq, kk, kv = jax.random.split(key, 5)
        x = jax.random.normal(kx, (2, 512, DIM), dtype=jnp.float32)
        context = jax.random.normal(kc, (2, 64, DIM), dtype=jnp.float32)
        std = 0.02
        Wq = jax.random.normal(kq, (DIM, DIM), dtype=jnp.float32) * std
        Wk = jax.random.normal(kk, (DIM, DIM), dtype=jnp.float32) * std
        Wv = jax.random.normal(kv, (DIM, DIM), dtype=jnp.float32) * std
        return {'x': x, 'context': context, 'Wq': Wq, 'Wk': Wk, 'Wv': Wv}
    _L3_xattn_all = _L3_xattn_setup()
    _L3_xattn_in = {k: v for k, v in _L3_xattn_all.items() if k in ('Wq', 'Wk', 'Wv')}
    del _L3_xattn_all

    def _L3_ffn_setup():
        import jax, jax.numpy as jnp
        import numpy as np
        H, LAT, INTER, E, G, TOPK_G, TOP_K = (256, 128, 128, 32, 4, 2, 8)
        SHARED_INTER = 512
        ROUTED_SCALE = 2.5
        B, S = (2, 128)

        def relu2(x):
            return jnp.square(jax.nn.relu(x))
        key = jax.random.key(seed)
        ks = jax.random.split(key, 9)
        w = 0.02
        return {'hidden_states': jax.random.normal(ks[0], (B, S, H), jnp.float32), 'gate_w': jax.random.normal(ks[1], (E, H), jnp.float32) * w, 'gate_bias': jax.random.normal(ks[2], (E,), jnp.float32) * w, 'fc1_w': jax.random.normal(ks[3], (LAT, H), jnp.float32) * w, 'fc2_w': jax.random.normal(ks[4], (H, LAT), jnp.float32) * w, 'w1': jax.random.normal(ks[5], (E, INTER, LAT), jnp.float32) * w, 'w2': jax.random.normal(ks[6], (E, LAT, INTER), jnp.float32) * w, 'shared_up_w': jax.random.normal(ks[7], (SHARED_INTER, H), jnp.float32) * w, 'shared_down_w': jax.random.normal(ks[8], (H, SHARED_INTER), jnp.float32) * w}
    _L3_ffn_all = _L3_ffn_setup()
    _L3_ffn_in = {k: v for k, v in _L3_ffn_all.items() if k in ('gate_w', 'gate_bias', 'fc1_w', 'fc2_w', 'w1', 'w2', 'shared_up_w', 'shared_down_w')}
    del _L3_ffn_all
    return {'x': x, 'ctx_2048': ctx_2048, '_lenS2': _lenS2, 'mask_BxS2_bk0': mask_BxS2_bk0, 'mask_BxS2_ik0': mask_BxS2_ik0, 'g_xattn': g_xattn, 'g_ffn': g_ffn, 'L0_xattn_w_q': _L0_xattn_in['w_q'], 'L0_xattn_b_q': _L0_xattn_in['b_q'], 'L0_xattn_w_k': _L0_xattn_in['w_k'], 'L0_xattn_b_k': _L0_xattn_in['b_k'], 'L0_xattn_w_v': _L0_xattn_in['w_v'], 'L0_xattn_b_v': _L0_xattn_in['b_v'], 'L0_xattn_w_k_img': _L0_xattn_in['w_k_img'], 'L0_xattn_b_k_img': _L0_xattn_in['b_k_img'], 'L0_xattn_w_v_img': _L0_xattn_in['w_v_img'], 'L0_xattn_b_v_img': _L0_xattn_in['b_v_img'], 'L0_xattn_w_o': _L0_xattn_in['w_o'], 'L0_xattn_b_o': _L0_xattn_in['b_o'], 'L0_xattn_g_q': _L0_xattn_in['g_q'], 'L0_xattn_g_k': _L0_xattn_in['g_k'], 'L0_xattn_g_k_img': _L0_xattn_in['g_k_img'], 'L0_ffn_A': _L0_ffn_in['A'], 'L0_ffn_B': _L0_ffn_in['B'], 'L0_ffn_Wr': _L0_ffn_in['Wr'], 'L0_ffn_br': _L0_ffn_in['br'], 'L1_ffn_gate_w': _L1_ffn_in['gate_w'], 'L1_ffn_expert_gate_up': _L1_ffn_in['expert_gate_up'], 'L1_ffn_expert_down': _L1_ffn_in['expert_down'], 'L1_ffn_shared_gate_up': _L1_ffn_in['shared_gate_up'], 'L1_ffn_shared_down': _L1_ffn_in['shared_down'], 'L1_ffn_shared_gate_vec': _L1_ffn_in['shared_gate_vec'], 'L2_xattn_Wq': _L2_xattn_in['Wq'], 'L2_xattn_bq': _L2_xattn_in['bq'], 'L2_xattn_Wk': _L2_xattn_in['Wk'], 'L2_xattn_bk': _L2_xattn_in['bk'], 'L2_xattn_Wv': _L2_xattn_in['Wv'], 'L2_xattn_bv': _L2_xattn_in['bv'], 'L2_xattn_Wo': _L2_xattn_in['Wo'], 'L2_xattn_bo': _L2_xattn_in['bo'], 'L2_xattn_ln_gamma': _L2_xattn_in['ln_gamma'], 'L2_xattn_ln_beta': _L2_xattn_in['ln_beta'], 'L2_xattn_residual_scale': _L2_xattn_in['residual_scale'], 'L2_ffn_W1': _L2_ffn_in['W1'], 'L2_ffn_W2': _L2_ffn_in['W2'], 'L2_ffn_W3': _L2_ffn_in['W3'], 'L3_xattn_Wq': _L3_xattn_in['Wq'], 'L3_xattn_Wk': _L3_xattn_in['Wk'], 'L3_xattn_Wv': _L3_xattn_in['Wv'], 'L3_ffn_gate_w': _L3_ffn_in['gate_w'], 'L3_ffn_gate_bias': _L3_ffn_in['gate_bias'], 'L3_ffn_fc1_w': _L3_ffn_in['fc1_w'], 'L3_ffn_fc2_w': _L3_ffn_in['fc2_w'], 'L3_ffn_w1': _L3_ffn_in['w1'], 'L3_ffn_w2': _L3_ffn_in['w2'], 'L3_ffn_shared_up_w': _L3_ffn_in['shared_up_w'], 'L3_ffn_shared_down_w': _L3_ffn_in['shared_down_w']}

def reference(x, ctx_2048, _lenS2, mask_BxS2_bk0, mask_BxS2_ik0, g_xattn, g_ffn, L0_xattn_w_q, L0_xattn_b_q, L0_xattn_w_k, L0_xattn_b_k, L0_xattn_w_v, L0_xattn_b_v, L0_xattn_w_k_img, L0_xattn_b_k_img, L0_xattn_w_v_img, L0_xattn_b_v_img, L0_xattn_w_o, L0_xattn_b_o, L0_xattn_g_q, L0_xattn_g_k, L0_xattn_g_k_img, L0_ffn_A, L0_ffn_B, L0_ffn_Wr, L0_ffn_br, L1_ffn_gate_w, L1_ffn_expert_gate_up, L1_ffn_expert_down, L1_ffn_shared_gate_up, L1_ffn_shared_down, L1_ffn_shared_gate_vec, L2_xattn_Wq, L2_xattn_bq, L2_xattn_Wk, L2_xattn_bk, L2_xattn_Wv, L2_xattn_bv, L2_xattn_Wo, L2_xattn_bo, L2_xattn_ln_gamma, L2_xattn_ln_beta, L2_xattn_residual_scale, L2_ffn_W1, L2_ffn_W2, L2_ffn_W3, L3_xattn_Wq, L3_xattn_Wk, L3_xattn_Wv, L3_ffn_gate_w, L3_ffn_gate_bias, L3_ffn_fc1_w, L3_ffn_fc2_w, L3_ffn_w1, L3_ffn_w2, L3_ffn_shared_up_w, L3_ffn_shared_down_w):
    import jax
    import jax.numpy as jnp

    def _L0_xattn_ref(x, context, context_lens, w_q, b_q, w_k, b_k, w_v, b_v, w_k_img, b_k_img, w_v_img, b_v_img, w_o, b_o, g_q, g_k, g_k_img):
        import jax, jax.numpy as jnp
        import numpy as np
        DIM = 256
        HEADS = 16
        HEAD_DIM = DIM // HEADS
        EPS = 1e-06
        IMG_TOKENS = 257
        B, L1, L2 = (2, 512, 769)
        SCALE = 1.0 / np.sqrt(HEAD_DIM).astype(np.float32)

        def rms_norm(x, g):
            return x * jax.lax.rsqrt(jnp.mean(x * x, axis=-1, keepdims=True) + EPS) * g

        def attention(q, k, v, kv_mask=None):
            s = jnp.einsum('bqhd,bkhd->bhqk', q, k) * SCALE
            if kv_mask is not None:
                s = jnp.where(kv_mask[:, None, None, :], s, jnp.float32(-1000000000.0))
            p = jax.nn.softmax(s, axis=-1)
            return jnp.einsum('bhqk,bkhd->bqhd', p, v)
        b = x.shape[0]
        ctx_img = context[:, :IMG_TOKENS]
        ctx_txt = context[:, IMG_TOKENS:]
        q = rms_norm(x @ w_q.T + b_q, g_q).reshape(b, -1, HEADS, HEAD_DIM)
        k = rms_norm(ctx_txt @ w_k.T + b_k, g_k).reshape(b, -1, HEADS, HEAD_DIM)
        v = (ctx_txt @ w_v.T + b_v).reshape(b, -1, HEADS, HEAD_DIM)
        k_img = rms_norm(ctx_img @ w_k_img.T + b_k_img, g_k_img).reshape(b, -1, HEADS, HEAD_DIM)
        v_img = (ctx_img @ w_v_img.T + b_v_img).reshape(b, -1, HEADS, HEAD_DIM)
        txt_len = ctx_txt.shape[1]
        kv_mask = jnp.arange(txt_len)[None, :] < context_lens[:, None]
        img_x = attention(q, k_img, v_img)
        txt_x = attention(q, k, v, kv_mask)
        out = (txt_x + img_x).reshape(b, -1, DIM)
        return out @ w_o.T + b_o

    def _L0_ffn_ref(x, A, B, Wr, br):
        import jax, jax.numpy as jnp
        import numpy as np
        RANK = 64
        SCALING = 1.0 / RANK
        TEMPERATURE = 1.0
        batch, seq, d = x.shape
        E, out_dim = (B.shape[0], B.shape[1])
        x_flat = x.reshape(-1, d)
        logits = (x_flat @ Wr.T + br) / TEMPERATURE
        probs = jax.nn.softmax(logits, axis=-1)
        expert_idx = jnp.argmax(probs, axis=-1)
        expert_weight = jnp.max(probs, axis=-1)
        h = jnp.einsum('nd,erd->ner', x_flat, A)
        y = jnp.einsum('ner,eor->neo', h, B) * SCALING
        sel = jnp.take_along_axis(y, expert_idx[:, None, None], axis=1)[:, 0, :]
        out_flat = sel * expert_weight[:, None]
        return out_flat.reshape(batch, seq, out_dim)

    def _L1_xattn_ref(hidden_states, memory_tokens, memory_mask):
        import jax, jax.numpy as jnp
        import numpy as np
        B, S, D = hidden_states.shape
        scale = 1.0 / jnp.sqrt(jnp.asarray(D, hidden_states.dtype))
        scores = jnp.einsum('bsd,bmd->bsm', hidden_states, memory_tokens) * scale
        neg_inf = jnp.asarray(-1e+30, scores.dtype)
        scores = jnp.where(memory_mask[:, None, :], scores, neg_inf)
        attn = jax.nn.softmax(scores, axis=-1)
        readout = jnp.einsum('bsm,bmd->bsd', attn, memory_tokens)
        valid_b = jnp.any(memory_mask, axis=-1)
        out = jnp.where(valid_b[:, None, None], readout, jnp.zeros_like(readout))
        return out

    def _L1_ffn_ref(hidden_states, gate_w, expert_gate_up, expert_down, shared_gate_up, shared_down, shared_gate_vec):
        import jax, jax.numpy as jnp
        import numpy as np
        B, S, H = (4, 128, 256)
        E, K, I, SI = (16, 4, 176, 704)

        def _silu_mul(gu, inter):
            return jax.nn.silu(gu[:, :inter]) * gu[:, inter:]
        orig_shape = hidden_states.shape
        x = hidden_states.reshape(-1, H)
        router_logits = x @ gate_w.T
        routing_probs = jax.nn.softmax(router_logits.astype(jnp.float32), axis=-1)
        topk_w, topk_idx = jax.lax.top_k(routing_probs, K)
        topk_w = topk_w / topk_w.sum(axis=-1, keepdims=True)
        topk_w = topk_w.astype(x.dtype)
        combine = (jax.nn.one_hot(topk_idx, E, dtype=x.dtype) * topk_w[..., None]).sum(1)
        shared = _silu_mul(x @ shared_gate_up.T, SI) @ shared_down.T
        shared = shared * jax.nn.sigmoid(x @ shared_gate_vec.T)

        def step(acc, ew):
            w_gu, w_d, cw = ew
            h = _silu_mul(x @ w_gu.T, I)
            return (acc + h @ w_d.T * cw[:, None], None)
        acc0 = jnp.zeros_like(x)
        sparse, _ = jax.lax.scan(step, acc0, (expert_gate_up, expert_down, combine.T))
        return (shared + sparse).reshape(orig_shape)

    def _L2_xattn_ref(hidden_states, audio_tokens, attention_mask, Wq, bq, Wk, bk, Wv, bv, Wo, bo, ln_gamma, ln_beta, residual_scale):
        import jax, jax.numpy as jnp
        import numpy as np
        import math
        H = 256
        NH = 16
        HD = H // NH
        EPS_LN = 1e-05
        RES_SCALE_MAX = 0.3

        def _nan_clean(x, lim=10000.0):
            return jnp.nan_to_num(x, nan=0.0, posinf=lim, neginf=-lim)
        B, S, _ = hidden_states.shape
        T = audio_tokens.shape[1]
        hs = _nan_clean(hidden_states).astype(jnp.float32)
        at = _nan_clean(audio_tokens).astype(jnp.float32)

        def proj(x, W, b, L):
            y = x @ W.T + b
            return y.reshape(B, L, NH, HD).transpose(0, 2, 1, 3)
        q = _nan_clean(proj(hs, Wq, bq, S))
        k = _nan_clean(proj(at, Wk, bk, T))
        v = _nan_clean(proj(at, Wv, bv, T))
        scale = max(math.sqrt(HD), 1e-08)
        scores = jnp.einsum('bhsd,bhtd->bhst', q, k) / scale
        scores = jnp.clip(scores, -50.0, 50.0)
        scores = jnp.nan_to_num(scores, nan=0.0, posinf=50.0, neginf=-50.0)
        attend = (attention_mask.astype(jnp.float32) > 0.5)[:, None, None, :]
        scores = jnp.where(attend, scores, -10000.0)
        scores = jnp.clip(scores, -50.0, 50.0)
        probs = jax.nn.softmax(scores, axis=-1)
        probs = jnp.nan_to_num(probs, nan=0.0, posinf=1.0, neginf=0.0)
        probs = probs / (probs.sum(axis=-1, keepdims=True) + 1e-08)
        ctx = jnp.einsum('bhst,bhtd->bhsd', probs, v)
        ctx = ctx.transpose(0, 2, 1, 3).reshape(B, S, H)
        delta = _nan_clean(ctx @ Wo.T + bo)
        rs = jnp.clip(residual_scale, 0.0, RES_SCALE_MAX)
        delta = rs * delta
        mu = delta.mean(axis=-1, keepdims=True)
        var = jnp.mean((delta - mu) ** 2, axis=-1, keepdims=True)
        delta = (delta - mu) / jnp.sqrt(var + EPS_LN) * ln_gamma + ln_beta
        return delta

    def _L2_ffn_ref(x, W1, W2, W3):
        import jax, jax.numpy as jnp
        import numpy as np
        B, S, D, H = (4, 256, 256, 1024)

        def fwht(x):
            orig_shape = x.shape
            n = orig_shape[-1]
            x = x.reshape(-1, n)
            h = 1
            while h < n:
                xb = x.reshape(-1, n // (2 * h), 2, h)
                a = xb[:, :, 0, :]
                b = xb[:, :, 1, :]
                x = jnp.stack([a + b, a - b], axis=2).reshape(-1, n)
                h *= 2
            scale = jnp.asarray(1.0 / np.sqrt(n), dtype=x.dtype)
            return (x * scale).reshape(orig_shape)
        up_gate = jnp.einsum('bsd,hd->bsh', x, W1)
        up_lin = jnp.einsum('bsd,hd->bsh', x, W3)
        hidden = jax.nn.silu(up_gate) * up_lin
        hidden = fwht(hidden)
        out = jnp.einsum('bsh,dh->bsd', hidden, W2)
        return out

    def _L3_xattn_ref(x, context, Wq, Wk, Wv):
        import jax, jax.numpy as jnp
        import numpy as np
        DIM = 256
        NHEADS = 32
        HEAD_DIM = DIM // NHEADS
        EPS = 1e-06

        def _rmsnorm(t):
            return t * jax.lax.rsqrt(jnp.mean(t * t, axis=-1, keepdims=True) + EPS)
        b, n, _ = x.shape
        m = context.shape[1]
        q = x @ Wq.T
        k_raw = context @ Wk.T
        v_raw = context @ Wv.T
        q = q.reshape(b, n, NHEADS, HEAD_DIM).transpose(0, 2, 1, 3)
        kv = jnp.concatenate([k_raw, v_raw], axis=-1)
        kv = kv.reshape(b, m, NHEADS, HEAD_DIM, 2)
        k = kv[..., 0].transpose(0, 2, 1, 3)
        v = kv[..., 1].transpose(0, 2, 1, 3)
        q = _rmsnorm(q)
        k = _rmsnorm(k)
        scale = HEAD_DIM ** (-0.5)
        scores = jnp.einsum('bhnd,bhmd->bhnm', q, k) * scale
        attn = jax.nn.softmax(scores, axis=-1)
        out = jnp.einsum('bhnm,bhmd->bhnd', attn, v)
        return out.transpose(0, 2, 1, 3).reshape(b, n, NHEADS * HEAD_DIM)

    def _L3_ffn_ref(hidden_states, gate_w, gate_bias, fc1_w, fc2_w, w1, w2, shared_up_w, shared_down_w):
        import jax, jax.numpy as jnp
        import numpy as np
        H, LAT, INTER, E, G, TOPK_G, TOP_K = (256, 128, 128, 32, 4, 2, 8)
        SHARED_INTER = 512
        ROUTED_SCALE = 2.5
        B, S = (2, 128)

        def relu2(x):
            return jnp.square(jax.nn.relu(x))
        orig_shape = hidden_states.shape
        x = hidden_states.reshape(-1, H)
        T = x.shape[0]
        logits = jnp.einsum('th,eh->te', x.astype(jnp.float32), gate_w)
        scores = jax.nn.sigmoid(logits)
        sb = scores + gate_bias
        grp = sb.reshape(T, G, E // G)
        group_scores = jax.lax.top_k(grp, 2)[0].sum(-1)
        _, gidx = jax.lax.top_k(group_scores, TOPK_G)
        gmask = jax.nn.one_hot(gidx, G, dtype=sb.dtype).sum(1)
        masked = jnp.where(gmask[:, :, None] > 0, grp, -jnp.inf).reshape(T, E)
        _, topi = jax.lax.top_k(masked, TOP_K)
        wsel = jnp.take_along_axis(scores, topi, axis=1)
        wsel = wsel / wsel.sum(-1, keepdims=True) * ROUTED_SCALE
        cw = jnp.zeros((T, E), jnp.float32).at[jnp.arange(T)[:, None], topi].add(wsel)
        x_lat = x @ fc1_w.T
        h = relu2(jnp.einsum('tl,eil->eti', x_lat, w1))
        h = h * cw.T[:, :, None]
        y_lat = jnp.einsum('eti,eli->tl', h, w2)
        routed = y_lat @ fc2_w.T
        shared = relu2(x @ shared_up_w.T) @ shared_down_w.T
        return (shared + routed).reshape(orig_shape)
    x = x + jnp.tanh(g_xattn[0]) * _L0_xattn_ref(_layernorm(x, axis=-1), ctx_2048, _lenS2, L0_xattn_w_q, L0_xattn_b_q, L0_xattn_w_k, L0_xattn_b_k, L0_xattn_w_v, L0_xattn_b_v, L0_xattn_w_k_img, L0_xattn_b_k_img, L0_xattn_w_v_img, L0_xattn_b_v_img, L0_xattn_w_o, L0_xattn_b_o, L0_xattn_g_q, L0_xattn_g_k, L0_xattn_g_k_img)
    x = x + jnp.tanh(g_ffn[0]) * _L0_ffn_ref(_layernorm(x, axis=-1), L0_ffn_A, L0_ffn_B, L0_ffn_Wr, L0_ffn_br)
    x = x + jnp.tanh(g_xattn[1]) * _L1_xattn_ref(_layernorm(x, axis=-1), ctx_2048, mask_BxS2_bk0)
    x = x + jnp.tanh(g_ffn[1]) * _L1_ffn_ref(_layernorm(x, axis=-1), L1_ffn_gate_w, L1_ffn_expert_gate_up, L1_ffn_expert_down, L1_ffn_shared_gate_up, L1_ffn_shared_down, L1_ffn_shared_gate_vec)
    x = x + jnp.tanh(g_xattn[2]) * _L2_xattn_ref(_layernorm(x, axis=-1), ctx_2048, mask_BxS2_ik0, L2_xattn_Wq, L2_xattn_bq, L2_xattn_Wk, L2_xattn_bk, L2_xattn_Wv, L2_xattn_bv, L2_xattn_Wo, L2_xattn_bo, L2_xattn_ln_gamma, L2_xattn_ln_beta, L2_xattn_residual_scale)
    x = x + jnp.tanh(g_ffn[2]) * _L2_ffn_ref(_layernorm(x, axis=-1), L2_ffn_W1, L2_ffn_W2, L2_ffn_W3)
    x = x + jnp.tanh(g_xattn[3]) * _L3_xattn_ref(_layernorm(x, axis=-1), ctx_2048, L3_xattn_Wq, L3_xattn_Wk, L3_xattn_Wv)
    x = x + jnp.tanh(g_ffn[3]) * _L3_ffn_ref(_layernorm(x, axis=-1), L3_ffn_gate_w, L3_ffn_gate_bias, L3_ffn_fc1_w, L3_ffn_fc2_w, L3_ffn_w1, L3_ffn_w2, L3_ffn_shared_up_w, L3_ffn_shared_down_w)
    return x

_drawn_inputs = setup_inputs


def setup_inputs(seed=0):
    import zlib

    import numpy as np

    out = dict(_drawn_inputs(seed))
    spreads = {'L0_xattn_b_q': (0.0, 0.8),
     'L0_xattn_b_k': (0.0, 0.1),
     'L0_xattn_b_v': (0.0, 0.1),
     'L0_xattn_b_k_img': (0.0, 0.8),
     'L0_xattn_b_v_img': (0.0, 0.448),
     'L0_xattn_b_o': (0.0, 0.1),
     'L0_xattn_g_q': (1.0, 0.6),
     'L0_xattn_g_k': (1.0, 0.2),
     'L0_xattn_g_k_img': (1.0, 0.6),
     'L0_ffn_br': (0.0, 0.8),
     'L2_xattn_bq': (0.0, 0.321),
     'L2_xattn_bk': (0.0, 2.0),
     'L2_xattn_bv': (0.0, 0.1),
     'L2_xattn_bo': (0.0, 0.1),
     'L2_xattn_ln_gamma': (1.0, 0.2),
     'L2_xattn_ln_beta': (0.0, 0.1)}
    factors = {'g_ffn': 8.0,
     'L0_xattn_w_q': 4.744,
     'L0_xattn_w_k_img': 4.533,
     'L0_ffn_A': 8.0,
     'L0_ffn_B': 8.0,
     'L0_ffn_Wr': 8.0,
     'L1_ffn_gate_w': 8.0,
     'L1_ffn_expert_gate_up': 8.0,
     'L1_ffn_expert_down': 8.0,
     'L1_ffn_shared_gate_up': 5.629,
     'L1_ffn_shared_down': 5.669,
     'L1_ffn_shared_gate_vec': 8.0,
     'L3_ffn_gate_w': 8.0,
     'L3_ffn_gate_bias': 8.0,
     'L3_ffn_fc1_w': 8.0,
     'L3_ffn_fc2_w': 8.0,
     'L3_ffn_w1': 8.0,
     'L3_ffn_w2': 8.0,
     'L3_ffn_shared_up_w': 8.0,
     'L3_ffn_shared_down_w': 8.0}
    for name, (base, spread) in spreads.items():
        noise = np.random.default_rng([zlib.crc32(name.encode()), seed]).standard_normal(out[name].shape)
        drawn = base * np.exp(spread * noise) if base else spread * noise
        out[name] = jnp.asarray(drawn.astype(out[name].dtype))
    for name, factor in factors.items():
        out[name] = (out[name] * factor).astype(out[name].dtype)
    return out
```

```python
from contextlib import ExitStack, contextmanager

import numpy as np

import concourse.bass as bass
from concourse import mybir

F32 = mybir.dt.float32
BF16 = mybir.dt.bfloat16
I32 = mybir.dt.int32
U8 = mybir.dt.uint8
ALU = mybir.AluOpType
ACT = mybir.ActivationFunctionType
AX = mybir.AxisListType

P = 128
B, S, D = 16, 64, 256
TOK = B * S
NT = TOK // P
KC = D // P
BT = P // S
HALF = 512
NL = 8
BIG = 3.0e38
NEG = -1.0e30

E0, R0 = 8, 64
E1, I1, SI1 = 16, 176, 704
TOP1 = 4
EP1 = 24
C1 = -(-(E1 * I1 + SI1) // P)
H2 = 1024
C2 = H2 // P
E3, LAT3, SH3, G3 = 32, 128, 512, 4
TOP3, TOPG3, SCALE3 = 8, 2, 2.5
C3S = SH3 // P

ROWS = [("bq0", D), ("bk0", D), ("bv0", D), ("bo0", D), ("gq0", D), ("gk0", D), ("br0", E0),
        ("bv2", D), ("bo2", D), ("gamma2", D), ("beta2", D), ("bias3", E3), ("rs2", 1), ("gates", 8),
        ("first8", E0), ("lower4", G3 * G3)]
EARLY = [("wk0", KC * D), ("wq0", KC * D), ("wv0", KC * D), ("wo0", KC * D), ("ident", P), ("pair", 2), ("quad", 4)]
LATE = [("A0", KC * E0 * R0), ("B0", (E0 * R0 // P) * D), ("wr0", KC * E0), ("gate1", KC * (E1 + 1)),
        ("wk2", KC * D), ("wq2", KC * D), ("wv2", KC * D), ("wo2", KC * D), ("bqk2", 2 * KC),
        ("had", P), ("w2f", C2 * D),
        ("wk3", KC * D), ("wq3", KC * D), ("wv3", KC * D), ("gate3", KC * E3), ("fc1", KC * LAT3),
        ("fc2", D), ("up3", C3S * KC * P), ("down3", C3S * D)]


def columns(pack):
    at, out = 0, {}
    for name, n in pack:
        out[name] = (at, n)
        at += n
    return out, at


RCOL, RN = columns(ROWS)
ECOL, EN = columns(EARLY)
LCOL, LN_ = columns(LATE)
W1COLS = KC * 2 * P + D
W2COLS = KC * 2 * P
W3COLS = P + LAT3


class Chain:

    def __init__(self, eng, sem):
        self.eng, self.sem, self.n, self.i, self.per = eng, sem, 0, None, 0

    def value(self):
        return self.n if self.i is None else self.i * self.per + self.n

    def link(self, ins):
        ins.then_inc(self.sem, 1)
        self.n += 1
        self.eng.wait_ge(self.sem, self.value())

    @contextmanager
    def loop(self, start, end, per):
        base = self.n
        with self.eng.Fori(start, end) as i:
            self.i, self.per, self.n = i, per, base - start * per
            yield i
            assert self.n == base - start * per + per, (self.n, base, start, per)
        self.i, self.n = None, base + (end - start) * per


def flamingo_kernel(nc, x_in, ctx_in, ctxT_in, rows_in, early_in, late_in, w1_in, w2_in, w3_in,
                    mask1_in, mask2_in, identb_in, sel0_in, sel1_in, sel3_in, out):
    with ExitStack() as stack:
        def sb(name, shape, dt=F32):
            return stack.enter_context(nc.sbuf_tensor(name, shape, dt))

        def sem(name):
            return stack.enter_context(nc.semaphore(name))

        x = sb("x", [P, NT, D])
        xn = sb("xn", [P, NT, D])
        xT = sb("xT", [P, KC, TOK])
        ctx = sb("ctx", [P, NT, D])
        ctxT = sb("ctxT", [P, KC, TOK])
        qT = sb("qT", [P, KC, TOK])
        kpair = sb("kpair", [P, KC * B * 4 * S])
        vpair = sb("vpair", [P, B * 288])
        probs = sb("probs", [P, 2, 2048])
        rows = sb("rows", [P, RN])
        early = sb("early", [P, EN])
        late = sb("late", [P, LN_])

        wring = sb("wring", [P, 2, W1COLS])
        sbuf_s = sb("act_s", [P, 2, HALF])
        sbuf_t = sb("mid_t", [P, 2, HALF])
        raw, nrm = sbuf_s[:, 0, :].rearrange("p (a n) -> p a n", a=2), sbuf_s[:, 1, :].rearrange("p (a n) -> p a n", a=2)
        junk, oN = sbuf_t[:, 0, :].rearrange("p (a n) -> p a n", a=2), sbuf_t[:, 1, :].rearrange("p (a n) -> p a n", a=2)
        sbuf_h = sb("hid_h", [P, 2, HALF])
        oT = sbuf_h[:, 1, :].rearrange("p (a n) -> p a n", a=2)
        gT = sb("gT", [3 * E3, TOK], BF16)
        identb = sb("identb", [P, P], BF16)
        sel0 = sb("sel0", [3 * E0, E0 * R0], BF16)
        sel1 = sb("sel1", [3 * EP1, C1 * P], BF16)
        sel3 = ctx[:, :, :].rearrange("p t n -> p (t n)").bitcast(BF16)[0:3 * E3, :]
        m8 = sb("m8", [P, NT, S], U8)
        m32 = kpair[:, 16 * NT * E3:18 * NT * E3].bitcast(I32).rearrange("p (t s) -> p t s", t=NT)
        mraw = sb("mraw", [P, B], I32)
        hi2 = sb("hi2", [P, B])
        st = sb("st", [P, NT, 6])
        mv = sb("mv", [P, NT, 2])
        mhalf = sb("mhalf", [P, 32])
        rstd = sb("rstd", [P, NT])
        ve = sb("ve", [P, NT])
        ss = sb("ss", [P, 2, 32])
        ssr = sb("ssr", [P, 2, 32])
        ssv = sb("ssv", [P, 2, 32])
        mx = sb("mx", [P, 2, 16])
        rden = sb("rden", [P, 2, 32])
        den2 = sb("den2", [P, 2, 32])
        tg = sb("tg", [P, 8])
        rs = sb("rs", [P, 1])
        lg, la, lb, lc, ld, top8 = (kpair[:, n * NT * E3:(n + 1) * NT * E3] for n in range(6))
        gsc = sb("gsc", [P, NT * G3])
        gsd = sb("gsd", [P, NT * G3])
        rk, rk2 = (kpair[:, at:at + NT * G3 * G3] for at in (6 * NT * E3, 6 * NT * E3 + NT * G3 * G3))
        red = sb("red", [P, NT])
        red2 = sb("red2", [P, NT])
        vm = sb("vm", [P, NT])
        g3 = kpair[:, 7 * NT * E3:9 * NT * E3].bitcast(BF16)[:, 0:NT * 3 * E3]
        cm = sbuf_h[:, 0, :].bitcast(I32)
        cr = sb("cr", [P, HALF])
        ps = stack.enter_context(nc.psum_tensor("ps", [P, 8, 512], F32))

        def E(name):
            a, n = ECOL[name]
            return early[:, a:a + n]

        def L(name):
            a, n = LCOL[name]
            return late[:, a:a + n]

        def R(name):
            a, n = RCOL[name]
            return rows[:, a:a + n]

        def kc(ap):
            return ap.rearrange("p (k n) -> p k n", k=KC)

        ident = E("ident")
        w2h = probs[:, 0, :]
        Kp = kpair[:, 0:KC * B * 2 * S].rearrange("p (c b h s) -> p c b h s", c=KC, b=B, h=2)
        Kq = kpair[:, :].rearrange("p (c b m s) -> p c b m s", c=KC, b=B, m=4)
        Vp = vpair[:, 0:B * 272].rearrange("p (b j h e) -> p b j h e", b=B, j=8, h=2)
        Vq = vpair[:, 0:B * 288].rearrange("p (b j h e) -> p b j h e", b=B, j=16, h=2)

        def tok(t):
            return slice(t * P, (t + 1) * P)

        s_x, s_ctxT, s_early, s_rows, s_late, s_misc, s_out = map(sem, (
            "x_landed", "ctxT_landed", "early_landed", "rows_landed", "late_landed", "misc_landed", "out_stored"))
        s_dve, s_pool, s_act = sem("dve_chain"), sem("pool_chain"), sem("act_chain")
        s_cst = sem("consts_ready")
        s_tanh = sem("tanh_ready")
        ln_var, ln_rstd, ln_xn, ln_Tfull, ln_xT = map(sem, (
            "ln_variance", "ln_rstd", "ln_normed", "ln_transposed", "ln_xT"))
        w2_bf, w2_mm, w2_ev = sem("w2_butterfly"), sem("w2_hadamard"), sem("w2_ready")
        A = {}
        for l in (0, 4, 6):
            A[l] = {n: sem(f"a{l}_{n}") for n in (
                ["v_full", "v_done", "q_ready", "k_ready", "sc_full", "sc_free", "p_ready", "pv_full", "o_norm",
                 "oT_full", "oT_ready", "o_proj", "resid"]
                + (["pr_full", "raw", "ss", "rms", "normed", "T_full", "T_done"] if l != 4 else
                   ["kq_full", "kq_done"])
                + (["pT_full", "pT_act", "pT_dve"] if l == 0 else [])
                + (["sq"] if l == 6 else []) + (["dvar", "drstd"] if l == 4 else []))}
        a2 = {n: sem(f"a2_{n}") for n in ("sc_full", "shift", "p_ready", "pT_full", "pT_ready", "pv_full", "resid")}
        Fs = {}
        for l in (1, 3, 5, 7, 8):
            Fs[l] = {n: sem(f"f{l}_{n}") for n in (
                ["up", "act", "h", "down", "resid"]
                + (["cw"] if l in (1, 3, 7) else []) + (["mid"] if l in (3, 7) else [])
                + (["logits", "e", "gates", "gT_full", "gT_ready", "lread"] if l in (1, 3, 7) else [])
                + (["land0", "land1"] if l in (3, 5, 7) else []))}
        s_lat, s_latE, s_yl = sem("lat_full"), sem("lat_ready"), sem("y_ready")
        s_vq = sem("vq_cleared")
        s_sel3 = sem("sel3_landed")

        block = stack.enter_context(nc.Block())
        FF = {1: 8, 3: 2 * C1, 5: 2 * C2, 7: 2 * E3, 8: 2 * C3S}

        @block.sync
        def _(sp):
            sp.dma_start(early[:, :], early_in).then_inc(s_early, 16)
            sp.dma_start(ctxT[:, :, :], ctxT_in).then_inc(s_ctxT, 16)
            sp.dma_start(rows[:, :], rows_in.partition_broadcast(P)).then_inc(s_rows, 16)
            sp.dma_start(late[:, :], late_in).then_inc(s_late, 16)
            for dst, src in ((identb[:, :], identb_in), (sel0[:, :], sel0_in), (sel1[:, :], sel1_in),
                             (m8[:, :, :], mask1_in), (mraw[:, :], mask2_in),
                             (ctx[:, :, :], ctx_in)):
                sp.dma_start(dst, src).then_inc(s_misc, 16)
            before = None
            for l, w, cols, chunks in ((3, w1_in, W1COLS, C1), (5, w2_in, W2COLS, C2), (7, w3_in, W3COLS, E3)):
                f = Fs[l]
                if before is not None:
                    sp.wait_ge(Fs[before]["down"], FF[before])
                    if l == 5:
                        sp.dma_start(sel3, sel3_in).then_inc(s_sel3, 16)
                before = l
                for c in range(2):
                    sp.dma_start(wring[:, c, 0:cols], w[c]).then_inc(f[f"land{c}"], 16)
                with sp.Fori(1, chunks // 2) as i:
                    for c in range(2):
                        sp.wait_ge(f["down"], i * 4 + (2 * c - 2))
                        sp.dma_start(wring[:, c, 0:cols], w[bass.ds(i * 2 + c, 1)].rearrange("o p n -> (o p) n")
                                     ).then_inc(f[f"land{c}"], 16)
            for t in range(NT):
                sp.wait_ge(Fs[8]["resid"], t + 1)
                sp.dma_start(out[:, t, :], x[:, t, :]).then_inc(s_out, 16)
            sp.wait_ge(s_out, 16 * NT)

        @block.gpsimd
        def _(pool):
            ch = Chain(pool, s_pool)
            pool.dma_start(x[:, :, :], x_in).then_inc(s_x, 16)
            pool.memset(mhalf[:, :], -0.5).then_inc(s_cst, 1)

            def block_diagonal(v, e, first):
                if first:
                    pool.memset(vpair[:, :], 0.0).then_inc(s_cst, 1)
                else:
                    ch.link(pool.memset(vpair[:, :], 0.0))
                if first:
                    pool.wait_ge(s_cst, 2)
                for h in range(2):
                    pool.memset(v[h * S:(h + 1) * S, :, :, h, e:e + 1].rearrange("p b j e -> p b (j e)"), 1.0).then_inc(
                        s_cst if first else s_vq, 1)
                    pool.wait_ge(*((s_cst, 3 + h) if first else (s_vq, 1 + h)))

            block_diagonal(Vp, 16, True)

            def rsqrt(out_ap, tmp, src, mul, eps, n, done):
                ch.link(pool.tensor_scalar(tmp, src, mul, eps, ALU.mult, ALU.add))
                pool.tensor_tensor(out_ap, tmp, mhalf[:, 0:n], ALU.pow).then_inc(done, 1)

            def ln(l):
                for t in range(NT):
                    pool.wait_ge(ln_var, NT * l + t + 1)
                    rsqrt(rstd[:, t:t + 1], ve[:, t:t + 1], mv[:, t, 1:2], 1.0, 1e-5, 1, ln_rstd)

            def rms(a, n, mul, first):
                for m in range(first, first + NT):
                    pool.wait_ge(a["ss"], m + 1)
                    rsqrt(ssr[:, m % 2, 0:n], ssv[:, m % 2, 0:n], ss[:, m % 2, 0:n], mul, 1e-6, n, a["rms"])

            ln(0)
            rms(A[0], 1, 1.0 / D, 0)
            rms(A[0], 1, 1.0 / D, NT)
            for l in range(1, NL):
                if l == 5:
                    for t in range(NT):
                        pool.wait_ge(A[4]["dvar"], t + 1)
                        rsqrt(rstd[:, t:t + 1], ve[:, t:t + 1], mv[:, t, 1:2], 1.0, 1e-5, 1, A[4]["drstd"])
                        if t >= 1:
                            pool.wait_ge(ln_var, NT * l + t)
                            rsqrt(rstd[:, t - 1:t], ve[:, t - 1:t], mv[:, t - 1, 1:2], 1.0, 1e-5, 1, ln_rstd)
                    pool.wait_ge(ln_var, NT * l + NT)
                    rsqrt(rstd[:, NT - 1:NT], ve[:, NT - 1:NT], mv[:, NT - 1, 1:2], 1.0, 1e-5, 1, ln_rstd)
                    block_diagonal(Vq, 8, False)
                else:
                    ln(l)
                if l == 3:
                    pool.wait_ge(s_late, 16)
                    src, dst = L("w2f"), w2h[:, :]
                    for stage in range(3):
                        n = (1 << stage) * D
                        u = src.rearrange("p (a two n) -> p a two n", two=2, n=n)
                        v = dst.rearrange("p (a two n) -> p a two n", two=2, n=n)
                        for k, op in enumerate((ALU.add, ALU.subtract)):
                            pool.tensor_tensor(v[:, :, k, :], u[:, :, 0, :], u[:, :, 1, :], op).then_inc(w2_bf, 1)
                        pool.wait_ge(w2_bf, 2 * stage + 2)
                        src, dst = dst, src
                if l == 6:
                    rms(A[6], 32, 1.0 / 8, 0)
                    rms(A[6], 32, 1.0 / 8, NT)

        @block.tensor
        def _(pe):
            def mm(o, lhsT, rhs, start=True, stop=True):
                return pe.matmul(o, lhsT, rhs, start=start, stop=stop, skip_group_check=True)

            def rows_by_width(bank, actT, t, w):
                for k in range(KC):
                    ins = mm(ps[:, bank, 0:D], actT[:, k, tok(t)], w[:, k, :], k == 0, k == KC - 1)
                return ins

            def layernorm_T(l):
                for k in range(NT // 2):
                    pe.wait_ge(ln_xn, NT * l + 2 * k + 2)
                    for j in range(2):
                        for c in range(KC):
                            ins = pe.transpose(ps[:, k, j * D + c * P:j * D + (c + 1) * P],
                                               xn[:, 2 * k + j, c * P:(c + 1) * P], ident)
                    ins.then_inc(ln_Tfull, 1)

            def xT_ready(l, tiles):
                pe.wait_ge(ln_xT, (NT // 2) * l + (tiles + 1) // 2)

            def normed_projection(a, actT, w, first, l):
                held = a["normed"] if l == 6 else a["raw"]
                for s in range(NT + 1):
                    if s < NT:
                        m = first + s
                        if first:
                            xT_ready(l, s + 1)
                        if s >= 2:
                            pe.wait_ge(held, m - 1)
                        rows_by_width(4 + s % 2, actT, s, kc(w)).then_inc(a["pr_full"], 1)
                    if s >= 1:
                        m = first + s - 1
                        pe.wait_ge(a["normed"], m + 1)
                        if s >= 3:
                            pe.wait_ge(a["T_done"], m - 1)
                        for c in range(KC):
                            ins = pe.transpose(ps[:, 6 + m % 2, c * P:(c + 1) * P], nrm[:, m % 2, c * P:(c + 1) * P], ident)
                        ins.then_inc(a["T_full"], 1)

            def values(a, w):
                for b in range(B):
                    if b >= 4:
                        pe.wait_ge(a["v_done"], b - 3)
                    for h in range(2):
                        for k in range(KC):
                            ins = mm(ps[h * S:(h + 1) * S, 4 + b % 4, 0:D // 2], ctxT[:, k, b * S:(b + 1) * S],
                                     kc(w)[:, k, h * (D // 2):(h + 1) * (D // 2)], k == 0, k == KC - 1)
                    ins.then_inc(a["v_full"], 1)

            def pv(a, t, bank, lhs, V, n, width):
                for b in range(BT):
                    for j in range(n):
                        ins = mm(ps[b * S:(b + 1) * S, bank, j * width:(j + 1) * width], lhs(j, b),
                                 V[:, BT * t + b, j, :, :].rearrange("p h e -> p (h e)"))
                ins.then_inc(a["pv_full"], 1)

            def out_T(a, t, bank):
                pe.wait_ge(a["o_norm"], t + 1)
                for c in range(KC):
                    ins = pe.transpose(ps[:, bank, c * P:(c + 1) * P], oN[:, t % 2, c * P:(c + 1) * P], ident)
                ins.then_inc(a["oT_full"], 1)

            def out_projection(a, t, bank, w):
                pe.wait_ge(a["oT_ready"], t + 1)
                for k in range(KC):
                    ins = mm(ps[:, bank, D:2 * D], oT[:, t % 2, k * P:(k + 1) * P], kc(w)[:, k, :], k == 0, k == KC - 1)
                ins.then_inc(a["o_proj"], 1)

            a = A[0]
            pe.wait_ge(s_early, 16)
            pe.wait_ge(s_ctxT, 16)
            normed_projection(a, ctxT, E("wk0"), 0, 0)
            pe.wait_ge(a["T_done"], NT)
            pe.wait_ge(a["raw"], NT)
            values(a, E("wv0"))
            layernorm_T(0)
            pe.wait_ge(a["v_done"], B)
            normed_projection(a, xT, E("wq0"), NT, 0)
            pe.wait_ge(a["T_done"], 2 * NT)
            for s in range(NT + 3):
                t = s
                if t < NT:
                    for j in range(4):
                        if t >= 1:
                            pe.wait_ge(a["sc_free"], 4 * (t - 1) + j + 1)
                        g = slice(32 * j, 32 * j + 32)
                        for c in range(KC):
                            for b in range(BT):
                                ins = mm(ps[b * S:(b + 1) * S, j, c * P:(c + 1) * P],
                                         qT[g, c, t * P + b * S:t * P + (b + 1) * S],
                                         Kp[g, c, BT * t + b, :, :].rearrange("p h s -> p (h s)"))
                        ins.then_inc(a["sc_full"], 1)
                t = s - 3
                if 0 <= t:
                    if t >= 1:
                        pe.wait_ge(a["resid"], t)
                    out_T(a, t, 7)
                t = s - 1
                if 0 <= t < NT:
                    pe.wait_ge(a["p_ready"], 4 * t + 4)
                    Pt = probs[:, t % 2, 0:1024].rearrange("p (j n) -> p j n", j=8)
                    if t >= 1:
                        pe.wait_ge(a["pT_act"], t)
                    for n in range(8):
                        if n == 4 and t >= 1:
                            pe.wait_ge(a["pT_dve"], t)
                        ins = pe.transpose(ps[:, 4 + n // 4, (n % 4) * P:(n % 4 + 1) * P], Pt[:, n, :], ident)
                        if n % 4 == 3:
                            ins.then_inc(a["pT_full"], 1)
                t = s - 3
                if 0 <= t:
                    out_projection(a, t, 7, E("wo0"))
                t = s - 2
                if 0 <= t < NT:
                    pe.wait_ge(a["pT_act"], t + 1)
                    pe.wait_ge(a["pT_dve"], t + 1)
                    if t >= 1:
                        pe.wait_ge(a["o_norm"], t)
                    PT = probs[:, t % 2, 1024:2048].rearrange("p (j c n) -> p j c n", j=4, c=KC)
                    pv(a, t, 6, lambda n, b: PT[:, n % 4, n // 4, b * S:(b + 1) * S], Vp, 8, 34)
            def gates_T(l, e):
                f = Fs[l]
                pe.wait_ge(f["gates"], 1)
                gv = g3[:, 0:NT * 3 * e].rearrange("p (t n) -> p t n", t=NT)
                for t in range(NT):
                    ins = pe.transpose(ps[:, 1, :].bitcast(BF16)[0:3 * e, tok(t)], gv[:, t, :], identb[:, :])
                ins.then_inc(f["gT_full"], 1)
                pe.wait_ge(f["gT_ready"], 1)

            def logits(l, w, e):
                for t in range(NT):
                    xT_ready(l, t + 1)
                    for k in range(KC):
                        ins = mm(ps[:, 0, t * e:(t + 1) * e], xT[:, k, tok(t)], w[:, k, :], k == 0, k == KC - 1)
                ins.then_inc(Fs[l]["logits"], 1)

            def up2(o, w, half):
                for k in range(KC):
                    ins = mm(o, w[:, k, :], xT[:, k, half * HALF:(half + 1) * HALF], k == 0, k == KC - 1)
                return ins

            def down_tokens(hid, half, w, first):
                for q in range(4):
                    t = 4 * half + q
                    ins = mm(ps[:, t // 2, (t % 2) * D:(t % 2 + 1) * D], hid[:, q * P:(q + 1) * P], w,
                             first and t % 2 == 0, True)
                return ins

            def at_least(sm, n, low):
                if low >= 1:
                    pe.wait_ge(sm, n)

            def run_units(units, up, down):
                groups = units // 4

                def group(base, low, last, first):
                    for k in range(4):
                        if not (last and k == 3):
                            up(base + (k + 1), low + k + 1, (k + 1) % 4)
                        down(base + k, low + k, k, first and k < 2)
                up(0, 0, 0)
                group(0, 0, groups == 1, True)
                if groups > 2:
                    with pe.Fori(1, groups - 1) as i:
                        group(i * 4, 4, False, False)
                if groups > 1:
                    group(4 * (groups - 1), 4 * (groups - 1), True, False)

            f = Fs[1]
            pe.wait_ge(s_late, 16)
            pe.wait_ge(s_misc, 16 * 6)
            layernorm_T(1)
            logits(1, kc(L("wr0")), E0)
            gates_T(1, E0)
            a0 = L("A0").rearrange("p (k n) -> p k n", k=KC)
            b0 = L("B0").rearrange("p (k n) -> p k n", n=D)

            def up_1(n, low, k):
                c, half = n // 2, n % 2
                at_least(f["act"], n - 1, low - 1)
                up2(ps[:, 4 + 2 * (n % 2), :], a0[:, :, c * P:(c + 1) * P], half).then_inc(f["up"], 1)
                at_least(f["h"], n - 1, low - 1)
                mm(ps[:, 5 + 2 * (n % 2), :], sel0[:, c * P:(c + 1) * P], gT[0:3 * E0, half * HALF:(half + 1) * HALF]
                   ).then_inc(f["cw"], 1)

            def down_1(n, low, k, first):
                pe.wait_ge(f["h"], n + 1)
                down_tokens(sbuf_h[:, n % 2, :], n % 2, b0[:, n // 2, :], first).then_inc(f["down"], 1)

            up_1(0, 0, 0)
            for n in range(FF[1]):
                if n + 1 < FF[1]:
                    up_1(n + 1, n + 1, 0)
                down_1(n, n, 0, n < 2)
            layernorm_T(2)
            for t in range(NT):
                xT_ready(2, t + 1)
                for b in range(BT):
                    for k in range(KC):
                        q = slice(t * P + b * S, t * P + (b + 1) * S)
                        ins = mm(ps[b * S:(b + 1) * S, 4 + t // 4, (t % 4) * S:(t % 4 + 1) * S], xT[:, k, q],
                                 ctxT[:, k, q], k == 0, k == KC - 1)
                if t % 4 == 3:
                    ins.then_inc(a2["sc_full"], 1)
            pe.wait_ge(a2["shift"], 2)
            for s in range(NT + 1):
                if s < NT:
                    pe.wait_ge(a2["p_ready"], 2 * (s // 4) + 2)
                    if s >= 2:
                        pe.wait_ge(a2["pT_ready"], s - 1)
                    pe.transpose(ps[:, 6 + s % 2, 0:P], probs[:, 0, tok(s)], ident).then_inc(a2["pT_full"], 1)
                t = s - 1
                if t >= 0:
                    pe.wait_ge(a2["pT_ready"], t + 1)
                    if t >= 2:
                        pe.wait_ge(a2["resid"], t - 1)
                    mm(ps[:, 4 + t % 2, 0:D], probs[:, 1, (t % 2) * P:(t % 2 + 1) * P], ctx[:, t, :]
                       ).then_inc(a2["pv_full"], 1)
            f3 = Fs[3]
            layernorm_T(3)
            logits(3, kc(L("gate1")), E1 + 1)
            gates_T(3, EP1)
            ring1 = [wring[:, c, 0:KC * 2 * P].rearrange("p (k g n) -> p k g n", k=KC, g=2) for c in range(2)]

            def up_3(n, low, k):
                c, half = k // 2, k % 2
                if half == 0:
                    pe.wait_ge(f3[f"land{c}"], (n - k) * 4 + 16)
                at_least(f3["h"], n - 1, low - 1)
                up2(ps[:, 4 + (3 * k) % 4, :], ring1[c][:, :, 0, :], half)
                at_least(f3["act"], n, low)
                up2(ps[:, 4 + (3 * k + 1) % 4, :], ring1[c][:, :, 1, :], half).then_inc(f3["up"], 1)
                at_least(f3["mid"], n, low)
                if isinstance(n, int):
                    chunk = sel1[:, (n // 2) * P:(n // 2 + 1) * P]
                else:
                    chunk = sel1[:, bass.ds((n - k) * (P // 2) + c * P, P)]
                mm(ps[:, 4 + (3 * k + 2) % 4, :], chunk, gT[0:3 * EP1, half * HALF:(half + 1) * HALF]
                   ).then_inc(f3["cw"], 1)

            def down_3(n, low, k, first):
                pe.wait_ge(f3["h"], n + 1)
                down_tokens(sbuf_h[:, k % 2, :], k % 2, wring[:, k // 2, KC * 2 * P:W1COLS], first).then_inc(f3["down"], 1)

            run_units(FF[3], up_3, down_3)
            a = A[4]

            def projection_T(w, actT, n0):
                for c in range(KC):
                    for half in range(2):
                        for k in range(KC):
                            ins = mm(ps[:, 4 + 2 * c + half, :], w[:, k, c * P:(c + 1) * P],
                                     actT[:, k, half * HALF:(half + 1) * HALF], k == 0, k == KC - 1)
                        ins.then_inc(a["kq_full"], 1)

            projection_T(kc(L("wk2")), ctxT, 0)
            pe.wait_ge(w2_bf, 6)
            for n in range(4):
                pe.wait_ge(a["kq_done"], n + 1)
                mm(ps[:, 4 + n, :], L("had"), w2h[:, n * 512:(n + 1) * 512]).then_inc(w2_mm, 1)
            pe.wait_ge(w2_ev, 4)
            values(a, L("wv2"))
            layernorm_T(4)
            xT_ready(4, NT)
            pe.wait_ge(a["v_done"], B)
            projection_T(kc(L("wq2")), xT, 4)
            pe.wait_ge(a["q_ready"], 4)
            for s in range(NT + 2):
                t = s
                if t < NT:
                    pe.wait_ge(a["k_ready"], 8)
                    if t >= 1:
                        pe.wait_ge(a["sc_free"], t)
                    for j in range(4):
                        g = slice(32 * j, 32 * j + 32)
                        for c in range(KC):
                            for b in range(BT):
                                ins = mm(ps[:, j, c * P + b * S:c * P + (b + 1) * S],
                                         Kp[g, c, BT * t + b, :, :].rearrange("p h s -> p (h s)"),
                                         qT[g, c, t * P + b * S:t * P + (b + 1) * S])
                    ins.then_inc(a["sc_full"], 1)
                t = s - 2
                if t >= 0:
                    if t >= 2:
                        pe.wait_ge(a["resid"], t - 1)
                    out_T(a, t, 6 + t % 2)
                t = s - 1
                if 0 <= t < NT:
                    pe.wait_ge(a["p_ready"], t + 1)
                    if t >= 2:
                        pe.wait_ge(a["o_norm"], t - 1)
                    PT = probs[:, t % 2, 0:1024].rearrange("p (j c n) -> p j c n", j=4, c=KC)
                    pv(a, t, 4 + t % 2, lambda n, b: PT[:, n % 4, n // 4, b * S:(b + 1) * S], Vp, 8, 34)
                t = s - 2
                if t >= 0:
                    out_projection(a, t, 6 + t % 2, L("wo2"))
            f5 = Fs[5]
            layernorm_T(5)
            xT_ready(5, NT)
            ring2 = [wring[:, c, 0:W2COLS].rearrange("p (k g n) -> p k g n", k=KC, g=2) for c in range(2)]

            def up_5(n, low, k):
                c, half = k // 2, k % 2
                if half == 0:
                    pe.wait_ge(f5[f"land{c}"], (n - k) * 4 + 16)
                at_least(f5["act"], n - 1, low - 1)
                up2(ps[:, 4 + 2 * (k % 2), :], ring2[c][:, :, 0, :], half)
                at_least(f5["h"], n - 1, low - 1)
                up2(ps[:, 5 + 2 * (k % 2), :], ring2[c][:, :, 1, :], half).then_inc(f5["up"], 1)

            def down_5(n, low, k, first):
                pe.wait_ge(f5["h"], n + 1)
                at = (n // 2) * D if isinstance(n, int) else (n - k) * (D // 2) + (k // 2) * D
                down_tokens(sbuf_h[:, k % 2, :], k % 2, L("w2f")[:, bass.ds(at, D)], first).then_inc(f5["down"], 1)

            run_units(FF[5], up_5, down_5)
            a = A[6]
            normed_projection(a, ctxT, L("wk3"), 0, 6)
            pe.wait_ge(a["T_done"], NT)
            values(a, L("wv3"))
            layernorm_T(6)
            pe.wait_ge(a["v_done"], B)
            normed_projection(a, xT, L("wq3"), NT, 6)
            pe.wait_ge(a["T_done"], 2 * NT)
            for s in range(NT + 1):
                t = s
                if t < NT:
                    for j in range(4):
                        if t >= 1:
                            pe.wait_ge(a["p_ready"], 4 * (t - 1) + j + 1)
                        g = slice(32 * j, 32 * j + 32)
                        for c in range(KC):
                            for u in range(2):
                                for b in range(BT):
                                    at = (2 * c + u) * P + b * S
                                    ins = mm(ps[:, j, at:at + S],
                                             Kq[g, c, BT * t + b, 2 * u:2 * u + 2, :].rearrange("p m s -> p (m s)"),
                                             qT[g, c, t * P + b * S:t * P + (b + 1) * S])
                        ins.then_inc(a["sc_full"], 1)
                t = s - 1
                if t >= 0:
                    pe.wait_ge(a["p_ready"], 4 * t + 4)
                    if t >= 2:
                        pe.wait_ge(a["o_norm"], t - 1)
                    PT = probs[:, t % 2, :].rearrange("p (j c u n) -> p j c u n", j=4, c=KC, u=2)
                    pv(a, t, 4 + t % 2,
                       lambda n, b: PT[:, (n % 8) // 2, n // 8, n % 2, b * S:(b + 1) * S], Vq, 16, 18)
            f7, f8 = Fs[7], Fs[8]
            layernorm_T(7)
            logits(7, kc(L("gate3")), E3)
            fc1 = kc(L("fc1"))
            for half in range(2):
                for k in range(KC):
                    ins = mm(ps[:, 2 + half, :], fc1[:, k, :], xT[:, k, half * HALF:(half + 1) * HALF],
                             k == 0, k == KC - 1)
                ins.then_inc(s_lat, 1)
            gates_T(7, E3)
            pe.wait_ge(s_sel3, 16)
            pe.wait_ge(s_latE, 2)

            def up_7(n, low, k):
                c, half = k // 2, k % 2
                if half == 0:
                    pe.wait_ge(f7[f"land{c}"], (n - k) * 4 + 16)
                at_least(f7["act"], n - 1, low - 1)
                mm(ps[:, 4 + 2 * (k % 2), :], wring[:, c, 0:P], qT[:, 0, half * HALF:(half + 1) * HALF]
                   ).then_inc(f7["up"], 1)
                at_least(f7["mid"], n - 1, low - 1)
                if isinstance(n, int):
                    chunk = sel3[:, (n // 2) * P:(n // 2 + 1) * P]
                else:
                    chunk = sel3[:, bass.ds((n - k) * (P // 2) + c * P, P)]
                mm(ps[:, 5 + 2 * (k % 2), :], chunk, gT[0:3 * E3, half * HALF:(half + 1) * HALF]).then_inc(f7["cw"], 1)

            def down_7(n, low, k, first):
                pe.wait_ge(f7["h"], n + 1)
                mm(ps[:, k % 2, :], wring[:, k // 2, P:P + LAT3], sbuf_h[:, k % 2, :], first, True).then_inc(f7["down"], 1)

            run_units(FF[7], up_7, down_7)
            u3 = L("up3").rearrange("p (c k n) -> p c k n", c=C3S, k=KC)
            d3 = L("down3").rearrange("p (c n) -> p c n", c=C3S)

            def up_8(n):
                if n >= 4:
                    pe.wait_ge(f8["act"], n - 3)
                up2(ps[:, 4 + n % 4, :], u3[:, n // 2, :, :], n % 2).then_inc(f8["up"], 1)

            up_8(0)
            up_8(1)
            pe.wait_ge(s_yl, 2)
            for t in range(NT):
                mm(ps[:, t // 2, (t % 2) * D:(t % 2 + 1) * D], qT[:, 1, tok(t)], L("fc2"), t % 2 == 0, True)
            for n in range(FF[8]):
                if n + 2 < FF[8]:
                    up_8(n + 2)
                pe.wait_ge(f8["h"], n + 1)
                down_tokens(sbuf_h[:, n % 2, :], n % 2, d3[:, n // 2, :], False).then_inc(f8["down"], 1)

        @block.scalar
        def _(act):
            def copy(o, i):
                return nc.scalar.activation(o, i, ACT.Copy)

            def layernorm_evac(l):
                for k in range(NT // 2):
                    act.wait_ge(ln_Tfull, (NT // 2) * l + k + 1)
                    copy(xT[:, :, 2 * k * P:2 * (k + 1) * P].rearrange("p c (t n) -> p t c n", t=2),
                         ps[:, k, :].rearrange("p (t c n) -> p t c n", t=2, c=KC)).then_inc(ln_xT, 1)

            def keys_masked(a, m, t, K, heads, mask, src, src_b):
                for h in range(heads):
                    ins = nc.scalar.activation(K[:, :, BT * t:BT * t + src_b, h, :], src, ACT.Copy,
                                               scale=mask[:, h:h + 1])
                return ins

            def normed_projection(a, first, l):
                for s in range(NT + 1):
                    if s < NT:
                        m = first + s
                        if l == 6:
                            act.wait_ge(a["pr_full"], m + 1)
                            if m >= 2:
                                act.wait_ge(a["ss"], m - 1)
                            nc.scalar.activation(junk[:, m % 2, :], ps[:, 4 + s % 2, 0:D], ACT.Square).then_inc(a["sq"], 1)
                        else:
                            act.wait_ge(a["raw"], m + 1)
                            if m >= 2:
                                act.wait_ge(a["rms"], m - 1)
                            nc.scalar.activation(junk[:, m % 2, :], raw[:, m % 2, :], ACT.Square,
                                                 accum_out=ss[:, m % 2, 0:1]).then_inc(a["ss"], 1)
                    if s >= 1:
                        m = first + s - 1
                        t = s - 1
                        act.wait_ge(a["T_full"], m + 1)
                        bank = ps[:, 6 + m % 2, 0:D]
                        if first:
                            copy(qT[:, :, tok(t)], bank.rearrange("p (c n) -> p c n", c=KC)).then_inc(a["T_done"], 1)
                        else:
                            K, heads, mask = (Kq, 4, E("quad")) if l == 6 else (Kp, 2, E("pair"))
                            keys_masked(a, m, t, K, heads, mask, bank.rearrange("p (c b s) -> p c b s", c=KC, b=BT),
                                        BT).then_inc(a["T_done"], 1)

            def out_T_evac(a, t, bank):
                act.wait_ge(a["oT_full"], t + 1)
                copy(oT[:, t % 2, :], ps[:, bank, 0:D]).then_inc(a["oT_ready"], 1)

            a = A[0]
            act.wait_ge(s_rows, 16)
            nc.scalar.activation(tg[:, :], R("gates"), ACT.Tanh).then_inc(s_tanh, 1)
            act.wait_ge(s_early, 16)
            normed_projection(a, 0, 0)
            layernorm_evac(0)
            normed_projection(a, NT, 0)
            for s in range(NT + 3):
                t = s
                if t < NT:
                    for j in range(4):
                        act.wait_ge(a["sc_free"], 4 * t + j + 1)
                        v = probs[:, t % 2, j * D:(j + 1) * D]
                        nc.scalar.activation(v, v, ACT.Exp, scale=0.25).then_inc(a["p_ready"], 1)
                t = s - 1
                if 0 <= t < NT:
                    act.wait_ge(a["pT_full"], 2 * t + 1)
                    if t >= 2:
                        act.wait_ge(a["pv_full"], t - 1)
                    copy(probs[:, t % 2, 1024:1536], ps[:, 4, :]).then_inc(a["pT_act"], 1)
                t = s - 3
                if t >= 0:
                    out_T_evac(a, t, 7)
            def gates_evac(l, e):
                f = Fs[l]
                act.wait_ge(f["gT_full"], 1)
                copy(gT[0:3 * e, :], ps[:, 1, :].bitcast(BF16)[0:3 * e, :]).then_inc(f["gT_ready"], 1)

            def run_units(units, one):
                for k in range(4):
                    one(k, k, k)
                with act.Fori(1, units // 4) as i:
                    for k in range(4):
                        one(i * 4 + k, 4 + k, k)

            def unit(f, func, bank, o_free):
                def one(n, low, k):
                    act.wait_ge(f["up"], n + 1)
                    if low >= 2:
                        act.wait_ge(f[o_free], n - 1)
                    nc.scalar.activation(sbuf_s[:, k % 2, :], ps[:, bank(k), :], func).then_inc(f["act"], 1)
                return one

            f = Fs[1]
            layernorm_evac(1)
            act.wait_ge(f["lread"], 1)
            nc.scalar.activation(lb[:, 0:NT * E0], la[:, 0:NT * E0], ACT.Exp).then_inc(f["e"], 1)
            gates_evac(1, E0)
            for n in range(FF[1]):
                unit(f, ACT.Copy, lambda k: 4 + 2 * (k % 2), "h")(n, n, n)
            layernorm_evac(2)
            pd = probs[:, 0, 0:NT * P].rearrange("p (t n) -> p t n", t=NT)
            sv = cr[:, :].rearrange("p (t n) -> p t n", t=NT)
            for half in range(2):
                act.wait_ge(a2["shift"], half + 1)
                for b in range(BT):
                    r, ts = slice(b * S, (b + 1) * S), slice(4 * half, 4 * half + 4)
                    nc.scalar.activation(pd[r, ts, b * S:(b + 1) * S], sv[r, ts, :], ACT.Exp,
                                         scale=D ** -0.5).then_inc(a2["p_ready"], 1)
            for t in range(NT):
                act.wait_ge(a2["pT_full"], t + 1)
                if t >= 2:
                    act.wait_ge(a2["pv_full"], t - 1)
                copy(probs[:, 1, (t % 2) * P:(t % 2 + 1) * P], ps[:, 6 + t % 2, 0:P]).then_inc(a2["pT_ready"], 1)
            f = Fs[3]
            layernorm_evac(3)
            lg17 = lg[:, 0:NT * (E1 + 1)].rearrange("p (t e) -> p t e", t=NT)
            act.wait_ge(f["lread"], 1)
            nc.scalar.activation(rk[:, 0:NT], lg17[:, :, E1], ACT.Exp, scale=-1.0).then_inc(f["e"], 1)
            act.wait_ge(f["lread"], 2)
            nc.scalar.activation(lb[:, 0:NT * E1], lb[:, 0:NT * E1], ACT.Exp).then_inc(f["e"], 1)
            gates_evac(3, EP1)
            run_units(FF[3], unit(f, ACT.Silu, lambda k: 4 + (3 * k) % 4, "h"))
            a = A[4]
            for g in range(4):
                c, half = g // 2, g % 2
                act.wait_ge(a["kq_done"], g + 1)
                src = (raw if g % 2 == 0 else nrm)[:, :, :].rearrange("p a n -> p (a n)")
                for h in range(2):
                    nc.scalar.activation(Kp[:, c, half * 8:half * 8 + 8, h, :], src.rearrange("p (b s) -> p b s", s=S),
                                         ACT.Copy, scale=E("pair")[:, h:h + 1]).then_inc(a["k_ready"], 1)
            for n in range(4):
                act.wait_ge(w2_mm, n + 1)
                nc.scalar.activation(L("w2f")[:, n * 512:(n + 1) * 512], ps[:, 4 + n, :], ACT.Copy,
                                     scale=1.0 / 32).then_inc(w2_ev, 1)
            layernorm_evac(4)
            for s in range(NT + 2):
                t = s
                if t < NT:
                    act.wait_ge(a["sc_free"], t + 1)
                    v = probs[:, t % 2, 0:1024]
                    nc.scalar.activation(v, v, ACT.Exp, scale=0.25).then_inc(a["p_ready"], 1)
                t = s - 2
                if t >= 0:
                    out_T_evac(a, t, 6 + t % 2)
            layernorm_evac(5)
            run_units(FF[5], unit(Fs[5], ACT.Silu, lambda k: 4 + 2 * (k % 2), "h"))
            a = A[6]
            normed_projection(a, 0, 6)
            layernorm_evac(6)
            normed_projection(a, NT, 6)
            for t in range(NT):
                for j in range(4):
                    act.wait_ge(a["sc_full"], 4 * t + j + 1)
                    if t >= 2:
                        act.wait_ge(a["pv_full"], t - 1)
                    nc.scalar.activation(probs[:, t % 2, j * 512:(j + 1) * 512], ps[:, j, :], ACT.Exp,
                                         scale=8 ** -0.5).then_inc(a["p_ready"], 1)
            f = Fs[7]
            layernorm_evac(7)
            act.wait_ge(f["logits"], 1)
            nc.scalar.activation(lb[:, :], ps[:, 0, 0:NT * E3], ACT.Exp, scale=-1.0).then_inc(f["e"], 1)
            for half in range(2):
                act.wait_ge(s_lat, half + 1)
                copy(qT[:, 0, half * HALF:(half + 1) * HALF], ps[:, 2 + half, :]).then_inc(s_latE, 1)
            gates_evac(7, E3)
            run_units(FF[7], unit(f, ACT.Relu, lambda k: 4 + 2 * (k % 2), "h"))
            act.wait_ge(f["down"], FF[7])
            for half in range(2):
                copy(qT[:, 1, half * HALF:(half + 1) * HALF], ps[:, half, :]).then_inc(s_yl, 1)
            for n in range(FF[8]):
                unit(Fs[8], ACT.Relu, lambda k: 4 + k % 4, "h")(n, n, n)

        @block.vector
        def _(v):
            ch = Chain(v, s_dve)
            link = ch.link

            def ln_stats(l, t):
                link(v.bn_stats(st[:, t, :], x[:, t, :]))
                v.bn_aggr(mv[:, t, :], st[:, t, :]).then_inc(ln_var, 1)

            def ln_norm(l, t):
                v.wait_ge(ln_rstd, NT * l + t + 1)
                v.tensor_scalar(xn[:, t, :], x[:, t, :], mv[:, t, 0:1], rstd[:, t:t + 1], ALU.subtract,
                                ALU.mult).then_inc(ln_xn, 1)

            def normed_projection(a, first, l):
                bias, gain = (R("bq0"), R("gq0")) if first else (R("bk0"), R("gk0"))
                for s in range(NT + 1):
                    if s < NT:
                        m = first + s
                        if l == 6:
                            v.wait_ge(a["sq"], m + 1)
                            v.tensor_reduce(ss[:, m % 2, 0:32], junk[:, m % 2, :].rearrange("p (h e) -> p h e", e=8),
                                            AX.X, ALU.add).then_inc(a["ss"], 1)
                        else:
                            v.wait_ge(a["pr_full"], m + 1)
                            if m >= 2:
                                v.wait_ge(a["ss"], m - 1)
                            v.tensor_tensor(raw[:, m % 2, :], ps[:, 4 + s % 2, 0:D], bias, ALU.add).then_inc(a["raw"], 1)
                    if s >= 1:
                        m = first + s - 1
                        v.wait_ge(a["rms"], m + 1)
                        if m >= 2:
                            v.wait_ge(a["T_full"], m - 1)
                        if l == 6:
                            v.tensor_tensor(nrm[:, m % 2, :].rearrange("p (h e) -> p h e", e=8),
                                            ps[:, 4 + (s - 1) % 2, 0:D].rearrange("p (h e) -> p h e", e=8),
                                            ssr[:, m % 2, 0:32].unsqueeze(2).to_broadcast([P, 32, 8]),
                                            ALU.mult).then_inc(a["normed"], 1)
                        else:
                            v.scalar_tensor_tensor(out=nrm[:, m % 2, :], in0=raw[:, m % 2, :],
                                                   scalar=ssr[:, m % 2, 0:1], in1=gain, op0=ALU.mult,
                                                   op1=ALU.mult).then_inc(a["normed"], 1)

            def values(a, V, e, bias):
                for b in range(B):
                    v.wait_ge(a["v_full"], b + 1)
                    for h in range(2):
                        r = slice(h * S, (h + 1) * S)
                        src = ps[r, 4 + b % 4, 0:D // 2].rearrange("p (j e) -> p j e", e=e)
                        dst = V[r, b, :, h, 0:e]
                        if bias is None:
                            ins = v.tensor_copy(dst, src)
                        else:
                            ins = v.tensor_tensor(dst, src,
                                                  bias[r, h * (D // 2):(h + 1) * (D // 2)].rearrange("p (j e) -> p j e", e=e),
                                                  ALU.add)
                    ins.then_inc(a["v_done"], 1)

            def gate(l):
                return tg[:, (l // 2 if l % 2 == 0 else 4 + l // 2):][:, 0:1]

            def clean(ap, n):
                c, m = cr[:, 0:n], cm[:, 0:n]
                link(v.tensor_scalar(c, ap, 0.0, 1e4, ALU.max, ALU.min))
                v.tensor_scalar(m, ap, 0.0, 0.0, ALU.mult, ALU.not_equal)
                link(v.scalar_tensor_tensor(out=c, in0=ap, scalar=0.0, in1=c, op0=ALU.min, op1=ALU.add))
                link(v.tensor_scalar(c, c, -1e4, None, ALU.max))
                return v.copy_predicated(ap, m, c)

            def head_norm(a, t, bank, heads, e, eps):
                par = t % 2
                o = ps[:, bank, 0:heads * (e + 1)].rearrange("p (h e) -> p h e", e=e + 1)
                r = rden[:, par, 0:heads]
                if eps:
                    d = den2[:, par, 0:heads]
                    link(v.tensor_copy(d, o[:, :, e]))
                    link(v.scalar_tensor_tensor(out=d, in0=d, scalar=1e-8, in1=d, op0=ALU.mult, op1=ALU.add))
                    link(v.reciprocal(r, d))
                else:
                    link(v.reciprocal(r, o[:, :, e]))
                return v.tensor_tensor(oN[:, par, :].rearrange("p (h e) -> p h e", e=e), o[:, :, 0:e],
                                       r.unsqueeze(2).to_broadcast([P, heads, e]), ALU.mult)

            def residual(l, t, done, src, scalar):
                link(v.scalar_tensor_tensor(out=x[:, t, :], in0=src, scalar=scalar, in1=x[:, t, :], op0=ALU.mult,
                                            op1=ALU.add))
                if l + 1 < NL:
                    link(v.bn_stats(st[:, t, :], x[:, t, :]))
                    v.bn_aggr(mv[:, t, :], st[:, t, :]).then_inc(ln_var, 1)
                v.sem_inc(done, 1)

            a = A[0]
            v.wait_ge(s_x, 16)
            for t in range(NT):
                ln_stats(0, t)
                if t >= 2:
                    ln_norm(0, t - 2)
            for t in range(NT - 2, NT):
                ln_norm(0, t)
            v.wait_ge(s_rows, 16)
            normed_projection(a, 0, 0)
            v.wait_ge(s_cst, 4)
            values(a, Vp, 16, R("bv0"))
            normed_projection(a, NT, 0)
            v.wait_ge(s_tanh, 1)
            for s in range(NT + 4):
                t = s
                if t < NT:
                    for j in range(4):
                        v.wait_ge(a["sc_full"], 4 * t + j + 1)
                        if t >= 2 and j == 0:
                            v.wait_ge(a["pT_full"], 2 * (t - 1))
                        sc = ps[:, j, 0:D].rearrange("p (h s) -> p h s", s=S)
                        mj = mx[:, t % 2, 4 * j:4 * j + 4]
                        link(v.tensor_reduce(mj, sc, AX.X, ALU.max))
                        v.tensor_tensor(probs[:, t % 2, j * D:(j + 1) * D].rearrange("p (h s) -> p h s", s=S), sc,
                                        mj.unsqueeze(2).to_broadcast([P, 4, S]), ALU.subtract).then_inc(a["sc_free"], 1)
                t = s - 1
                if 0 <= t < NT:
                    v.wait_ge(a["pT_full"], 2 * t + 2)
                    v.tensor_copy(probs[:, t % 2, 1536:2048], ps[:, 5, :]).then_inc(a["pT_dve"], 1)
                t = s - 2
                if 0 <= t < NT:
                    v.wait_ge(a["pv_full"], t + 1)
                    head_norm(a, t, 6, 16, 16, False).then_inc(a["o_norm"], 1)
                t = s - 3
                if 0 <= t < NT:
                    v.wait_ge(a["o_proj"], t + 1)
                    link(v.tensor_tensor(junk[:, t % 2, :], ps[:, 7, D:2 * D], R("bo0"), ALU.add))
                    residual(0, t, a["resid"], junk[:, t % 2, :], gate(0))
                t = s - 4
                if 0 <= t:
                    ln_norm(1, t)
            def view(buf, e):
                return buf[:, 0:NT * e].rearrange("p (t e) -> p t e", t=NT)

            def over(small, e):
                return small.unsqueeze(2).to_broadcast([P, NT, e])

            def split(g, e, f):
                gv = g3[:, 0:NT * 3 * e].rearrange("p (t k e) -> p t k e", t=NT, k=3)
                r1, r2 = view(lc, e), view(la, e)
                link(v.tensor_copy(gv[:, :, 0, :], g))
                link(v.tensor_tensor(r1, g, gv[:, :, 0, :], ALU.subtract))
                link(v.tensor_copy(gv[:, :, 1, :], r1))
                link(v.tensor_tensor(r2, r1, gv[:, :, 1, :], ALU.subtract))
                v.tensor_copy(gv[:, :, 2, :], r2).then_inc(f["gates"], 1)

            def run_units(units, one):
                for k in range(4):
                    one(k, k, k)
                with v.Fori(1, units // 4) as i:
                    for k in range(4):
                        one(i * 4 + k, 4 + k, k)

            def ffn_residual(l, f, units):
                for t in range(NT + 1):
                    if t < NT:
                        v.wait_ge(f["down"], units - 1 + t // 4)
                        residual(l, t, f["resid"], ps[:, t // 2, (t % 2) * D:(t % 2 + 1) * D], gate(l))
                    if t >= 1:
                        ln_norm(l + 1, t - 1)

            f = Fs[1]
            v.wait_ge(f["logits"], 1)
            lgv, lav, lbv, lcv, ldv = (view(b_, E0) for b_ in (lg, la, lb, lc, ld))
            link(v.tensor_tensor(lgv, ps[:, 0, 0:NT * E0].rearrange("p (t e) -> p t e", t=NT),
                                 R("br0").unsqueeze(1).to_broadcast([P, NT, E0]), ALU.add))
            link(v.tensor_reduce(red[:, :], lgv, AX.X, ALU.max))
            v.tensor_tensor(lav, lgv, over(red[:, :], E0), ALU.subtract).then_inc(f["lread"], 1)
            v.wait_ge(f["lread"], 1)
            link(v.tensor_scalar(lcv, lav, 0.0, None, ALU.is_ge))
            link(v.tensor_tensor(ldv, lcv, R("first8").unsqueeze(1).to_broadcast([P, NT, E0]), ALU.mult))
            link(v.tensor_reduce(red2[:, :], ldv, AX.X, ALU.max))
            link(v.tensor_tensor(lcv, ldv, over(red2[:, :], E0), ALU.is_equal))
            v.wait_ge(f["e"], 1)
            link(v.tensor_reduce(vm[:, :], lbv, AX.X, ALU.add))
            link(v.reciprocal(red[:, :], vm[:, :]))
            link(v.tensor_scalar(red[:, :], red[:, :], 1.0 / R0, None, ALU.mult))
            link(v.tensor_tensor(ldv, lcv, over(red[:, :], E0), ALU.mult))
            split(ldv, E0, f)

            def one_1(n, low, k):
                v.wait_ge(f["act"], n + 1)
                v.wait_ge(f["cw"], n + 1)
                if low >= 2:
                    v.wait_ge(f["down"], n - 1)
                v.tensor_tensor(sbuf_h[:, k % 2, :], sbuf_s[:, k % 2, :], ps[:, 5 + 2 * (k % 2), :],
                                ALU.mult).then_inc(f["h"], 1)

            for n in range(FF[1]):
                one_1(n, n, n)
            v.wait_ge(s_misc, 16 * 6)
            link(v.tensor_copy(m32[:, :, :], m8[:, :, :]))
            link(v.tensor_reduce(vm[:, :], m32[:, :, :], AX.X, ALU.max))
            v.memset(cr[:, :], NEG * D ** 0.5)
            link(v.memset(probs[:, 0, 0:NT * P], 0.0))
            ffn_residual(1, f, FF[1])
            sv = cr[:, :].rearrange("p (t n) -> p t n", t=NT)
            for half in range(2):
                ts = slice(4 * half, 4 * half + 4)
                v.wait_ge(a2["sc_full"], half + 1)
                link(v.copy_predicated(sv[:, ts, :], m32[:, ts, :],
                                       ps[:, 4 + half, 0:4 * S].rearrange("p (t n) -> p t n", t=4)))
                link(v.tensor_reduce(red[:, ts], sv[:, ts, :], AX.X, ALU.max))
                v.tensor_tensor(sv[:, ts, :], sv[:, ts, :], red[:, ts].unsqueeze(2).to_broadcast([P, 4, S]),
                                ALU.subtract).then_inc(a2["shift"], 1)
            pd = probs[:, 0, 0:NT * P].rearrange("p (t n) -> p t n", t=NT)
            v.wait_ge(a2["p_ready"], 4)
            link(v.tensor_reduce(red2[:, :], pd, AX.X, ALU.add))
            link(v.reciprocal(red2[:, :], red2[:, :]))
            link(v.tensor_tensor(red2[:, :], red2[:, :], vm[:, :], ALU.mult))
            link(v.tensor_scalar(red2[:, :], red2[:, :], gate(2), None, ALU.mult))
            for t in range(NT + 1):
                if t < NT:
                    v.wait_ge(a2["pv_full"], t + 1)
                    residual(2, t, a2["resid"], ps[:, 4 + t % 2, 0:D], red2[:, t:t + 1])
                if t >= 1:
                    ln_norm(3, t - 1)
            f3 = Fs[3]
            EX = E1 + 8 - TOP1
            lc20, la20 = (b_[:, 0:NT * EX].rearrange("p (t e) -> p t e", t=NT) for b_ in (lc, la))
            lg17, ld24 = view(lg, E1 + 1), view(ld, EP1)
            lbv = view(lb, E1)
            t8 = top8[:, 0:NT * 8].rearrange("p (t e) -> p t e", t=NT)
            link(v.memset(lc20[:, :, E1:EX], BIG))
            v.wait_ge(f3["logits"], 1)
            v.tensor_copy(lg17, ps[:, 0, 0:NT * (E1 + 1)].rearrange("p (t e) -> p t e", t=NT)).then_inc(f3["lread"], 1)
            v.wait_ge(f3["lread"], 1)
            link(v.tensor_copy(lc20[:, :, 0:E1], lg17[:, :, 0:E1]))
            for t in range(NT):
                ins = v.max(t8[:, t, :], lc20[:, t, :])
            link(ins)
            v.tensor_tensor(lbv, lg17[:, :, 0:E1], over(t8[:, :, 8 - TOP1], E1), ALU.subtract).then_inc(f3["lread"], 1)
            for t in range(NT):
                ins = v.match_replace(out=la20[:, t, :], in_to_replace=t8[:, t, :], in_values=lc20[:, t, :],
                                      imm_value=-BIG)
            link(ins)
            link(v.tensor_tensor(la20, la20, lc20, ALU.not_equal))
            v.wait_ge(f3["e"], 2)
            link(v.tensor_tensor(lbv, lbv, la20[:, :, 0:E1], ALU.mult))
            link(v.tensor_reduce(red[:, :], lbv, AX.X, ALU.add))
            link(v.reciprocal(red[:, :], red[:, :]))
            link(v.memset(ld24[:, :, E1 + 1:EP1], 0.0))
            v.tensor_tensor(ld24[:, :, 0:E1], lbv, over(red[:, :], E1), ALU.mult)
            link(v.tensor_scalar(rk[:, 0:NT], rk[:, 0:NT], 1.0, None, ALU.add))
            link(v.reciprocal(ld24[:, :, E1], rk[:, 0:NT]))
            split(ld24, EP1, f3)

            def one_3(n, low, k):
                v.wait_ge(f3["act"], n + 1)
                if low >= 1:
                    v.wait_ge(f3["h"], n)
                v.tensor_tensor(sbuf_t[:, k % 2, :], sbuf_s[:, k % 2, :], ps[:, 4 + (3 * k + 1) % 4, :],
                                ALU.mult).then_inc(f3["mid"], 1)
                v.wait_ge(f3["mid"], n + 1)
                v.wait_ge(f3["cw"], n + 1)
                if low >= 2:
                    v.wait_ge(f3["down"], n - 1)
                v.tensor_tensor(sbuf_h[:, k % 2, :], sbuf_t[:, k % 2, :], ps[:, 4 + (3 * k + 2) % 4, :],
                                ALU.mult).then_inc(f3["h"], 1)

            run_units(FF[3], one_3)
            ffn_residual(3, f3, FF[3])
            a = A[4]
            bqk = L("bqk2")
            link(v.tensor_scalar(hi2[:, :], mraw[:, :], 0.5, 400.0, ALU.is_gt, ALU.mult))
            link(v.tensor_scalar(hi2[:, :], hi2[:, :], -200.0, None, ALU.add))
            link(v.tensor_scalar(rs[:, :], R("rs2"), 0.0, 0.3, ALU.max, ALU.min))
            for g in range(4):
                c = g // 2
                v.wait_ge(a["kq_full"], g + 1)
                if g >= 2:
                    v.wait_ge(a["k_ready"], 2 * (g - 1))
                dst = (raw if g % 2 == 0 else nrm)[:, :, :].rearrange("p a n -> p (a n)")
                link(v.tensor_scalar(dst, ps[:, 4 + g, :], bqk[:, KC + c:KC + c + 1], None, ALU.add))
                clean(dst, HALF).then_inc(a["kq_done"], 1)
            values(a, Vp, 16, R("bv2"))
            v.wait_ge(a["v_done"], B)
            for at in range(0, B * 272, HALF):
                n = min(HALF, B * 272 - at)
                link(clean(vpair[:, at:at + n], n))
            for g in range(4):
                c, half = g // 2, g % 2
                v.wait_ge(a["kq_full"], 4 + g + 1)
                dst = qT[:, c, half * HALF:(half + 1) * HALF]
                link(v.tensor_scalar(dst, ps[:, 4 + g, :], bqk[:, c:c + 1], None, ALU.add))
                clean(dst, HALF).then_inc(a["q_ready"], 1)
            for s in range(NT + 4):
                t = s
                if t < NT:
                    v.wait_ge(a["sc_full"], t + 1)
                    if t >= 2:
                        v.wait_ge(a["pv_full"], t - 1)
                    for b in range(BT):
                        ins = v.tensor_scalar(
                            probs[:, t % 2, 0:1024].rearrange("p (j c b n) -> p j c b n", j=4, c=KC, b=BT)[:, :, :, b, :],
                            ps[:, 0:4, 0:D].rearrange("p j (c b n) -> p j c b n", c=KC, b=BT)[:, :, :, b, :],
                            hi2[:, BT * t + b:BT * t + b + 1], -200.0, ALU.min, ALU.max)
                    ins.then_inc(a["sc_free"], 1)
                t = s - 1
                if 0 <= t < NT:
                    v.wait_ge(a["pv_full"], t + 1)
                    head_norm(a, t, 4 + t % 2, 16, 16, True).then_inc(a["o_norm"], 1)
                t = s - 2
                if 0 <= t < NT:
                    v.wait_ge(a["o_proj"], t + 1)
                    d = junk[:, t % 2, :]
                    link(v.tensor_tensor(d, ps[:, 6 + t % 2, D:2 * D], R("bo2"), ALU.add))
                    link(clean(d, D))
                    link(v.tensor_scalar(d, d, rs[:, 0:1], None, ALU.mult))
                    link(v.bn_stats(st[:, t, :], d))
                    v.bn_aggr(mv[:, t, :], st[:, t, :]).then_inc(a["dvar"], 1)
                t = s - 3
                if 0 <= t < NT:
                    d = junk[:, t % 2, :]
                    v.wait_ge(a["drstd"], t + 1)
                    link(v.tensor_scalar(d, d, mv[:, t, 0:1], rstd[:, t:t + 1], ALU.subtract, ALU.mult))
                    link(v.tensor_tensor(d, d, R("gamma2"), ALU.mult))
                    link(v.tensor_tensor(d, d, R("beta2"), ALU.add))
                    residual(4, t, a["resid"], d, gate(4))
                t = s - 4
                if 0 <= t:
                    ln_norm(5, t)
            f5 = Fs[5]

            def one_5(n, low, k):
                v.wait_ge(f5["act"], n + 1)
                if low >= 2:
                    v.wait_ge(f5["down"], n - 1)
                v.tensor_tensor(sbuf_h[:, k % 2, :], sbuf_s[:, k % 2, :], ps[:, 5 + 2 * (k % 2), :],
                                ALU.mult).then_inc(f5["h"], 1)

            run_units(FF[5], one_5)
            ffn_residual(5, f5, FF[5])
            a = A[6]
            normed_projection(a, 0, 6)
            v.wait_ge(s_vq, 2)
            values(a, Vq, 8, None)
            normed_projection(a, NT, 6)
            for t in range(NT + 1):
                if t < NT:
                    v.wait_ge(a["pv_full"], t + 1)
                    link(head_norm(a, t, 4 + t % 2, 32, 8, False))
                    v.sem_inc(a["o_norm"], 1)
                    residual(6, t, a["resid"], oN[:, t % 2, :], gate(6))
                if t >= 1:
                    ln_norm(7, t - 1)
            f7, f8 = Fs[7], Fs[8]
            sig, sbv, mk, rep = la, lg, lc, ld
            v.wait_ge(f7["e"], 1)
            link(v.tensor_scalar(lb[:, :], lb[:, :], 1.0, None, ALU.add))
            link(v.reciprocal(sig[:, :], lb[:, :]))
            link(v.tensor_tensor(view(sbv, E3), view(sig, E3), R("bias3").unsqueeze(1).to_broadcast([P, NT, E3]),
                                 ALU.add))
            for g in range(NT * G3):
                ins = v.max(top8[:, g * 8:g * 8 + 8], sbv[:, g * 8:g * 8 + 8])
            link(ins)
            tops = top8[:, :].rearrange("p (g e) -> p g e", e=8)
            link(v.tensor_tensor(gsc[:, :], tops[:, :, 0], tops[:, :, 1], ALU.add))
            gs = gsc[:, :].rearrange("p (t g) -> p t g", t=NT)
            other = gs.unsqueeze(2).to_broadcast([P, NT, G3, G3])
            own = gs.unsqueeze(3).to_broadcast([P, NT, G3, G3])
            r4, r4b = (b_[:, :].rearrange("p (t g o) -> p t g o", t=NT, g=G3) for b_ in (rk, rk2))
            v.tensor_tensor(r4, other, own, ALU.is_gt)
            link(v.tensor_tensor(r4b, other, own, ALU.is_equal))
            link(v.tensor_tensor(rk2[:, :].rearrange("p (t n) -> p t n", t=NT), rk2[:, :].rearrange("p (t n) -> p t n", t=NT),
                                 R("lower4").unsqueeze(1).to_broadcast([P, NT, G3 * G3]), ALU.mult))
            link(v.tensor_tensor(rk[:, :], rk[:, :], rk2[:, :], ALU.add))
            link(v.tensor_reduce(gsd[:, :], rk[:, :].rearrange("p (g o) -> p g o", o=G3), AX.X, ALU.add))
            link(v.tensor_scalar(gsd[:, :], gsd[:, :], TOPG3 - 0.5, None, ALU.is_lt))
            link(v.tensor_scalar(gsc[:, :], gsd[:, :], -NEG, NEG, ALU.mult, ALU.add))

            def by_group(buf):
                return buf[:, :].rearrange("p (g e) -> p g e", e=8)

            link(v.tensor_tensor(by_group(mk), by_group(sbv), gsd[:, :].unsqueeze(2).to_broadcast([P, NT * G3, 8]), ALU.mult))
            link(v.tensor_tensor(by_group(mk), by_group(mk), gsc[:, :].unsqueeze(2).to_broadcast([P, NT * G3, 8]), ALU.add))
            for t in range(NT):
                ins = v.max(top8[:, t * 8:t * 8 + 8], mk[:, t * E3:(t + 1) * E3])
            link(ins)
            for t in range(NT):
                ins = v.match_replace(out=rep[:, t * E3:(t + 1) * E3], in_to_replace=top8[:, t * 8:t * 8 + 8],
                                      in_values=mk[:, t * E3:(t + 1) * E3], imm_value=-BIG)
            link(ins)
            link(v.tensor_tensor(rep[:, :], rep[:, :], mk[:, :], ALU.not_equal))
            link(v.tensor_tensor(lb[:, :], sig[:, :], rep[:, :], ALU.mult))
            link(v.tensor_reduce(red[:, :], view(lb, E3), AX.X, ALU.add))
            link(v.reciprocal(red[:, :], red[:, :]))
            link(v.tensor_scalar(red[:, :], red[:, :], SCALE3, None, ALU.mult))
            link(v.tensor_tensor(view(ld, E3), view(lb, E3), over(red[:, :], E3), ALU.mult))
            split(view(ld, E3), E3, f7)

            def one_7(n, low, k):
                v.wait_ge(f7["act"], n + 1)
                v.wait_ge(f7["cw"], n + 1)
                if low >= 1:
                    v.wait_ge(f7["h"], n)
                v.tensor_tensor(sbuf_t[:, k % 2, :], sbuf_s[:, k % 2, :], ps[:, 5 + 2 * (k % 2), :],
                                ALU.mult).then_inc(f7["mid"], 1)
                v.wait_ge(f7["mid"], n + 1)
                if low >= 2:
                    v.wait_ge(f7["down"], n - 1)
                v.tensor_tensor(sbuf_h[:, k % 2, :], sbuf_t[:, k % 2, :], sbuf_s[:, k % 2, :],
                                ALU.mult).then_inc(f7["h"], 1)

            run_units(FF[7], one_7)
            for n in range(FF[8]):
                v.wait_ge(f8["act"], n + 1)
                if n >= 2:
                    v.wait_ge(f8["down"], n - 1)
                else:
                    v.wait_ge(f7["down"], FF[7])
                v.tensor_tensor(sbuf_h[:, n % 2, :], sbuf_s[:, n % 2, :], sbuf_s[:, n % 2, :], ALU.mult).then_inc(f8["h"], 1)
            for t in range(NT):
                v.wait_ge(f8["down"], FF[8] - 1 + t // 4)
                residual(7, t, f8["resid"], ps[:, t // 2, (t % 2) * D:(t % 2 + 1) * D], gate(7))



def kernel(**inputs):
    import ml_dtypes
    import concourse.bacc as _bacc
    from concourse.bass_utils import run_bass_kernel_spmd as _run

    a = {k: np.asarray(v) for k, v in inputs.items()}
    f = np.float32

    def tiles(v):
        return v.reshape(NT, P, D).transpose(1, 0, 2)

    def wT(w):
        return w.T.reshape(-1, P, w.shape[0]).transpose(1, 0, 2).reshape(P, -1)

    def row(v):
        return v.reshape(1, -1)

    def even_odd(v, e):
        return np.moveaxis(v.reshape(*v.shape[:-1], D // 2 // e, 2, e), -2, -3).reshape(v.shape)

    first8 = np.arange(E0, 0, -1, dtype=f)
    lower4 = np.tril(np.ones((G3, G3), f), -1)
    rows_d = dict(bq0=a["L0_xattn_b_q"], bk0=a["L0_xattn_b_k_img"], bv0=even_odd(a["L0_xattn_b_v_img"], 16), bo0=a["L0_xattn_b_o"],
                  gq0=a["L0_xattn_g_q"], gk0=a["L0_xattn_g_k_img"], br0=a["L0_ffn_br"], bv2=even_odd(a["L2_xattn_bv"], 16),
                  bo2=a["L2_xattn_bo"], gamma2=a["L2_xattn_ln_gamma"], beta2=a["L2_xattn_ln_beta"],
                  bias3=a["L3_ffn_gate_bias"], rs2=a["L2_xattn_residual_scale"],
                  gates=np.concatenate([a["g_xattn"], a["g_ffn"]]), first8=first8, lower4=lower4)
    rows = np.concatenate([row(rows_d[n]) for n, _ in ROWS], 1)

    part = np.arange(P)
    pair = (part[:, None] // 16 % 2 == np.arange(2)).astype(f)
    quad = (part[:, None] // 8 % 4 == np.arange(4)).astype(f)
    early_d = dict(wk0=wT(a["L0_xattn_w_k_img"]), wq0=wT(a["L0_xattn_w_q"]), wv0=wT(even_odd(a["L0_xattn_w_v_img"].T, 16).T),
                   wo0=wT(a["L0_xattn_w_o"]), ident=np.eye(P, dtype=f), pair=pair, quad=quad)
    early = np.concatenate([early_d[n] for n, _ in EARLY], 1)

    had = np.ones((1, 1), f)
    while had.shape[0] < P:
        had = np.block([[had, had], [had, -had]])
    kv3 = np.concatenate([a["L3_xattn_Wk"], a["L3_xattn_Wv"]])
    col = lambda b: b.reshape(KC, P).T
    late_d = dict(
        A0=wT(a["L0_ffn_A"].reshape(E0 * R0, D)), B0=wT(a["L0_ffn_B"].transpose(1, 0, 2).reshape(D, E0 * R0)),
        wr0=wT(a["L0_ffn_Wr"]), gate1=wT(np.concatenate([a["L1_ffn_gate_w"], a["L1_ffn_shared_gate_vec"]])),
        wk2=wT(a["L2_xattn_Wk"]), wq2=wT(a["L2_xattn_Wq"]), wv2=wT(even_odd(a["L2_xattn_Wv"].T, 16).T), wo2=wT(a["L2_xattn_Wo"]),
        bqk2=np.concatenate([col(a["L2_xattn_bq"]), col(a["L2_xattn_bk"])], 1),
        had=had, w2f=wT(a["L2_ffn_W2"]), wk3=wT(kv3[0::2]), wq3=wT(a["L3_xattn_Wq"]), wv3=wT(even_odd(kv3[1::2].T, 8).T),
        gate3=wT(a["L3_ffn_gate_w"]), fc1=wT(a["L3_ffn_fc1_w"]), fc2=wT(a["L3_ffn_fc2_w"]),
        up3=a["L3_ffn_shared_up_w"].reshape(C3S, P, KC, P).transpose(3, 0, 2, 1).reshape(P, -1),
        down3=wT(a["L3_ffn_shared_down_w"]))
    late = np.concatenate([late_d[n] for n, _ in LATE], 1)

    gu = a["L1_ffn_expert_gate_up"]
    sgu = a["L1_ffn_shared_gate_up"]
    pad = np.zeros((C1 * P - E1 * I1 - SI1, D), f)
    g_rows = np.concatenate([gu[:, :I1].reshape(-1, D), sgu[:SI1], pad])
    u_rows = np.concatenate([gu[:, I1:].reshape(-1, D), sgu[SI1:], pad])
    d_rows = np.concatenate([a["L1_ffn_expert_down"].transpose(0, 2, 1).reshape(-1, D), a["L1_ffn_shared_down"].T, pad])

    def chunks_up(g, u, n):
        both = np.stack([g.reshape(n, P, KC, P), u.reshape(n, P, KC, P)])
        return both.transpose(1, 4, 3, 0, 2).reshape(n, P, KC * 2 * P)

    w1 = np.concatenate([chunks_up(g_rows, u_rows, C1), d_rows.reshape(C1, P, D)], 2)
    w2 = chunks_up(a["L2_ffn_W1"], a["L2_ffn_W3"], C2)
    w3 = np.concatenate([a["L3_ffn_w1"].transpose(0, 2, 1), a["L3_ffn_w2"].transpose(0, 2, 1)], 2)

    def selector(expert_of, e):
        one = (expert_of[None, :] == np.arange(e)[:, None])
        return np.concatenate([one] * 3).astype(ml_dtypes.bfloat16)

    h1 = np.arange(C1 * P)
    e1 = np.where(h1 < E1 * I1, h1 // I1, E1)
    mask1 = a["mask_BxS2_bk0"].reshape(NT, BT, 1, S).repeat(S, 2).reshape(NT, P, S).transpose(1, 0, 2)
    mask2 = np.tile(a["mask_BxS2_ik0"].T, (2, 1))
    arrays = dict(
        x_dram=tiles(a["x"]), ctx_dram=tiles(a["ctx_2048"]),
        ctxT_dram=a["ctx_2048"].reshape(TOK, KC, P).transpose(2, 1, 0), rows_dram=rows, early_dram=early,
        late_dram=late, w1_dram=w1, w2_dram=w2, w3_dram=w3, mask1_dram=mask1, mask2_dram=mask2,
        identb_dram=np.eye(P, dtype=ml_dtypes.bfloat16), sel0_dram=selector(np.arange(E0 * R0) // R0, E0),
        sel1_dram=selector(e1, EP1), sel3_dram=selector(np.arange(E3 * P) // P, E3))
    arrays = {k: np.ascontiguousarray(v) for k, v in arrays.items()}

    nc = _bacc.Bacc("TRN2", target_bir_lowering=False, num_devices=1)
    args = [nc.dram_tensor(k, v.shape, U8 if v.dtype == bool else mybir.dt.from_np(v.dtype), kind="ExternalInput").ap() for k, v in arrays.items()]
    args.append(nc.dram_tensor("out_dram", (P, NT, D), F32, kind="ExternalOutput").ap())
    flamingo_kernel(nc, *args)
    r = _run(nc, [arrays], core_ids=[0])
    return r.results[0]["out_dram"].transpose(1, 0, 2).reshape(B, S, D)
```

```python
from contextlib import ExitStack, contextmanager

import numpy as np

import concourse.bass as bass
from concourse import mybir

F32 = mybir.dt.float32
BF16 = mybir.dt.bfloat16
F16 = mybir.dt.float16
F32R = mybir.dt.float32r
I32 = mybir.dt.int32
U8 = mybir.dt.uint8
ALU = mybir.AluOpType
ACT = mybir.ActivationFunctionType
AX = mybir.AxisListType

P = 128
B, S, D = 16, 64, 256
TOK = B * S
NT = TOK // P
KC = D // P
BT = P // S
HALF = 512
NL = 8
BIG = 3.0e38
NEG = -1.0e30

E0, R0 = 8, 64
E1, I1, SI1 = 16, 176, 704
TOP1 = 4
EP1 = 24
C1 = -(-(E1 * I1 + SI1) // P)
H2 = 1024
C2 = H2 // P
E3, LAT3, SH3, G3 = 32, 128, 512, 4
TOP3, TOPG3, SCALE3 = 8, 2, 2.5
C3S = SH3 // P

ROWS = [("bq0", D), ("bk0", D), ("bv0", D), ("bo0", D), ("gq0", D), ("gk0", D), ("br0", E0),
        ("bv2", D), ("bo2", D), ("gamma2", D), ("beta2", D), ("bias3", E3), ("rs2", 1), ("gates", 8),
        ("first8", E0), ("lower4", G3 * G3)]
EARLY = [("wk0", KC * D), ("wq0", KC * D), ("wv0", KC * D), ("wo0", KC * D), ("ident", P), ("pair", 2), ("quad", 4)]
LATE = [("A0", KC * E0 * R0), ("B0", (E0 * R0 // P) * D), ("wr0", KC * E0), ("gate1", KC * (E1 + 1)),
        ("wk2", KC * D), ("wq2", KC * D), ("wv2", KC * D), ("wo2", KC * D), ("bqk2", 2 * KC),
        ("had", P), ("w2f", C2 * D),
        ("wk3", KC * D), ("wq3", KC * D), ("wv3", KC * D), ("gate3", KC * E3), ("fc1", KC * LAT3),
        ("fc2", D), ("up3", C3S * KC * P), ("down3", C3S * D)]


def columns(pack):
    at, out = 0, {}
    for name, n in pack:
        out[name] = (at, n)
        at += n
    return out, at


RCOL, RN = columns(ROWS)
ECOL, EN = columns(EARLY)
LCOL, LN_ = columns(LATE)
W1COLS = KC * 2 * P + D
W2COLS = KC * 2 * P
W3COLS = P + LAT3


class Chain:

    def __init__(self, eng, sem):
        self.eng, self.sem, self.n, self.i, self.per = eng, sem, 0, None, 0

    def value(self):
        return self.n if self.i is None else self.i * self.per + self.n

    def link(self, ins):
        ins.then_inc(self.sem, 1)
        self.n += 1
        self.eng.wait_ge(self.sem, self.value())

    @contextmanager
    def loop(self, start, end, per):
        base = self.n
        with self.eng.Fori(start, end) as i:
            self.i, self.per, self.n = i, per, base - start * per
            yield i
            assert self.n == base - start * per + per, (self.n, base, start, per)
        self.i, self.n = None, base + (end - start) * per


def flamingo_kernel(nc, x_in, ctx_in, ctxT_in, rows_in, early_in, late_in, w1_in, w2_in, w3_in,
                    mask1_in, mask2_in, identb_in, sel0_in, sel1_in, sel3_in, out):
    with ExitStack() as stack:
        def sb(name, shape, dt=F32):
            return stack.enter_context(nc.sbuf_tensor(name, shape, dt))

        def sem(name):
            return stack.enter_context(nc.semaphore(name))

        def sb_twice(name, shape):
            with nc.sbuf_tensor(name, shape, F32) as full:
                pass
            return full, sb(name + "_r", shape, F32R)

        x = sb("x", [P, NT, D])
        xn, xn_r = sb_twice("xn", [P, NT, D])
        xT = sb("xT", [P, KC, TOK])
        ctx = sb("ctx", [P, NT, D])
        ctxT = sb("ctxT", [P, KC, TOK])
        qT, qT_r = sb_twice("qT", [P, KC, TOK])
        k_tok = qT[:, :, :].rearrange("p c (t n) -> p (c t) n", n=D)
        q_tok = xn
        kpair, kpair_r = sb_twice("kpair", [P, KC * B * 4 * S])
        vpair = sb("vpair", [P, B * 288])
        probs, probs_r = sb_twice("probs", [P, 2, 2048])
        rows = sb("rows", [P, RN])
        early = sb("early", [P, EN])
        late = sb("late", [P, LN_])

        wring = sb("wring", [P, 2, W1COLS])
        sbuf_s = sb("act_s", [P, 2, HALF])
        sbuf_t = sb("mid_t", [P, 2, HALF])
        junk, oN = sbuf_t[:, 0, :].rearrange("p (a n) -> p a n", a=2), sbuf_t[:, 1, :].rearrange("p (a n) -> p a n", a=2)
        sbuf_h, hid_r = sb_twice("hid_h", [P, 2, HALF])
        oT = sbuf_h[:, 1, :].rearrange("p (a n) -> p a n", a=2)
        gT = sb("gT", [3 * E3, TOK], BF16)
        identb = sb("identb", [P, P], BF16)
        sel0 = sb("sel0", [3 * E0, E0 * R0], BF16)
        sel1 = sb("sel1", [3 * EP1, C1 * P], BF16)
        sel3 = ctx[:, :, :].rearrange("p t n -> p (t n)").bitcast(BF16)[0:3 * E3, :]
        m8 = sb("m8", [P, NT, S], U8)
        m32 = kpair[:, 16 * NT * E3:18 * NT * E3].bitcast(I32).rearrange("p (t s) -> p t s", t=NT)
        mraw = sb("mraw", [P, B], I32)
        hi2 = sb("hi2", [P, B])
        st = sb("st", [P, NT, 6])
        mv = sb("mv", [P, NT, 2])
        mhalf = sb("mhalf", [P, 32])
        rstd = sb("rstd", [P, NT])
        ve = sb("ve", [P, NT])
        cr = sb("cr", [P, HALF])
        ss, ssv = (cr[:, n * NT * 32:(n + 1) * NT * 32].rearrange("p (t n) -> p t n", t=NT) for n in range(2))
        ssr = sb("ssr", [P, NT, 32])
        mx = sb("mx", [P, 2, 16])
        rden = sb("rden", [P, 2, 32])
        den2 = sb("den2", [P, 2, 32])
        tg = sb("tg", [P, 8])
        rs = sb("rs", [P, 1])
        SCR = 18 * NT * E3
        lg, la, lb, lc, ld, top8 = (kpair[:, SCR + n * NT * E3:SCR + (n + 1) * NT * E3] for n in range(6))
        gsc = sb("gsc", [P, NT * G3])
        gsd = sb("gsd", [P, NT * G3])
        rk, rk2 = (kpair[:, at:at + NT * G3 * G3] for at in (SCR + 6 * NT * E3, SCR + 6 * NT * E3 + NT * G3 * G3))
        red = sb("red", [P, NT])
        red2 = sb("red2", [P, NT])
        vm = sb("vm", [P, NT])
        g3 = kpair[:, SCR + 7 * NT * E3:SCR + 9 * NT * E3].bitcast(BF16)[:, 0:NT * 3 * E3]
        cm = sbuf_h[:, 0, :].bitcast(I32)
        ps = stack.enter_context(nc.psum_tensor("ps", [P, 8, 512], F32))

        def E(name):
            a, n = ECOL[name]
            return early[:, a:a + n]

        def L(name):
            a, n = LCOL[name]
            return late[:, a:a + n]

        def R(name):
            a, n = RCOL[name]
            return rows[:, a:a + n]

        def kc(ap):
            return ap.rearrange("p (k n) -> p k n", k=KC)

        ident = E("ident")
        w2h = kpair[:, 0:C2 * D]
        s3 = probs_r[:, :, :].rearrange("p a n -> p (a n)")
        s5 = kpair_r[:, 4096:8192]
        W_ = W1COLS
        WH, WL, HH = ({l: r[:, a:b].rearrange("p (c n) -> p c n", c=2) for l, r in ((3, s3), (5, s5))}
                      for a, b in ((0, 2 * W_), (2 * W_, 4 * W_), (4 * W_, 4 * W_ + 2 * HALF)))
        HL = hid_r
        XH = qT_r
        XL = {3: xn_r[:, :, :].rearrange("p t n -> p (t n)").rearrange("p (c n) -> p c n", c=KC),
              5: kpair_r[:, 0:KC * TOK].rearrange("p (c n) -> p c n", c=KC)}
        yT = qT
        Kp = kpair[:, 0:KC * B * 2 * S].rearrange("p (c b h s) -> p c b h s", c=KC, b=B, h=2)
        Kq = kpair[:, :].bitcast(F16).rearrange("p (i c b m s) -> p i c b m s", i=2, c=KC, b=B, m=4)
        k16 = probs[:, 1, :].bitcast(F16).rearrange("p (i c n) -> p i c n", i=2, c=KC)
        q16 = qT[:, :, :].rearrange("p c n -> p (c n)").bitcast(F16).rearrange("p (i c n) -> p i c n", i=2, c=KC)
        Vp = vpair[:, 0:B * 272].rearrange("p (b j h e) -> p b j h e", b=B, j=8, h=2)
        Vq = vpair[:, 0:B * 288].rearrange("p (b j h e) -> p b j h e", b=B, j=16, h=2)

        def tok(t):
            return slice(t * P, (t + 1) * P)

        s_x, s_ctxT, s_early, s_rows, s_late, s_misc, s_out = map(sem, (
            "x_landed", "ctxT_landed", "early_landed", "rows_landed", "late_landed", "misc_landed", "out_stored"))
        s_dve, s_pool = sem("dve_chain"), sem("pool_chain")
        s_cst = sem("consts_ready")
        s_tanh = sem("tanh_ready")
        ln_var, ln_rstd, ln_xn, ln_Tfull, ln_xT = map(sem, (
            "ln_variance", "ln_rstd", "ln_normed", "ln_transposed", "ln_xT"))
        w2_bf, w2_mm, w2_ev = sem("w2_butterfly"), sem("w2_hadamard"), sem("w2_ready")
        class Named(dict):

            def __init__(self, prefix):
                super().__init__()
                self.prefix = prefix

            def __missing__(self, name):
                self[name] = sem(self.prefix + name)
                return self[name]

        A = {l: Named(f"attention{l}_") for l in (0, 4, 6)}
        a2 = Named("attention2_")
        Fs = {l: Named(f"ffn{l}_") for l in (1, 3, 5, 7, 8)}
        s_lat, s_latE, s_yl = sem("lat_full"), sem("lat_ready"), sem("y_ready")
        s_vq = sem("vq_cleared")
        s_sel3 = sem("sel3_landed")

        block = stack.enter_context(nc.Block())
        FF = {1: 8, 3: 2 * C1, 5: 2 * C2, 7: 2 * E3, 8: 2 * C3S}

        def down_weights(l, i, c):
            if l == 3:
                return wring[:, c, W2COLS:W1COLS]
            return L("w2f")[:, (slice(c * D, (c + 1) * D) if isinstance(i, int) else bass.ds(i * (2 * D) + c * D, D))]

        @block.sync
        def _(sp):
            sp.dma_start(early[:, :], early_in).then_inc(s_early, 16)
            sp.dma_start(ctxT[:, :, :], ctxT_in).then_inc(s_ctxT, 16)
            sp.dma_start(rows[:, :], rows_in.partition_broadcast(P)).then_inc(s_rows, 16)
            sp.dma_start(late[:, :], late_in).then_inc(s_late, 16)
            for dst, src in ((identb[:, :], identb_in), (sel0[:, :], sel0_in), (sel1[:, :], sel1_in),
                             (m8[:, :, :], mask1_in), (mraw[:, :], mask2_in),
                             (ctx[:, :, :], ctx_in)):
                sp.dma_start(dst, src).then_inc(s_misc, 16)
            for l, w, cols, chunks in ((3, w1_in, W1COLS, C1), (5, w2_in, W2COLS, C2), (7, w3_in, W3COLS, E3)):
                f = Fs[l]
                if l > 3:
                    before = Fs[l - 2]
                    sp.wait_ge(before["up_lo"], C1 if l == 5 else C2)
                    if l == 5:
                        sp.wait_ge(before["down_lo"], C1)
                        sp.dma_start(sel3, sel3_in).then_inc(s_sel3, 16)
                for c in range(2):
                    sp.dma_start(wring[:, c, 0:cols], w[c]).then_inc(f[f"land{c}"], 16)
                with sp.Fori(1, chunks // 2) as i:
                    for c in range(2):
                        if l == 7:
                            sp.wait_ge(f["down"], i * 4 + (2 * c - 2))
                        else:
                            sp.wait_ge(f["up_lo"], i * 2 + (c - 1))
                        if l == 3:
                            sp.wait_ge(f["down_lo"], i * 2 + (c - 1))
                        sp.dma_start(wring[:, c, 0:cols], w[bass.ds(i * 2 + c, 1)].rearrange("o p n -> (o p) n")
                                     ).then_inc(f[f"land{c}"], 16)
            for t in range(NT):
                sp.wait_ge(Fs[8]["resid"], t + 1)
                sp.dma_start(out[:, t, :], x[:, t, :]).then_inc(s_out, 16)
            sp.wait_ge(s_out, 16 * NT)

        @block.gpsimd
        def _(pool):
            ch = Chain(pool, s_pool)
            pool.dma_start(x[:, :, :], x_in).then_inc(s_x, 16)
            pool.memset(mhalf[:, :], -0.5).then_inc(s_cst, 1)

            def block_diagonal(v, e, first):
                if first:
                    pool.memset(vpair[:, :], 0.0).then_inc(s_cst, 1)
                else:
                    ch.link(pool.memset(vpair[:, :], 0.0))
                if first:
                    pool.wait_ge(s_cst, 2)
                for h in range(2):
                    pool.memset(v[h * S:(h + 1) * S, :, :, h, e:e + 1].rearrange("p b j e -> p b (j e)"), 1.0).then_inc(
                        s_cst if first else s_vq, 1)
                    pool.wait_ge(*((s_cst, 3 + h) if first else (s_vq, 1 + h)))

            block_diagonal(Vp, 16, True)

            def rsqrt(out_ap, tmp, src, mul, eps, n, done):
                ch.link(pool.tensor_scalar(tmp, src, mul, eps, ALU.mult, ALU.add))
                pool.tensor_tensor(out_ap, tmp, mhalf[:, 0:n], ALU.pow).then_inc(done, 1)

            def ln(l):
                for t in range(NT):
                    pool.wait_ge(ln_var, NT * l + t + 1)
                    rsqrt(rstd[:, t:t + 1], ve[:, t:t + 1], mv[:, t, 1:2], 1.0, 1e-5, 1, ln_rstd)

            def rms_0(first):
                for q in range(2):
                    pool.wait_ge(A[0]["ss"], first + 4 * q + 4)
                    r = slice(4 * q, 4 * q + 4)
                    rsqrt(ssr[:, first // NT, r], ssv[:, first // NT, r], ss[:, first // NT, r], 1.0 / D, 1e-6, 4,
                          A[0]["rms"])

            def split_weights(l, chunks, first=True, others=True):
                f = Fs[l]

                def one(c, at, down):
                    pool.wait_ge(f["up_hi"], at + 1)
                    pool.tensor_tensor(WL[l][:, c, 0:W2COLS], wring[:, c, 0:W2COLS], WH[l][:, c, 0:W2COLS],
                                       ALU.subtract).then_inc(f["up_lo"], 1)
                    pool.wait_ge(f["up_lo"], at + 1)
                    pool.wait_ge(f["down_hi"], at + 1)
                    pool.tensor_tensor(WL[l][:, c, W2COLS:W1COLS], down, WH[l][:, c, W2COLS:W1COLS],
                                       ALU.subtract).then_inc(f["down_lo"], 1)
                    pool.wait_ge(f["down_lo"], at + 1)

                if first:
                    for c in range(2):
                        one(c, c, down_weights(l, 0, c))
                if others:
                    with pool.Fori(1, chunks // 2) as i:
                        for c in range(2):
                            one(c, i * 2 + c, down_weights(l, i, c))

            def squares_6(buf, first):
                for t in range(NT):
                    pool.wait_ge(A[6]["raw"], first + t + 1)
                    if first + t >= 2:
                        pool.wait_ge(A[6]["sum"], first + t - 1)
                    pool.tensor_tensor(junk[:, t % 2, :], buf[:, t, :], buf[:, t, :], ALU.mult).then_inc(A[6]["sq"], 1)

            ln(0)
            rms_0(0)
            rms_0(NT)
            for l in range(1, NL):
                if l == 5:
                    for t in range(NT):
                        pool.wait_ge(A[4]["dvar"], t + 1)
                        rsqrt(rstd[:, t:t + 1], ve[:, t:t + 1], mv[:, t, 1:2], 1.0, 1e-5, 1, A[4]["drstd"])
                        if t >= 1:
                            pool.wait_ge(ln_var, NT * l + t)
                            rsqrt(rstd[:, t - 1:t], ve[:, t - 1:t], mv[:, t - 1, 1:2], 1.0, 1e-5, 1, ln_rstd)
                    pool.wait_ge(ln_var, NT * l + NT)
                    rsqrt(rstd[:, NT - 1:NT], ve[:, NT - 1:NT], mv[:, NT - 1, 1:2], 1.0, 1e-5, 1, ln_rstd)
                    block_diagonal(Vq, 8, False)
                    split_weights(5, C2, first=False)
                else:
                    ln(l)
                if l == 4:
                    split_weights(5, C2, others=False)
                if l == 1:
                    pool.wait_ge(s_late, 16)
                    pool.wait_ge(A[0]["sc_full"], 4 * NT)
                    src, dst = L("w2f"), w2h
                    for stage in range(3):
                        n = (1 << stage) * D
                        u = src.rearrange("p (a two n) -> p a two n", two=2, n=n)
                        v = dst.rearrange("p (a two n) -> p a two n", two=2, n=n)
                        for k, op in enumerate((ALU.add, ALU.subtract)):
                            pool.tensor_tensor(v[:, :, k, :], u[:, :, 0, :], u[:, :, 1, :], op).then_inc(w2_bf, 1)
                        pool.wait_ge(w2_bf, 2 * stage + 2)
                        src, dst = dst, src
                if l == 3:
                    for k in range(4):
                        pool.wait_ge(Fs[3]["x_hi"], k + 1)
                        q = slice(k * D, (k + 1) * D)
                        pool.tensor_tensor(XL[3][:, :, q], xT[:, :, q], XH[:, :, q], ALU.subtract).then_inc(
                            Fs[3]["x_lo"], 1)
                        pool.wait_ge(Fs[3]["x_lo"], k + 1)
                    split_weights(3, C1)
                if l == 6:
                    squares_6(k_tok, 0)
                    squares_6(q_tok, NT)

        @block.tensor
        def _(pe):
            def mm(o, lhsT, rhs, start=True, stop=True):
                return pe.matmul(o, lhsT, rhs, start=start, stop=stop, skip_group_check=True)

            def rows_by_width(bank, actT, t, w):
                for k in range(KC):
                    ins = mm(ps[:, bank, 0:D], actT[:, k, tok(t)], w[:, k, :], k == 0, k == KC - 1)
                return ins

            def layernorm_T(l):
                for k in range(NT // 2):
                    pe.wait_ge(ln_xn, NT * l + 2 * k + 2)
                    for j in range(2):
                        for c in range(KC):
                            ins = pe.transpose(ps[:, k, j * D + c * P:j * D + (c + 1) * P],
                                               xn[:, 2 * k + j, c * P:(c + 1) * P], ident)
                    ins.then_inc(ln_Tfull, 1)

            def xT_ready(l, tiles):
                pe.wait_ge(ln_xT, (NT // 2) * l + (tiles + 1) // 2)

            def project(a, actT, w, first, l):
                for t in range(NT):
                    if first:
                        xT_ready(l, t + 1)
                    if t >= 4:
                        pe.wait_ge(a["raw"], first + t - 3)
                    elif first:
                        pe.wait_ge(a["v_done"], B - 3 + t)
                    rows_by_width(4 + t % 4, actT, t, kc(w)).then_inc(a["pr_full"], 1)

            def transpose_normed(a, buf, first):
                for t in range(NT):
                    pe.wait_ge(a["normed"], first + t + 1)
                    if first or t >= 4:
                        pe.wait_ge(a["T_done"], first + t - 3)
                    else:
                        pe.wait_ge(a["raw"], 2 * NT - 3 + t)
                    for c in range(KC):
                        ins = pe.transpose(ps[:, 4 + t % 4, c * P:(c + 1) * P], buf[:, t, c * P:(c + 1) * P], ident)
                    ins.then_inc(a["T_full"], 1)

            def values(a, w):
                for b in range(B):
                    if b >= 4:
                        pe.wait_ge(a["v_done"], b - 3)
                    elif a is not A[4]:
                        pe.wait_ge(a["raw"], NT - 3 + b)
                    for h in range(2):
                        for k in range(KC):
                            ins = mm(ps[h * S:(h + 1) * S, 4 + b % 4, 0:D // 2], ctxT[:, k, b * S:(b + 1) * S],
                                     kc(w)[:, k, h * (D // 2):(h + 1) * (D // 2)], k == 0, k == KC - 1)
                    ins.then_inc(a["v_full"], 1)

            def pv(a, t, bank, lhs, V, n, width):
                for j in range(n):
                    for b in range(BT):
                        ins = mm(ps[b * S:(b + 1) * S, bank, j * width:(j + 1) * width], lhs(j, b),
                                 V[:, BT * t + b, j, :, :].rearrange("p h e -> p (h e)"))
                ins.then_inc(a["pv_full"], 1)

            def out_T(a, t, bank):
                pe.wait_ge(a["o_norm"], t + 1)
                for c in range(KC):
                    ins = pe.transpose(ps[:, bank, c * P:(c + 1) * P], oN[:, t % 2, c * P:(c + 1) * P], ident)
                ins.then_inc(a["oT_full"], 1)

            def out_projection(a, t, bank, w):
                pe.wait_ge(a["oT_ready"], t + 1)
                for k in range(KC):
                    ins = mm(ps[:, bank, D:2 * D], oT[:, t % 2, k * P:(k + 1) * P], kc(w)[:, k, :], k == 0, k == KC - 1)
                ins.then_inc(a["o_proj"], 1)

            a = A[0]
            pe.wait_ge(s_early, 16)
            pe.wait_ge(s_ctxT, 16)
            project(a, ctxT, E("wk0"), 0, 0)
            values(a, E("wv0"))
            layernorm_T(0)
            project(a, xT, E("wq0"), NT, 0)
            transpose_normed(a, k_tok, 0)
            transpose_normed(a, q_tok, NT)
            pe.wait_ge(a["T_done"], 2 * NT)
            for s in range(NT + 3):
                t = s
                if t < NT:
                    for j in range(4):
                        if t >= 1:
                            pe.wait_ge(a["sc_free"], 4 * (t - 1) + j + 1)
                        g = slice(32 * j, 32 * j + 32)
                        for c in range(KC):
                            for b in range(BT):
                                ins = mm(ps[b * S:(b + 1) * S, j, c * P:(c + 1) * P],
                                         qT[g, c, t * P + b * S:t * P + (b + 1) * S],
                                         Kp[g, c, BT * t + b, :, :].rearrange("p h s -> p (h s)"))
                        ins.then_inc(a["sc_full"], 1)
                t = s - 3
                if 0 <= t:
                    if t >= 1:
                        pe.wait_ge(a["resid"], t)
                    out_T(a, t, 7)
                t = s - 1
                if 0 <= t < NT:
                    pe.wait_ge(a["p_ready"], 4 * t + 4)
                    Pt = probs[:, t % 2, 0:1024].rearrange("p (j n) -> p j n", j=8)
                    if t >= 1:
                        pe.wait_ge(a["pT_act"], t)
                    for n in range(8):
                        if n == 4 and t >= 1:
                            pe.wait_ge(a["pT_dve"], t)
                        ins = pe.transpose(ps[:, 4 + n // 4, (n % 4) * P:(n % 4 + 1) * P], Pt[:, n, :], ident)
                        if n % 4 == 3:
                            ins.then_inc(a["pT_full"], 1)
                t = s - 3
                if 0 <= t:
                    out_projection(a, t, 7, E("wo0"))
                t = s - 2
                if 0 <= t < NT:
                    pe.wait_ge(a["pT_act"], t + 1)
                    pe.wait_ge(a["pT_dve"], t + 1)
                    if t >= 1:
                        pe.wait_ge(a["o_norm"], t)
                    PT = probs[:, t % 2, 1024:2048].rearrange("p (j c n) -> p j c n", j=4, c=KC)
                    pv(a, t, 6, lambda n, b: PT[:, n % 4, n // 4, b * S:(b + 1) * S], Vp, 8, 34)
            def gates_T(l, e):
                f = Fs[l]
                pe.wait_ge(f["gates"], 1)
                gv = g3[:, 0:NT * 3 * e].rearrange("p (t n) -> p t n", t=NT)
                for t in range(NT):
                    ins = pe.transpose(ps[:, 1, :].bitcast(BF16)[0:3 * e, tok(t)], gv[:, t, :], identb[:, :])
                ins.then_inc(f["gT_full"], 1)
                pe.wait_ge(f["gT_ready"], 1)

            def logits(l, w, e):
                for t in range(NT):
                    xT_ready(l, t + 1)
                    for k in range(KC):
                        ins = mm(ps[:, 0, t * e:(t + 1) * e], xT[:, k, tok(t)], w[:, k, :], k == 0, k == KC - 1)
                ins.then_inc(Fs[l]["logits"], 1)

            def up2(o, w, half):
                for k in range(KC):
                    ins = mm(o, w[:, k, :], xT[:, k, half * HALF:(half + 1) * HALF], k == 0, k == KC - 1)
                return ins

            def down_tokens(hid, half, w, first):
                for q in range(4):
                    t = 4 * half + q
                    ins = mm(ps[:, t // 2, (t % 2) * D:(t % 2 + 1) * D], hid[:, q * P:(q + 1) * P], w,
                             first and t % 2 == 0, True)
                return ins

            def at_least(sm, n, low):
                if low >= 1:
                    pe.wait_ge(sm, n)

            def run_units(units, up, down):
                groups = units // 4

                def group(base, low, last, first):
                    for k in range(4):
                        if not (last and k == 3):
                            up(base + (k + 1), low + k + 1, (k + 1) % 4)
                        down(base + k, low + k, k, first and k < 2)
                up(0, 0, 0)
                group(0, 0, groups == 1, True)
                if groups > 2:
                    with pe.Fori(1, groups - 1) as i:
                        group(i * 4, 4, False, False)
                if groups > 1:
                    group(4 * (groups - 1), 4 * (groups - 1), True, False)

            f = Fs[1]
            pe.wait_ge(s_late, 16)
            pe.wait_ge(s_misc, 16 * 6)
            layernorm_T(1)
            logits(1, kc(L("wr0")), E0)
            gates_T(1, E0)
            a0 = L("A0").rearrange("p (k n) -> p k n", k=KC)
            b0 = L("B0").rearrange("p (k n) -> p k n", n=D)

            def up_1(n, low, k):
                c, half = n // 2, n % 2
                at_least(f["act"], n - 1, low - 1)
                up2(ps[:, 4 + 2 * (n % 2), :], a0[:, :, c * P:(c + 1) * P], half).then_inc(f["up"], 1)
                at_least(f["h"], n - 1, low - 1)
                mm(ps[:, 5 + 2 * (n % 2), :], sel0[:, c * P:(c + 1) * P], gT[0:3 * E0, half * HALF:(half + 1) * HALF]
                   ).then_inc(f["cw"], 1)

            def down_1(n, low, k, first):
                pe.wait_ge(f["h"], n + 1)
                down_tokens(sbuf_h[:, n % 2, :], n % 2, b0[:, n // 2, :], first).then_inc(f["down"], 1)

            up_1(0, 0, 0)
            for n in range(FF[1]):
                if n + 1 < FF[1]:
                    up_1(n + 1, n + 1, 0)
                down_1(n, n, 0, n < 2)
            layernorm_T(2)
            for t in range(NT):
                xT_ready(2, t + 1)
                for b in range(BT):
                    for k in range(KC):
                        q = slice(t * P + b * S, t * P + (b + 1) * S)
                        ins = mm(ps[b * S:(b + 1) * S, 4 + t // 4, (t % 4) * S:(t % 4 + 1) * S], xT[:, k, q],
                                 ctxT[:, k, q], k == 0, k == KC - 1)
                if t % 4 == 3:
                    ins.then_inc(a2["sc_full"], 1)
            pe.wait_ge(a2["shift"], 2)
            for s in range(NT + 1):
                if s < NT:
                    pe.wait_ge(a2["p_ready"], 2 * (s // 4) + 2)
                    if s >= 2:
                        pe.wait_ge(a2["pT_ready"], s - 1)
                    pe.transpose(ps[:, 6 + s % 2, 0:P], probs[:, 0, tok(s)], ident).then_inc(a2["pT_full"], 1)
                t = s - 1
                if t >= 0:
                    pe.wait_ge(a2["pT_ready"], t + 1)
                    if t >= 2:
                        pe.wait_ge(a2["resid"], t - 1)
                    mm(ps[:, 4 + t % 2, 0:D], probs[:, 1, (t % 2) * P:(t % 2 + 1) * P], ctx[:, t, :]
                       ).then_inc(a2["pv_full"], 1)
            f3 = Fs[3]
            layernorm_T(3)
            logits(3, kc(L("gate1")), E1 + 1)
            pe.wait_ge(w2_bf, 6)
            for n in range(4):
                mm(ps[:, 4 + n, :], L("had"), w2h[:, n * 512:(n + 1) * 512]).then_inc(w2_mm, 1)
            gates_T(3, EP1)

            def chunk_of(n, k):
                return n // 2 if isinstance(n, int) else n // 2

            def gate_up(l, o, c, g, half):
                w = [W[l][:, c, 0:W2COLS].rearrange("p (k g n) -> p k g n", k=KC, g=2)[:, :, g, :] for W in (WH, WL)]
                for n, (wi, xs) in enumerate(((w[1], XH), (w[0], XL[l]), (w[0], XH))):
                    for k in range(KC):
                        ins = mm(o, wi[:, k, :], xs[:, k, half * HALF:(half + 1) * HALF], n == 0 and k == 0,
                                 n == 2 and k == KC - 1)
                return ins

            def down_T(l, n, k, first):
                f, c, half = Fs[l], k // 2, k % 2
                pe.wait_ge(f["h_lo"], n + 1)
                if half == 0:
                    pe.wait_ge(f["down_lo"], chunk_of(n, k) + 1)
                for d in range(KC):
                    w = [W[l][:, c, W2COLS + d * P:W2COLS + (d + 1) * P] for W in (WH, WL)]
                    for m, (wi, hs) in enumerate(((w[1], HH[l]), (w[0], HL), (w[0], HH[l]))):
                        ins = mm(ps[:, 2 * half + d, :], wi, hs[:, half, :], first and m == 0, m == 2)
                ins.then_inc(f["down"], 1)

            def back_to_tokens(l):
                for t in range(NT):
                    if t % 4 == 0:
                        pe.wait_ge(Fs[l]["yT"], 2 * (t // 4) + 2)
                    for d in range(KC):
                        ins = pe.transpose(ps[:, t // 2, (t % 2) * D + d * P:(t % 2) * D + (d + 1) * P],
                                           yT[:, d, tok(t)], ident)
                    if t % 2:
                        ins.then_inc(Fs[l]["y"], 1)

            def up_3(n, low, k):
                c, half = k // 2, k % 2
                if half == 0:
                    pe.wait_ge(f3["up_lo"], chunk_of(n, k) + 1)
                at_least(f3["h"], n - 1, low - 1)
                gate_up(3, ps[:, 4 + (3 * k) % 4, :], c, 0, half)
                at_least(f3["act"], n, low)
                gate_up(3, ps[:, 4 + (3 * k + 1) % 4, :], c, 1, half).then_inc(f3["up"], 1)
                at_least(f3["mid"], n, low)
                if isinstance(n, int):
                    chunk = sel1[:, (n // 2) * P:(n // 2 + 1) * P]
                else:
                    chunk = sel1[:, bass.ds((n - k) * (P // 2) + c * P, P)]
                mm(ps[:, 4 + (3 * k + 2) % 4, :], chunk, gT[0:3 * EP1, half * HALF:(half + 1) * HALF]
                   ).then_inc(f3["cw"], 1)

            def down_3(n, low, k, first):
                down_T(3, n, k, first)

            pe.wait_ge(f3["x_lo"], 4)
            pe.wait_ge(w2_ev, 4)
            run_units(FF[3], up_3, down_3)
            back_to_tokens(3)
            a = A[4]

            def projection_T(w, actT, n0):
                for c in range(KC):
                    for half in range(2):
                        for k in range(KC):
                            ins = mm(ps[:, 4 + 2 * c + half, :], w[:, k, c * P:(c + 1) * P],
                                     actT[:, k, half * HALF:(half + 1) * HALF], k == 0, k == KC - 1)
                        ins.then_inc(a["kq_full"], 1)

            projection_T(kc(L("wk2")), ctxT, 0)
            pe.wait_ge(a["kq_done"], 4)
            values(a, L("wv2"))
            layernorm_T(4)
            xT_ready(4, NT)
            pe.wait_ge(a["v_done"], B)
            projection_T(kc(L("wq2")), xT, 4)
            pe.wait_ge(a["q_ready"], 4)
            for s in range(NT + 2):
                t = s
                if t < NT:
                    pe.wait_ge(a["k_ready"], 8)
                    if t >= 1:
                        pe.wait_ge(a["sc_free"], t)
                    for c in range(KC):
                        for b in range(BT):
                            for j in range(4):
                                g = slice(32 * j, 32 * j + 32)
                                ins = mm(ps[:, j, c * P + b * S:c * P + (b + 1) * S],
                                         Kp[g, c, BT * t + b, :, :].rearrange("p h s -> p (h s)"),
                                         qT[g, c, t * P + b * S:t * P + (b + 1) * S])
                    ins.then_inc(a["sc_full"], 1)
                t = s - 2
                if t >= 0:
                    if t >= 2:
                        pe.wait_ge(a["resid"], t - 1)
                    out_T(a, t, 6 + t % 2)
                t = s - 1
                if 0 <= t < NT:
                    pe.wait_ge(a["p_ready"], t + 1)
                    if t >= 2:
                        pe.wait_ge(a["o_norm"], t - 1)
                    PT = probs[:, t % 2, 0:1024].rearrange("p (j c n) -> p j c n", j=4, c=KC)
                    pv(a, t, 4 + t % 2, lambda n, b: PT[:, n % 4, n // 4, b * S:(b + 1) * S], Vp, 8, 34)
                t = s - 2
                if t >= 0:
                    out_projection(a, t, 6 + t % 2, L("wo2"))
            f5 = Fs[5]
            layernorm_T(5)
            pe.wait_ge(f5["x_lo"], 4)

            def up_5(n, low, k):
                c, half = k // 2, k % 2
                if half == 0:
                    pe.wait_ge(f5["up_lo"], chunk_of(n, k) + 1)
                at_least(f5["act"], n - 1, low - 1)
                gate_up(5, ps[:, 4 + 2 * (k % 2), :], c, 0, half)
                at_least(f5["h"], n - 1, low - 1)
                gate_up(5, ps[:, 5 + 2 * (k % 2), :], c, 1, half).then_inc(f5["up"], 1)

            def down_5(n, low, k, first):
                down_T(5, n, k, first)

            run_units(FF[5], up_5, down_5)
            back_to_tokens(5)
            a = A[6]
            project(a, ctxT, L("wk3"), 0, 6)
            values(a, L("wv3"))
            layernorm_T(6)
            project(a, xT, L("wq3"), NT, 6)
            transpose_normed(a, k_tok, 0)
            transpose_normed(a, q_tok, NT)
            pe.wait_ge(a["masked"], 2)
            pe.wait_ge(a["T_done"], 2 * NT)
            for s in range(NT + 1):
                t = s
                if t < NT:
                    for j in range(4):
                        if t >= 1:
                            pe.wait_ge(a["p_ready"], 4 * (t - 1) + j + 1)
                        g = slice(32 * j, 32 * j + 32)
                        for c in range(KC):
                            for u in range(2):
                                for b in range(BT):
                                    at = (2 * c + u) * P + b * S
                                    for n, (ki, qi) in enumerate(((0, 1), (1, 0), (0, 0))):
                                        ins = mm(ps[:, j, at:at + S],
                                                 Kq[g, ki, c, BT * t + b, 2 * u:2 * u + 2, :].rearrange("p m s -> p (m s)"),
                                                 q16[g, qi, c, t * P + b * S:t * P + (b + 1) * S], n == 0, n == 2)
                        ins.then_inc(a["sc_full"], 1)
                t = s - 1
                if t >= 0:
                    pe.wait_ge(a["p_ready"], 4 * t + 4)
                    if t >= 2:
                        pe.wait_ge(a["o_norm"], t - 1)
                    PT = probs[:, t % 2, :].rearrange("p (j c u n) -> p j c u n", j=4, c=KC, u=2)
                    pv(a, t, 4 + t % 2,
                       lambda n, b: PT[:, (n % 8) // 2, n // 8, n % 2, b * S:(b + 1) * S], Vq, 16, 18)
            f7, f8 = Fs[7], Fs[8]
            layernorm_T(7)
            logits(7, kc(L("gate3")), E3)
            fc1 = kc(L("fc1"))
            for half in range(2):
                for k in range(KC):
                    ins = mm(ps[:, 2 + half, :], fc1[:, k, :], xT[:, k, half * HALF:(half + 1) * HALF],
                             k == 0, k == KC - 1)
                ins.then_inc(s_lat, 1)
            gates_T(7, E3)
            pe.wait_ge(s_sel3, 16)
            pe.wait_ge(s_latE, 2)

            def up_7(n, low, k):
                c, half = k // 2, k % 2
                if half == 0:
                    pe.wait_ge(f7[f"land{c}"], (n - k) * 4 + 16)
                at_least(f7["act"], n - 1, low - 1)
                mm(ps[:, 4 + 2 * (k % 2), :], wring[:, c, 0:P], qT[:, 0, half * HALF:(half + 1) * HALF]
                   ).then_inc(f7["up"], 1)
                at_least(f7["mid"], n - 1, low - 1)
                if isinstance(n, int):
                    chunk = sel3[:, (n // 2) * P:(n // 2 + 1) * P]
                else:
                    chunk = sel3[:, bass.ds((n - k) * (P // 2) + c * P, P)]
                mm(ps[:, 5 + 2 * (k % 2), :], chunk, gT[0:3 * E3, half * HALF:(half + 1) * HALF]).then_inc(f7["cw"], 1)

            def down_7(n, low, k, first):
                pe.wait_ge(f7["h"], n + 1)
                mm(ps[:, k % 2, :], wring[:, k // 2, P:P + LAT3], sbuf_h[:, k % 2, :], first, True).then_inc(f7["down"], 1)

            run_units(FF[7], up_7, down_7)
            u3 = L("up3").rearrange("p (c k n) -> p c k n", c=C3S, k=KC)
            d3 = L("down3").rearrange("p (c n) -> p c n", c=C3S)

            def up_8(n):
                if n >= 4:
                    pe.wait_ge(f8["act"], n - 3)
                up2(ps[:, 4 + n % 4, :], u3[:, n // 2, :, :], n % 2).then_inc(f8["up"], 1)

            up_8(0)
            up_8(1)
            pe.wait_ge(s_yl, 2)
            for t in range(NT):
                mm(ps[:, t // 2, (t % 2) * D:(t % 2 + 1) * D], qT[:, 1, tok(t)], L("fc2"), t % 2 == 0, True)
            for n in range(FF[8]):
                if n + 2 < FF[8]:
                    up_8(n + 2)
                pe.wait_ge(f8["h"], n + 1)
                down_tokens(sbuf_h[:, n % 2, :], n % 2, d3[:, n // 2, :], False).then_inc(f8["down"], 1)

        @block.scalar
        def _(act):
            def copy(o, i):
                return nc.scalar.activation(o, i, ACT.Copy)

            def layernorm_evac(l):
                for k in range(NT // 2):
                    act.wait_ge(ln_Tfull, (NT // 2) * l + k + 1)
                    copy(xT[:, :, 2 * k * P:2 * (k + 1) * P].rearrange("p c (t n) -> p t c n", t=2),
                         ps[:, k, :].rearrange("p (t c n) -> p t c n", t=2, c=KC)).then_inc(ln_xT, 1)

            def keys_masked(K, t, heads, mask, src):
                for h in range(heads):
                    ins = nc.scalar.activation(K[:, :, BT * t:BT * t + BT, h, :], src, ACT.Copy,
                                               scale=mask[:, h:h + 1])
                return ins

            def squares(a, buf, first):
                for t in range(NT):
                    act.wait_ge(a["raw"], first + t + 1)
                    if first + t >= 2:
                        act.wait_ge(a["ss"], first + t - 1)
                    nc.scalar.activation(junk[:, t % 2, :], buf[:, t, :], ACT.Square,
                                         accum_out=ss[:, first // NT, t:t + 1]).then_inc(a["ss"], 1)

            def by_tokens(a, buf, first):
                for t in range(NT):
                    act.wait_ge(a["pr_full"], first + t + 1)
                    copy(buf[:, t, :], ps[:, 4 + t % 4, 0:D]).then_inc(a["raw"], 1)
                for q in range(2):
                    act.wait_ge(a["ss"], first // 4 + q + 1)
                    nc.scalar.activation(ssr[:, 4 * q:4 * q + 4, :], ssv[:, 4 * q:4 * q + 4, :], ACT.Sqrt
                                         ).then_inc(a["rms"], 1)

            def keys_out(a):
                for t in range(NT):
                    act.wait_ge(a["T_full"], t + 1)
                    keys_masked(Kp, t, 2, E("pair"), ps[:, 4 + t % 4, 0:D].rearrange("p (c b s) -> p c b s", c=KC, b=BT)
                                ).then_inc(a["T_done"], 1)

            def queries_out(a):
                for t in range(NT):
                    act.wait_ge(a["T_full"], NT + t + 1)
                    copy(qT[:, :, tok(t)], ps[:, 4 + t % 4, 0:D].rearrange("p (c n) -> p c n", c=KC)
                         ).then_inc(a["T_done"], 1)

            def out_T_evac(a, t, bank):
                act.wait_ge(a["oT_full"], t + 1)
                copy(oT[:, t % 2, :], ps[:, bank, 0:D]).then_inc(a["oT_ready"], 1)

            a = A[0]
            act.wait_ge(s_rows, 16)
            nc.scalar.activation(tg[:, :], R("gates"), ACT.Tanh).then_inc(s_tanh, 1)
            act.wait_ge(s_early, 16)
            squares(a, k_tok, 0)
            layernorm_evac(0)
            squares(a, q_tok, NT)
            keys_out(a)
            queries_out(a)
            for s in range(NT + 3):
                t = s
                if t < NT:
                    for j in range(4):
                        act.wait_ge(a["sc_free"], 4 * t + j + 1)
                        v = probs[:, t % 2, j * D:(j + 1) * D]
                        nc.scalar.activation(v, v, ACT.Exp, scale=0.25).then_inc(a["p_ready"], 1)
                t = s - 1
                if 0 <= t < NT:
                    act.wait_ge(a["pT_full"], 2 * t + 1)
                    if t >= 2:
                        act.wait_ge(a["pv_full"], t - 1)
                    copy(probs[:, t % 2, 1024:1536], ps[:, 4, :]).then_inc(a["pT_act"], 1)
                t = s - 3
                if t >= 0:
                    out_T_evac(a, t, 7)
            def gates_evac(l, e):
                f = Fs[l]
                act.wait_ge(f["gT_full"], 1)
                copy(gT[0:3 * e, :], ps[:, 1, :].bitcast(BF16)[0:3 * e, :]).then_inc(f["gT_ready"], 1)

            def run_units(units, one):
                for k in range(4):
                    one(k, k, k)
                with act.Fori(1, units // 4) as i:
                    for k in range(4):
                        one(i * 4 + k, 4 + k, k)

            def unit(f, func, bank, o_free):
                def one(n, low, k):
                    act.wait_ge(f["up"], n + 1)
                    if low >= 2:
                        act.wait_ge(f[o_free], n - 1)
                    nc.scalar.activation(sbuf_s[:, k % 2, :], ps[:, bank(k), :], func).then_inc(f["act"], 1)
                return one

            def up_hi(l, c, slot):
                act.wait_ge(Fs[l][f"land{slot}"], (c - slot) * 8 + 16)
                copy(WH[l][:, slot, 0:W2COLS], wring[:, slot, 0:W2COLS]).then_inc(Fs[l]["up_hi"], 1)

            def down_hi(l, i, slot):
                copy(WH[l][:, slot, W2COLS:W1COLS], down_weights(l, i, slot)).then_inc(Fs[l]["down_hi"], 1)

            def run_split_units(l, units, bank):
                f = Fs[l]

                def group(i, first, last):
                    for k in range(4):
                        n = i * 4 + k
                        act.wait_ge(f["up"], n + 1)
                        if not (first and k < 2):
                            act.wait_ge(f["h"], n - 1)
                        nc.scalar.activation(sbuf_s[:, k % 2, :], ps[:, bank(k), :], ACT.Silu).then_inc(f["act"], 1)
                        if k == 0 and not first:
                            up_hi(l, i * 2 + 1, 1)
                        if k == 2 and not last:
                            up_hi(l, i * 2 + 2, 0)
                        if k == 1 and not first:
                            act.wait_ge(f["down"], n - 1)
                            down_hi(l, i, 1)
                        if k == 3 and not last:
                            act.wait_ge(f["down"], n - 1)
                            down_hi(l, i + 1, 0)
                        act.wait_ge(f["h"], n + 1)
                        copy(HH[l][:, k % 2, :], sbuf_h[:, k % 2, :]).then_inc(f["h_hi"], 1)

                group(0, True, False)
                with act.Fori(1, units // 4 - 1) as i:
                    group(i, False, False)
                group(units // 4 - 1, False, True)
                for half in range(2):
                    act.wait_ge(f["down"], units - 1 + half)
                    for d in range(KC):
                        copy(yT[:, d, half * HALF:(half + 1) * HALF], ps[:, 2 * half + d, :]).then_inc(f["yT"], 1)

            f = Fs[1]
            layernorm_evac(1)
            act.wait_ge(f["lread"], 1)
            nc.scalar.activation(lb[:, 0:NT * E0], la[:, 0:NT * E0], ACT.Exp).then_inc(f["e"], 1)
            gates_evac(1, E0)
            for n in range(FF[1]):
                unit(f, ACT.Copy, lambda k: 4 + 2 * (k % 2), "h")(n, n, n)
            layernorm_evac(2)
            pd = probs[:, 0, 0:NT * P].rearrange("p (t n) -> p t n", t=NT)
            sv = cr[:, :].rearrange("p (t n) -> p t n", t=NT)
            for half in range(2):
                act.wait_ge(a2["shift"], half + 1)
                for b in range(BT):
                    r, ts = slice(b * S, (b + 1) * S), slice(4 * half, 4 * half + 4)
                    nc.scalar.activation(pd[r, ts, b * S:(b + 1) * S], sv[r, ts, :], ACT.Exp,
                                         scale=D ** -0.5).then_inc(a2["p_ready"], 1)
            for t in range(NT):
                act.wait_ge(a2["pT_full"], t + 1)
                if t >= 2:
                    act.wait_ge(a2["pv_full"], t - 1)
                copy(probs[:, 1, (t % 2) * P:(t % 2 + 1) * P], ps[:, 6 + t % 2, 0:P]).then_inc(a2["pT_ready"], 1)
            f = Fs[3]
            layernorm_evac(3)
            lg17 = lg[:, 0:NT * (E1 + 1)].rearrange("p (t e) -> p t e", t=NT)
            act.wait_ge(f["lread"], 1)
            nc.scalar.activation(rk[:, 0:NT], lg17[:, :, E1], ACT.Exp, scale=-1.0).then_inc(f["e"], 1)
            act.wait_ge(f["lread"], 2)
            nc.scalar.activation(lb[:, 0:NT * E1], lb[:, 0:NT * E1], ACT.Exp).then_inc(f["e"], 1)
            for k in range(4):
                q = slice(k * D, (k + 1) * D)
                copy(XH[:, :, q], xT[:, :, q]).then_inc(f["x_hi"], 1)
            for c in range(2):
                up_hi(3, c, c)
                down_hi(3, 0, c)
            for n in range(4):
                act.wait_ge(w2_mm, n + 1)
                nc.scalar.activation(L("w2f")[:, n * 512:(n + 1) * 512], ps[:, 4 + n, :], ACT.Copy,
                                     scale=1.0 / 32).then_inc(w2_ev, 1)
            gates_evac(3, EP1)
            run_split_units(3, FF[3], lambda k: 4 + (3 * k) % 4)
            a = A[4]
            for g in range(4):
                c, half = g // 2, g % 2
                act.wait_ge(a["kq_done"], g + 1)
                src = sbuf_s[:, g % 2, :]
                for h in range(2):
                    nc.scalar.activation(Kp[:, c, half * 8:half * 8 + 8, h, :], src.rearrange("p (b s) -> p b s", s=S),
                                         ACT.Copy, scale=E("pair")[:, h:h + 1]).then_inc(a["k_ready"], 1)
            for c in range(2):
                up_hi(5, c, c)
                down_hi(5, 0, c)
            layernorm_evac(4)
            for s in range(NT + 2):
                t = s
                if t < NT:
                    act.wait_ge(a["sc_free"], t + 1)
                    v = probs[:, t % 2, 0:1024]
                    nc.scalar.activation(v, v, ACT.Exp, scale=0.25).then_inc(a["p_ready"], 1)
                t = s - 2
                if t >= 0:
                    out_T_evac(a, t, 6 + t % 2)
            for k in range(4):
                act.wait_ge(ln_Tfull, (NT // 2) * 5 + k + 1)
                copy(XH[:, :, 2 * k * P:2 * (k + 1) * P].rearrange("p c (t n) -> p t c n", t=2),
                     ps[:, k, :].rearrange("p (t c n) -> p t c n", t=2, c=KC)).then_inc(Fs[5]["x_hi"], 1)
                act.wait_ge(Fs[5]["x_hi"], k + 1)
                act.sem_inc(ln_xT, 1)
            run_split_units(5, FF[5], lambda k: 4 + 2 * (k % 2))
            a = A[6]
            by_tokens(a, k_tok, 0)
            layernorm_evac(6)
            by_tokens(a, q_tok, NT)
            for t in range(2 * NT):
                act.wait_ge(a["T_full"], t + 1)
                copy((k16 if t < NT else q16)[:, 0, :, tok(t % NT)],
                     ps[:, 4 + t % 4, 0:D].rearrange("p (c n) -> p c n", c=KC)).then_inc(a["hi"], 1)
            for t in range(NT):
                for j in range(4):
                    act.wait_ge(a["sc_full"], 4 * t + j + 1)
                    if t >= 2:
                        act.wait_ge(a["pv_full"], t - 1)
                    nc.scalar.activation(probs[:, t % 2, j * 512:(j + 1) * 512], ps[:, j, :], ACT.Exp,
                                         scale=8 ** -0.5).then_inc(a["p_ready"], 1)
            f = Fs[7]
            layernorm_evac(7)
            act.wait_ge(f["logits"], 1)
            nc.scalar.activation(lb[:, :], ps[:, 0, 0:NT * E3], ACT.Exp, scale=-1.0).then_inc(f["e"], 1)
            for half in range(2):
                act.wait_ge(s_lat, half + 1)
                copy(qT[:, 0, half * HALF:(half + 1) * HALF], ps[:, 2 + half, :]).then_inc(s_latE, 1)
            gates_evac(7, E3)
            run_units(FF[7], unit(f, ACT.Relu, lambda k: 4 + 2 * (k % 2), "h"))
            act.wait_ge(f["down"], FF[7])
            for half in range(2):
                copy(qT[:, 1, half * HALF:(half + 1) * HALF], ps[:, half, :]).then_inc(s_yl, 1)
            for n in range(FF[8]):
                unit(Fs[8], ACT.Relu, lambda k: 4 + k % 4, "h")(n, n, n)

        @block.vector
        def _(v):
            ch = Chain(v, s_dve)
            link = ch.link

            def ln_stats(l, t):
                link(v.bn_stats(st[:, t, :], x[:, t, :]))
                v.bn_aggr(mv[:, t, :], st[:, t, :]).then_inc(ln_var, 1)

            def ln_norm(l, t):
                v.wait_ge(ln_rstd, NT * l + t + 1)
                v.tensor_scalar(xn[:, t, :], x[:, t, :], mv[:, t, 0:1], rstd[:, t:t + 1], ALU.subtract,
                                ALU.mult).then_inc(ln_xn, 1)

            def biased(a, buf, first, bias):
                for t in range(NT):
                    v.wait_ge(a["pr_full"], first + t + 1)
                    v.tensor_tensor(buf[:, t, :], ps[:, 4 + t % 4, 0:D], bias, ALU.add).then_inc(a["raw"], 1)

            def normalize_0(a, buf, first, gain):
                for t in range(NT):
                    v.wait_ge(a["rms"], first // 4 + t // 4 + 1)
                    v.scalar_tensor_tensor(out=buf[:, t, :], in0=buf[:, t, :], scalar=ssr[:, first // NT, t:t + 1],
                                           in1=gain, op0=ALU.mult, op1=ALU.mult).then_inc(a["normed"], 1)

            def sums_6(a, first):
                for q in range(2):
                    for t in range(4 * q, 4 * q + 4):
                        v.wait_ge(a["sq"], first + t + 1)
                        v.tensor_reduce(ss[:, t, :], junk[:, t % 2, :].rearrange("p (h e) -> p h e", e=8), AX.X,
                                        ALU.add).then_inc(a["sum"], 1)
                    v.wait_ge(a["sum"], first + 4 * q + 4)
                    v.tensor_scalar(ssv[:, 4 * q:4 * q + 4, :], ss[:, 4 * q:4 * q + 4, :], 1.0 / 8, 1e-6, ALU.mult,
                                    ALU.add).then_inc(a["ss"], 1)

            def normalize_6(a, buf, first):
                for q in range(2):
                    r, m, y = (b_[:, 4 * q:4 * q + 4, :] for b_ in (ss, ssv, ssr))
                    v.wait_ge(a["rms"], first // 4 + q + 1)
                    link(v.reciprocal(y, y))
                    link(v.tensor_tensor(r, y, y, ALU.mult))
                    link(v.tensor_tensor(r, r, m, ALU.mult))
                    link(v.tensor_scalar(r, r, -0.5, 1.5, ALU.mult, ALU.add))
                    link(v.tensor_tensor(y, y, r, ALU.mult))
                    for t in range(4 * q, 4 * q + 4):
                        o = buf[:, t, :].rearrange("p (h e) -> p h e", e=8)
                        v.tensor_tensor(o, o, ssr[:, t, :].unsqueeze(2).to_broadcast([P, 32, 8]),
                                        ALU.mult).then_inc(a["normed"], 1)

            def values(a, V, e, bias):
                for b in range(B):
                    v.wait_ge(a["v_full"], b + 1)
                    for h in range(2):
                        r = slice(h * S, (h + 1) * S)
                        src = ps[r, 4 + b % 4, 0:D // 2].rearrange("p (j e) -> p j e", e=e)
                        dst = V[r, b, :, h, 0:e]
                        if bias is None:
                            ins = v.tensor_copy(dst, src)
                        else:
                            ins = v.tensor_tensor(dst, src,
                                                  bias[r, h * (D // 2):(h + 1) * (D // 2)].rearrange("p (j e) -> p j e", e=e),
                                                  ALU.add)
                    ins.then_inc(a["v_done"], 1)

            def gate(l):
                return tg[:, (l // 2 if l % 2 == 0 else 4 + l // 2):][:, 0:1]

            def clean(ap, n):
                c, m = cr[:, 0:n], cm[:, 0:n]
                link(v.tensor_scalar(c, ap, 0.0, 1e4, ALU.max, ALU.min))
                v.tensor_scalar(m, ap, 0.0, 0.0, ALU.mult, ALU.not_equal)
                link(v.scalar_tensor_tensor(out=c, in0=ap, scalar=0.0, in1=c, op0=ALU.min, op1=ALU.add))
                link(v.tensor_scalar(c, c, -1e4, None, ALU.max))
                return v.copy_predicated(ap, m, c)

            def head_norm(a, t, bank, heads, e, eps):
                par = t % 2
                o = ps[:, bank, 0:heads * (e + 1)].rearrange("p (h e) -> p h e", e=e + 1)
                r = rden[:, par, 0:heads]
                if eps:
                    d = den2[:, par, 0:heads]
                    link(v.tensor_copy(d, o[:, :, e]))
                    link(v.scalar_tensor_tensor(out=d, in0=d, scalar=1e-8, in1=d, op0=ALU.mult, op1=ALU.add))
                    link(v.reciprocal(r, d))
                else:
                    link(v.reciprocal(r, o[:, :, e]))
                return v.tensor_tensor(oN[:, par, :].rearrange("p (h e) -> p h e", e=e), o[:, :, 0:e],
                                       r.unsqueeze(2).to_broadcast([P, heads, e]), ALU.mult)

            def residual(l, t, done, src, scalar):
                link(v.scalar_tensor_tensor(out=x[:, t, :], in0=src, scalar=scalar, in1=x[:, t, :], op0=ALU.mult,
                                            op1=ALU.add))
                if l + 1 < NL:
                    link(v.bn_stats(st[:, t, :], x[:, t, :]))
                    v.bn_aggr(mv[:, t, :], st[:, t, :]).then_inc(ln_var, 1)
                if done is not None:
                    v.sem_inc(done, 1)

            a = A[0]
            v.wait_ge(s_x, 16)
            for t in range(NT):
                ln_stats(0, t)
                if t >= 2:
                    ln_norm(0, t - 2)
            for t in range(NT - 2, NT):
                ln_norm(0, t)
            v.wait_ge(s_rows, 16)
            biased(a, k_tok, 0, R("bk0"))
            v.wait_ge(s_cst, 4)
            values(a, Vp, 16, R("bv0"))
            normalize_0(a, k_tok, 0, R("gk0"))
            biased(a, q_tok, NT, R("bq0"))
            normalize_0(a, q_tok, NT, R("gq0"))
            v.wait_ge(s_tanh, 1)
            for s in range(NT + 4):
                t = s
                if t < NT:
                    for j in range(4):
                        v.wait_ge(a["sc_full"], 4 * t + j + 1)
                        if t >= 2 and j == 0:
                            v.wait_ge(a["pT_full"], 2 * (t - 1))
                        sc = ps[:, j, 0:D].rearrange("p (h s) -> p h s", s=S)
                        mj = mx[:, t % 2, 4 * j:4 * j + 4]
                        link(v.tensor_reduce(mj, sc, AX.X, ALU.max))
                        v.tensor_tensor(probs[:, t % 2, j * D:(j + 1) * D].rearrange("p (h s) -> p h s", s=S), sc,
                                        mj.unsqueeze(2).to_broadcast([P, 4, S]), ALU.subtract).then_inc(a["sc_free"], 1)
                t = s - 1
                if 0 <= t < NT:
                    v.wait_ge(a["pT_full"], 2 * t + 2)
                    v.tensor_copy(probs[:, t % 2, 1536:2048], ps[:, 5, :]).then_inc(a["pT_dve"], 1)
                t = s - 2
                if 0 <= t < NT:
                    v.wait_ge(a["pv_full"], t + 1)
                    head_norm(a, t, 6, 16, 16, False).then_inc(a["o_norm"], 1)
                t = s - 3
                if 0 <= t < NT:
                    v.wait_ge(a["o_proj"], t + 1)
                    link(v.tensor_tensor(junk[:, t % 2, :], ps[:, 7, D:2 * D], R("bo0"), ALU.add))
                    residual(0, t, a["resid"], junk[:, t % 2, :], gate(0))
                t = s - 4
                if 0 <= t:
                    ln_norm(1, t)
            def view(buf, e):
                return buf[:, 0:NT * e].rearrange("p (t e) -> p t e", t=NT)

            def over(small, e):
                return small.unsqueeze(2).to_broadcast([P, NT, e])

            def split(g, e, f):
                gv = g3[:, 0:NT * 3 * e].rearrange("p (t k e) -> p t k e", t=NT, k=3)
                r1, r2 = view(lc, e), view(la, e)
                link(v.tensor_copy(gv[:, :, 0, :], g))
                link(v.tensor_tensor(r1, g, gv[:, :, 0, :], ALU.subtract))
                link(v.tensor_copy(gv[:, :, 1, :], r1))
                link(v.tensor_tensor(r2, r1, gv[:, :, 1, :], ALU.subtract))
                v.tensor_copy(gv[:, :, 2, :], r2).then_inc(f["gates"], 1)

            def run_units(units, one):
                for k in range(4):
                    one(k, k, k)
                with v.Fori(1, units // 4) as i:
                    for k in range(4):
                        one(i * 4 + k, 4 + k, k)

            def remainder(l, n, k):
                v.wait_ge(Fs[l]["h_hi"], n + 1)
                v.tensor_tensor(HL[:, k % 2, :], sbuf_h[:, k % 2, :], HH[l][:, k % 2, :], ALU.subtract).then_inc(
                    Fs[l]["h_lo"], 1)

            def ffn_residual(l, f, units):
                for t in range(NT + 1):
                    if t < NT:
                        if l in (3, 5):
                            v.wait_ge(f["y"], t // 2 + 1)
                        else:
                            v.wait_ge(f["down"], units - 1 + t // 4)
                        residual(l, t, None, ps[:, t // 2, (t % 2) * D:(t % 2 + 1) * D], gate(l))
                    if t >= 1:
                        ln_norm(l + 1, t - 1)

            f = Fs[1]
            v.wait_ge(f["logits"], 1)
            lgv, lav, lbv, lcv, ldv = (view(b_, E0) for b_ in (lg, la, lb, lc, ld))
            link(v.tensor_tensor(lgv, ps[:, 0, 0:NT * E0].rearrange("p (t e) -> p t e", t=NT),
                                 R("br0").unsqueeze(1).to_broadcast([P, NT, E0]), ALU.add))
            link(v.tensor_reduce(red[:, :], lgv, AX.X, ALU.max))
            v.tensor_tensor(lav, lgv, over(red[:, :], E0), ALU.subtract).then_inc(f["lread"], 1)
            v.wait_ge(f["lread"], 1)
            link(v.tensor_scalar(lcv, lav, 0.0, None, ALU.is_ge))
            link(v.tensor_tensor(ldv, lcv, R("first8").unsqueeze(1).to_broadcast([P, NT, E0]), ALU.mult))
            link(v.tensor_reduce(red2[:, :], ldv, AX.X, ALU.max))
            link(v.tensor_tensor(lcv, ldv, over(red2[:, :], E0), ALU.is_equal))
            v.wait_ge(f["e"], 1)
            link(v.tensor_reduce(vm[:, :], lbv, AX.X, ALU.add))
            link(v.reciprocal(red[:, :], vm[:, :]))
            link(v.tensor_scalar(red[:, :], red[:, :], 1.0 / R0, None, ALU.mult))
            link(v.tensor_tensor(ldv, lcv, over(red[:, :], E0), ALU.mult))
            split(ldv, E0, f)

            def one_1(n, low, k):
                v.wait_ge(f["act"], n + 1)
                v.wait_ge(f["cw"], n + 1)
                if low >= 2:
                    v.wait_ge(f["down"], n - 1)
                v.tensor_tensor(sbuf_h[:, k % 2, :], sbuf_s[:, k % 2, :], ps[:, 5 + 2 * (k % 2), :],
                                ALU.mult).then_inc(f["h"], 1)

            for n in range(FF[1]):
                one_1(n, n, n)
            v.wait_ge(s_misc, 16 * 6)
            link(v.tensor_copy(m32[:, :, :], m8[:, :, :]))
            link(v.tensor_reduce(vm[:, :], m32[:, :, :], AX.X, ALU.max))
            v.memset(cr[:, :], NEG * D ** 0.5)
            link(v.memset(probs[:, 0, 0:NT * P], 0.0))
            ffn_residual(1, f, FF[1])
            sv = cr[:, :].rearrange("p (t n) -> p t n", t=NT)
            for half in range(2):
                ts = slice(4 * half, 4 * half + 4)
                v.wait_ge(a2["sc_full"], half + 1)
                link(v.copy_predicated(sv[:, ts, :], m32[:, ts, :],
                                       ps[:, 4 + half, 0:4 * S].rearrange("p (t n) -> p t n", t=4)))
                link(v.tensor_reduce(red[:, ts], sv[:, ts, :], AX.X, ALU.max))
                v.tensor_tensor(sv[:, ts, :], sv[:, ts, :], red[:, ts].unsqueeze(2).to_broadcast([P, 4, S]),
                                ALU.subtract).then_inc(a2["shift"], 1)
            pd = probs[:, 0, 0:NT * P].rearrange("p (t n) -> p t n", t=NT)
            v.wait_ge(a2["p_ready"], 4)
            link(v.tensor_reduce(red2[:, :], pd, AX.X, ALU.add))
            link(v.reciprocal(red2[:, :], red2[:, :]))
            link(v.tensor_tensor(red2[:, :], red2[:, :], vm[:, :], ALU.mult))
            link(v.tensor_scalar(red2[:, :], red2[:, :], gate(2), None, ALU.mult))
            for t in range(NT + 1):
                if t < NT:
                    v.wait_ge(a2["pv_full"], t + 1)
                    residual(2, t, a2["resid"], ps[:, 4 + t % 2, 0:D], red2[:, t:t + 1])
                if t >= 1:
                    ln_norm(3, t - 1)
            f3 = Fs[3]
            EX = E1 + 8 - TOP1
            lc20, la20 = (b_[:, 0:NT * EX].rearrange("p (t e) -> p t e", t=NT) for b_ in (lc, la))
            lg17, ld24 = view(lg, E1 + 1), view(ld, EP1)
            lbv = view(lb, E1)
            t8 = top8[:, 0:NT * 8].rearrange("p (t e) -> p t e", t=NT)
            link(v.memset(lc20[:, :, E1:EX], BIG))
            v.wait_ge(f3["logits"], 1)
            v.tensor_copy(lg17, ps[:, 0, 0:NT * (E1 + 1)].rearrange("p (t e) -> p t e", t=NT)).then_inc(f3["lread"], 1)
            v.wait_ge(f3["lread"], 1)
            link(v.tensor_copy(lc20[:, :, 0:E1], lg17[:, :, 0:E1]))
            for t in range(NT):
                ins = v.max(t8[:, t, :], lc20[:, t, :])
            link(ins)
            v.tensor_tensor(lbv, lg17[:, :, 0:E1], over(t8[:, :, 8 - TOP1], E1), ALU.subtract).then_inc(f3["lread"], 1)
            for t in range(NT):
                ins = v.match_replace(out=la20[:, t, :], in_to_replace=t8[:, t, :], in_values=lc20[:, t, :],
                                      imm_value=-BIG)
            link(ins)
            link(v.tensor_tensor(la20, la20, lc20, ALU.not_equal))
            v.wait_ge(f3["e"], 2)
            link(v.tensor_tensor(lbv, lbv, la20[:, :, 0:E1], ALU.mult))
            link(v.tensor_reduce(red[:, :], lbv, AX.X, ALU.add))
            link(v.reciprocal(red[:, :], red[:, :]))
            link(v.memset(ld24[:, :, E1 + 1:EP1], 0.0))
            v.tensor_tensor(ld24[:, :, 0:E1], lbv, over(red[:, :], E1), ALU.mult)
            link(v.tensor_scalar(rk[:, 0:NT], rk[:, 0:NT], 1.0, None, ALU.add))
            link(v.reciprocal(ld24[:, :, E1], rk[:, 0:NT]))
            split(ld24, EP1, f3)

            def one_3(n, low, k):
                v.wait_ge(f3["act"], n + 1)
                if low >= 1:
                    v.wait_ge(f3["h"], n)
                v.tensor_tensor(sbuf_t[:, k % 2, :], sbuf_s[:, k % 2, :], ps[:, 4 + (3 * k + 1) % 4, :],
                                ALU.mult).then_inc(f3["mid"], 1)
                v.wait_ge(f3["mid"], n + 1)
                v.wait_ge(f3["cw"], n + 1)
                if low >= 2:
                    v.wait_ge(f3["down"], n - 1)
                v.tensor_tensor(sbuf_h[:, k % 2, :], sbuf_t[:, k % 2, :], ps[:, 4 + (3 * k + 2) % 4, :],
                                ALU.mult).then_inc(f3["h"], 1)
                remainder(3, n, k)

            run_units(FF[3], one_3)
            ffn_residual(3, f3, FF[3])
            a = A[4]
            bqk = L("bqk2")
            link(v.tensor_scalar(hi2[:, :], mraw[:, :], 0.5, 400.0, ALU.is_gt, ALU.mult))
            link(v.tensor_scalar(hi2[:, :], hi2[:, :], -200.0, None, ALU.add))
            link(v.tensor_scalar(rs[:, :], R("rs2"), 0.0, 0.3, ALU.max, ALU.min))
            for g in range(4):
                c = g // 2
                v.wait_ge(a["kq_full"], g + 1)
                if g >= 2:
                    v.wait_ge(a["k_ready"], 2 * (g - 1))
                dst = sbuf_s[:, g % 2, :]
                link(v.tensor_scalar(dst, ps[:, 4 + g, :], bqk[:, KC + c:KC + c + 1], None, ALU.add))
                clean(dst, HALF).then_inc(a["kq_done"], 1)
            values(a, Vp, 16, R("bv2"))
            v.wait_ge(a["v_done"], B)
            for at in range(0, B * 272, HALF):
                n = min(HALF, B * 272 - at)
                link(clean(vpair[:, at:at + n], n))
            for g in range(4):
                c, half = g // 2, g % 2
                v.wait_ge(a["kq_full"], 4 + g + 1)
                dst = qT[:, c, half * HALF:(half + 1) * HALF]
                link(v.tensor_scalar(dst, ps[:, 4 + g, :], bqk[:, c:c + 1], None, ALU.add))
                clean(dst, HALF).then_inc(a["q_ready"], 1)
            def x_lo_5(k):
                v.wait_ge(Fs[5]["x_hi"], k + 1)
                v.tensor_tensor(XL[5][:, :, 2 * k * P:2 * (k + 1) * P].rearrange("p c (t n) -> p t c n", t=2),
                                ps[:, k, :].rearrange("p (t c n) -> p t c n", t=2, c=KC),
                                XH[:, :, 2 * k * P:2 * (k + 1) * P].rearrange("p c (t n) -> p t c n", t=2),
                                ALU.subtract).then_inc(Fs[5]["x_lo"], 1)

            for s in range(NT + 4):
                t = s
                if t < NT:
                    v.wait_ge(a["sc_full"], t + 1)
                    if t >= 2:
                        v.wait_ge(a["pv_full"], t - 1)
                    for b in range(BT):
                        ins = v.tensor_scalar(
                            probs[:, t % 2, 0:1024].rearrange("p (j c b n) -> p j c b n", j=4, c=KC, b=BT)[:, :, :, b, :],
                            ps[:, 0:4, 0:D].rearrange("p j (c b n) -> p j c b n", c=KC, b=BT)[:, :, :, b, :],
                            hi2[:, BT * t + b:BT * t + b + 1], -200.0, ALU.min, ALU.max)
                    ins.then_inc(a["sc_free"], 1)
                t = s - 1
                if 0 <= t < NT:
                    v.wait_ge(a["pv_full"], t + 1)
                    head_norm(a, t, 4 + t % 2, 16, 16, True).then_inc(a["o_norm"], 1)
                t = s - 2
                if 0 <= t < NT:
                    v.wait_ge(a["o_proj"], t + 1)
                    d = junk[:, t % 2, :]
                    link(v.tensor_tensor(d, ps[:, 6 + t % 2, D:2 * D], R("bo2"), ALU.add))
                    link(clean(d, D))
                    link(v.tensor_scalar(d, d, rs[:, 0:1], None, ALU.mult))
                    link(v.bn_stats(st[:, t, :], d))
                    v.bn_aggr(mv[:, t, :], st[:, t, :]).then_inc(a["dvar"], 1)
                t = s - 3
                if 0 <= t < NT:
                    d = junk[:, t % 2, :]
                    v.wait_ge(a["drstd"], t + 1)
                    link(v.tensor_scalar(d, d, mv[:, t, 0:1], rstd[:, t:t + 1], ALU.subtract, ALU.mult))
                    link(v.tensor_tensor(d, d, R("gamma2"), ALU.mult))
                    link(v.tensor_tensor(d, d, R("beta2"), ALU.add))
                    residual(4, t, a["resid"], d, gate(4))
                t = s - 4
                if 0 <= t:
                    ln_norm(5, t)
                if s >= NT + 2:
                    for k in range(2):
                        x_lo_5(2 * (s - NT - 2) + k)
            f5 = Fs[5]

            def one_5(n, low, k):
                v.wait_ge(f5["act"], n + 1)
                if low >= 2:
                    v.wait_ge(f5["down"], n - 1)
                v.tensor_tensor(sbuf_h[:, k % 2, :], sbuf_s[:, k % 2, :], ps[:, 5 + 2 * (k % 2), :],
                                ALU.mult).then_inc(f5["h"], 1)
                remainder(5, n, k)

            run_units(FF[5], one_5)
            ffn_residual(5, f5, FF[5])
            a = A[6]
            v.wait_ge(s_vq, 2)
            sums_6(a, 0)
            values(a, Vq, 8, None)
            normalize_6(a, k_tok, 0)
            sums_6(a, NT)

            def remainders(first, dst):
                for t in range(NT):
                    v.wait_ge(a["hi"], first + t + 1)
                    v.tensor_tensor(dst[:, 1, :, tok(t)], ps[:, 4 + t % 4, 0:D].rearrange("p (c n) -> p c n", c=KC),
                                    dst[:, 0, :, tok(t)], ALU.subtract).then_inc(a["T_done"], 1)

            remainders(0, k16)
            normalize_6(a, q_tok, NT)
            v.wait_ge(a["T_done"], NT)
            for half in range(2):
                bs = slice(half * 8, half * 8 + 8)
                for h in range(4):
                    for i in range(2):
                        ins = v.tensor_scalar(Kq[:, i, :, bs, h, :],
                                              k16[:, i, :, half * HALF:(half + 1) * HALF].rearrange("p c (b s) -> p c b s", s=S),
                                              E("quad")[:, h:h + 1], None, ALU.mult)
                ins.then_inc(a["masked"], 1)
            remainders(NT, q16)
            for t in range(NT + 1):
                if t < NT:
                    v.wait_ge(a["pv_full"], t + 1)
                    link(head_norm(a, t, 4 + t % 2, 32, 8, False))
                    v.sem_inc(a["o_norm"], 1)
                    residual(6, t, a["resid"], oN[:, t % 2, :], gate(6))
                if t >= 1:
                    ln_norm(7, t - 1)
            f7, f8 = Fs[7], Fs[8]
            sig, sbv, mk, rep = la, lg, lc, ld
            v.wait_ge(f7["e"], 1)
            link(v.tensor_scalar(lb[:, :], lb[:, :], 1.0, None, ALU.add))
            link(v.reciprocal(sig[:, :], lb[:, :]))
            link(v.tensor_tensor(view(sbv, E3), view(sig, E3), R("bias3").unsqueeze(1).to_broadcast([P, NT, E3]),
                                 ALU.add))
            for g in range(NT * G3):
                ins = v.max(top8[:, g * 8:g * 8 + 8], sbv[:, g * 8:g * 8 + 8])
            link(ins)
            tops = top8[:, :].rearrange("p (g e) -> p g e", e=8)
            link(v.tensor_tensor(gsc[:, :], tops[:, :, 0], tops[:, :, 1], ALU.add))
            gs = gsc[:, :].rearrange("p (t g) -> p t g", t=NT)
            other = gs.unsqueeze(2).to_broadcast([P, NT, G3, G3])
            own = gs.unsqueeze(3).to_broadcast([P, NT, G3, G3])
            r4, r4b = (b_[:, :].rearrange("p (t g o) -> p t g o", t=NT, g=G3) for b_ in (rk, rk2))
            v.tensor_tensor(r4, other, own, ALU.is_gt)
            link(v.tensor_tensor(r4b, other, own, ALU.is_equal))
            link(v.tensor_tensor(rk2[:, :].rearrange("p (t n) -> p t n", t=NT), rk2[:, :].rearrange("p (t n) -> p t n", t=NT),
                                 R("lower4").unsqueeze(1).to_broadcast([P, NT, G3 * G3]), ALU.mult))
            link(v.tensor_tensor(rk[:, :], rk[:, :], rk2[:, :], ALU.add))
            link(v.tensor_reduce(gsd[:, :], rk[:, :].rearrange("p (g o) -> p g o", o=G3), AX.X, ALU.add))
            link(v.tensor_scalar(gsd[:, :], gsd[:, :], TOPG3 - 0.5, None, ALU.is_lt))
            link(v.tensor_scalar(gsc[:, :], gsd[:, :], -NEG, NEG, ALU.mult, ALU.add))

            def by_group(buf):
                return buf[:, :].rearrange("p (g e) -> p g e", e=8)

            link(v.tensor_tensor(by_group(mk), by_group(sbv), gsd[:, :].unsqueeze(2).to_broadcast([P, NT * G3, 8]), ALU.mult))
            link(v.tensor_tensor(by_group(mk), by_group(mk), gsc[:, :].unsqueeze(2).to_broadcast([P, NT * G3, 8]), ALU.add))
            for t in range(NT):
                ins = v.max(top8[:, t * 8:t * 8 + 8], mk[:, t * E3:(t + 1) * E3])
            link(ins)
            for t in range(NT):
                ins = v.match_replace(out=rep[:, t * E3:(t + 1) * E3], in_to_replace=top8[:, t * 8:t * 8 + 8],
                                      in_values=mk[:, t * E3:(t + 1) * E3], imm_value=-BIG)
            link(ins)
            link(v.tensor_tensor(rep[:, :], rep[:, :], mk[:, :], ALU.not_equal))
            link(v.tensor_tensor(lb[:, :], sig[:, :], rep[:, :], ALU.mult))
            link(v.tensor_reduce(red[:, :], view(lb, E3), AX.X, ALU.add))
            link(v.reciprocal(red[:, :], red[:, :]))
            link(v.tensor_scalar(red[:, :], red[:, :], SCALE3, None, ALU.mult))
            link(v.tensor_tensor(view(ld, E3), view(lb, E3), over(red[:, :], E3), ALU.mult))
            split(view(ld, E3), E3, f7)

            def one_7(n, low, k):
                v.wait_ge(f7["act"], n + 1)
                v.wait_ge(f7["cw"], n + 1)
                if low >= 1:
                    v.wait_ge(f7["h"], n)
                v.tensor_tensor(sbuf_t[:, k % 2, :], sbuf_s[:, k % 2, :], ps[:, 5 + 2 * (k % 2), :],
                                ALU.mult).then_inc(f7["mid"], 1)
                v.wait_ge(f7["mid"], n + 1)
                if low >= 2:
                    v.wait_ge(f7["down"], n - 1)
                v.tensor_tensor(sbuf_h[:, k % 2, :], sbuf_t[:, k % 2, :], sbuf_s[:, k % 2, :],
                                ALU.mult).then_inc(f7["h"], 1)

            run_units(FF[7], one_7)
            for n in range(FF[8]):
                v.wait_ge(f8["act"], n + 1)
                if n >= 2:
                    v.wait_ge(f8["down"], n - 1)
                else:
                    v.wait_ge(f7["down"], FF[7])
                v.tensor_tensor(sbuf_h[:, n % 2, :], sbuf_s[:, n % 2, :], sbuf_s[:, n % 2, :], ALU.mult).then_inc(f8["h"], 1)
            for t in range(NT):
                v.wait_ge(f8["down"], FF[8] - 1 + t // 4)
                residual(7, t, f8["resid"], ps[:, t // 2, (t % 2) * D:(t % 2 + 1) * D], gate(7))



def kernel(**inputs):
    import ml_dtypes
    import concourse.bacc as _bacc
    from concourse.bass_utils import run_bass_kernel_spmd as _run

    a = {k: np.asarray(v) for k, v in inputs.items()}
    f = np.float32

    def tiles(v):
        return v.reshape(NT, P, D).transpose(1, 0, 2)

    def wT(w):
        return w.T.reshape(-1, P, w.shape[0]).transpose(1, 0, 2).reshape(P, -1)

    def row(v):
        return v.reshape(1, -1)

    def even_odd(v, e):
        return np.moveaxis(v.reshape(*v.shape[:-1], D // 2 // e, 2, e), -2, -3).reshape(v.shape)

    first8 = np.arange(E0, 0, -1, dtype=f)
    lower4 = np.tril(np.ones((G3, G3), f), -1)
    rows_d = dict(bq0=a["L0_xattn_b_q"], bk0=a["L0_xattn_b_k_img"], bv0=even_odd(a["L0_xattn_b_v_img"], 16), bo0=a["L0_xattn_b_o"],
                  gq0=a["L0_xattn_g_q"], gk0=a["L0_xattn_g_k_img"], br0=a["L0_ffn_br"], bv2=even_odd(a["L2_xattn_bv"], 16),
                  bo2=a["L2_xattn_bo"], gamma2=a["L2_xattn_ln_gamma"], beta2=a["L2_xattn_ln_beta"],
                  bias3=a["L3_ffn_gate_bias"], rs2=a["L2_xattn_residual_scale"],
                  gates=np.concatenate([a["g_xattn"], a["g_ffn"]]), first8=first8, lower4=lower4)
    rows = np.concatenate([row(rows_d[n]) for n, _ in ROWS], 1)

    part = np.arange(P)
    pair = (part[:, None] // 16 % 2 == np.arange(2)).astype(f)
    quad = (part[:, None] // 8 % 4 == np.arange(4)).astype(f)
    early_d = dict(wk0=wT(a["L0_xattn_w_k_img"]), wq0=wT(a["L0_xattn_w_q"]), wv0=wT(even_odd(a["L0_xattn_w_v_img"].T, 16).T),
                   wo0=wT(a["L0_xattn_w_o"]), ident=np.eye(P, dtype=f), pair=pair, quad=quad)
    early = np.concatenate([early_d[n] for n, _ in EARLY], 1)

    had = np.ones((1, 1), f)
    while had.shape[0] < P:
        had = np.block([[had, had], [had, -had]])
    kv3 = np.concatenate([a["L3_xattn_Wk"], a["L3_xattn_Wv"]])
    col = lambda b: b.reshape(KC, P).T
    late_d = dict(
        A0=wT(a["L0_ffn_A"].reshape(E0 * R0, D)), B0=wT(a["L0_ffn_B"].transpose(1, 0, 2).reshape(D, E0 * R0)),
        wr0=wT(a["L0_ffn_Wr"]), gate1=wT(np.concatenate([a["L1_ffn_gate_w"], a["L1_ffn_shared_gate_vec"]])),
        wk2=wT(a["L2_xattn_Wk"]), wq2=wT(a["L2_xattn_Wq"]), wv2=wT(even_odd(a["L2_xattn_Wv"].T, 16).T), wo2=wT(a["L2_xattn_Wo"]),
        bqk2=np.concatenate([col(a["L2_xattn_bq"]), col(a["L2_xattn_bk"])], 1),
        had=had, w2f=wT(a["L2_ffn_W2"]), wk3=wT(kv3[0::2]), wq3=wT(a["L3_xattn_Wq"]), wv3=wT(even_odd(kv3[1::2].T, 8).T),
        gate3=wT(a["L3_ffn_gate_w"]), fc1=wT(a["L3_ffn_fc1_w"]), fc2=wT(a["L3_ffn_fc2_w"]),
        up3=a["L3_ffn_shared_up_w"].reshape(C3S, P, KC, P).transpose(3, 0, 2, 1).reshape(P, -1),
        down3=wT(a["L3_ffn_shared_down_w"]))
    late = np.concatenate([late_d[n] for n, _ in LATE], 1)

    gu = a["L1_ffn_expert_gate_up"]
    sgu = a["L1_ffn_shared_gate_up"]
    pad = np.zeros((C1 * P - E1 * I1 - SI1, D), f)
    g_rows = np.concatenate([gu[:, :I1].reshape(-1, D), sgu[:SI1], pad])
    u_rows = np.concatenate([gu[:, I1:].reshape(-1, D), sgu[SI1:], pad])
    d_rows = np.concatenate([a["L1_ffn_expert_down"].transpose(0, 2, 1).reshape(-1, D), a["L1_ffn_shared_down"].T, pad])

    def chunks_up(g, u, n):
        both = np.stack([g.reshape(n, P, KC, P), u.reshape(n, P, KC, P)])
        return both.transpose(1, 4, 3, 0, 2).reshape(n, P, KC * 2 * P)

    w1 = np.concatenate([chunks_up(g_rows, u_rows, C1), d_rows.reshape(C1, P, D)], 2)
    w2 = chunks_up(a["L2_ffn_W1"], a["L2_ffn_W3"], C2)
    w3 = np.concatenate([a["L3_ffn_w1"].transpose(0, 2, 1), a["L3_ffn_w2"].transpose(0, 2, 1)], 2)

    def selector(expert_of, e):
        one = (expert_of[None, :] == np.arange(e)[:, None])
        return np.concatenate([one] * 3).astype(ml_dtypes.bfloat16)

    h1 = np.arange(C1 * P)
    e1 = np.where(h1 < E1 * I1, h1 // I1, E1)
    mask1 = a["mask_BxS2_bk0"].reshape(NT, BT, 1, S).repeat(S, 2).reshape(NT, P, S).transpose(1, 0, 2)
    mask2 = np.tile(a["mask_BxS2_ik0"].T, (2, 1))
    arrays = dict(
        x_dram=tiles(a["x"]), ctx_dram=tiles(a["ctx_2048"]),
        ctxT_dram=a["ctx_2048"].reshape(TOK, KC, P).transpose(2, 1, 0), rows_dram=rows, early_dram=early,
        late_dram=late, w1_dram=w1, w2_dram=w2, w3_dram=w3, mask1_dram=mask1, mask2_dram=mask2,
        identb_dram=np.eye(P, dtype=ml_dtypes.bfloat16), sel0_dram=selector(np.arange(E0 * R0) // R0, E0),
        sel1_dram=selector(e1, EP1), sel3_dram=selector(np.arange(E3 * P) // P, E3))
    arrays = {k: np.ascontiguousarray(v) for k, v in arrays.items()}

    nc = _bacc.Bacc("TRN2", target_bir_lowering=False, num_devices=1)
    args = [nc.dram_tensor(k, v.shape, U8 if v.dtype == bool else mybir.dt.from_np(v.dtype), kind="ExternalInput").ap() for k, v in arrays.items()]
    args.append(nc.dram_tensor("out_dram", (P, NT, D), F32, kind="ExternalOutput").ap())
    flamingo_kernel(nc, *args)
    r = _run(nc, [arrays], core_ids=[0])
    return r.results[0]["out_dram"].transpose(1, 0, 2).reshape(B, S, D)
```

```python
from contextlib import ExitStack, contextmanager

import numpy as np

import concourse.bass as bass
from concourse import mybir

F32 = mybir.dt.float32
BF16 = mybir.dt.bfloat16
F16 = mybir.dt.float16
F32R = mybir.dt.float32r
I32 = mybir.dt.int32
U8 = mybir.dt.uint8
ALU = mybir.AluOpType
ACT = mybir.ActivationFunctionType
AX = mybir.AxisListType

P = 128
B, S, D = 16, 64, 256
TOK = B * S
NT = TOK // P
KC = D // P
BT = P // S
HALF = 512
NL = 8
BIG = 3.0e38
NEG = -1.0e30

E0, R0 = 8, 64
E1, I1, SI1 = 16, 176, 704
TOP1 = 4
EP1 = 24
C1 = -(-(E1 * I1 + SI1) // P)
H2 = 1024
C2 = H2 // P
E3, LAT3, SH3, G3 = 32, 128, 512, 4
TOP3, TOPG3, SCALE3 = 8, 2, 2.5
C3S = SH3 // P

ROWS = [("bq0", D), ("bk0", D), ("bv0", D), ("bo0", D), ("gq0", D), ("gk0", D), ("br0", E0),
        ("bv2", D), ("bo2", D), ("gamma2", D), ("beta2", D), ("bias3", E3), ("rs2", 1), ("gates", 8),
        ("first8", E0), ("lower4", G3 * G3)]
EARLY = [("wk0", KC * D), ("wq0", KC * D), ("wv0", KC * D), ("wo0", KC * D), ("ident", P), ("pair", 2), ("quad", 4)]
LATE = [("A0", KC * E0 * R0), ("B0", (E0 * R0 // P) * D), ("wr0", KC * E0), ("gate1", KC * (E1 + 1)),
        ("wk2", KC * D), ("wq2", KC * D), ("wv2", KC * D), ("wo2", KC * D), ("bqk2", 2 * KC),
        ("had", P), ("w2f", C2 * D),
        ("wk3", KC * D), ("wq3", KC * D), ("wv3", KC * D), ("gate3", KC * E3), ("fc1", KC * LAT3),
        ("fc2", D), ("up3", C3S * KC * P), ("down3", C3S * D)]


PIECES = -(-B * 272 // HALF) + KC * TOK // HALF
STEPS = 7
LIFT = 64.0


def columns(pack):
    at, out = 0, {}
    for name, n in pack:
        out[name] = (at, n)
        at += n
    return out, at


RCOL, RN = columns(ROWS)
ECOL, EN = columns(EARLY)
LCOL, LN_ = columns(LATE)
W1COLS = KC * 2 * P + D
W2COLS = KC * 2 * P
W3COLS = P + LAT3


class Named(dict):

    def __init__(self, make, prefix):
        super().__init__()
        self.make, self.prefix = make, prefix

    def __missing__(self, name):
        self[name] = self.make(self.prefix + name)
        return self[name]


class Chain:

    def __init__(self, eng, sem):
        self.eng, self.sem, self.n, self.i, self.per = eng, sem, 0, None, 0

    def value(self):
        return self.n if self.i is None else self.i * self.per + self.n

    def link(self, ins):
        ins.then_inc(self.sem, 1)
        self.n += 1
        self.eng.wait_ge(self.sem, self.value())

    @contextmanager
    def loop(self, start, end, per):
        base = self.n
        with self.eng.Fori(start, end) as i:
            self.i, self.per, self.n = i, per, base - start * per
            yield i
            assert self.n == base - start * per + per, (self.n, base, start, per)
        self.i, self.n = None, base + (end - start) * per


def flamingo_kernel(nc, x_in, ctx_in, ctxT_in, rows_in, early_in, late_in, w1_in, w2_in, w3_in,
                    mask1_in, mask2_in, identb_in, sel0_in, sel1_in, sel3_in, out):
    with ExitStack() as stack:
        def sb(name, shape, dt=F32):
            return stack.enter_context(nc.sbuf_tensor(name, shape, dt))

        def sem(name):
            return stack.enter_context(nc.semaphore(name))

        def sb_twice(name, shape):
            with nc.sbuf_tensor(name, shape, F32) as full:
                pass
            return full, sb(name + "_r", shape, F32R)

        x = sb("x", [P, NT, D])
        xn, xn_r = sb_twice("xn", [P, NT, D])
        xT = sb("xT", [P, KC, TOK])
        ctx = sb("ctx", [P, NT, D])
        ctxT = sb("ctxT", [P, KC, TOK])
        qT, qT_r = sb_twice("qT", [P, KC, TOK])
        k_tok = qT[:, :, :].rearrange("p c (t n) -> p (c t) n", n=D)
        q_tok = xn
        kpair, kpair_r = sb_twice("kpair", [P, KC * B * 4 * S])
        vpair = sb("vpair", [P, B * 288])
        probs, probs_r = sb_twice("probs", [P, 2, 2048])
        rows = sb("rows", [P, RN])
        early = sb("early", [P, EN])
        late = sb("late", [P, LN_])

        wring = sb("wring", [P, 2, W1COLS])
        sbuf_s = sb("act_s", [P, 2, HALF])
        sbuf_t = sb("mid_t", [P, 2, HALF])
        junk, oN = sbuf_t[:, 0, :].rearrange("p (a n) -> p a n", a=2), sbuf_t[:, 1, :].rearrange("p (a n) -> p a n", a=2)
        sbuf_h, hid_r = sb_twice("hid_h", [P, 2, HALF])
        oT = sbuf_h[:, 1, :].rearrange("p (a n) -> p a n", a=2)
        gT = sb("gT", [3 * E3, TOK], BF16)
        identb = sb("identb", [P, P], BF16)
        sel0 = sb("sel0", [3 * E0, E0 * R0], BF16)
        sel1 = sb("sel1", [3 * EP1, C1 * P], BF16)
        sel3 = ctx[:, :, :].rearrange("p t n -> p (t n)").bitcast(BF16)[0:3 * E3, :]
        m8 = sb("m8", [P, NT, S], U8)
        m32 = kpair[:, 16 * NT * E3:18 * NT * E3].bitcast(I32).rearrange("p (t s) -> p t s", t=NT)
        mraw = sb("mraw", [P, B], I32)
        hi2 = sb("hi2", [P, B])
        st = sb("st", [P, NT, 6])
        mv = sb("mv", [P, NT, 2])
        mhalf = sb("mhalf", [P, 32])
        rstd = sb("rstd", [P, NT])
        ve = sb("ve", [P, NT])
        cr = sb("cr", [P, HALF])
        ss, ssv = (cr[:, n * NT * 32:(n + 1) * NT * 32].rearrange("p (t n) -> p t n", t=NT) for n in range(2))
        ssr = sb("ssr", [P, NT, 32])
        mx = sb("mx", [P, 2, 16])
        rden = sb("rden", [P, 2, 32])
        den2 = sb("den2", [P, 2, 32])
        tg = sb("tg", [P, 8])
        rs = sb("rs", [P, 1])
        SCR = 18 * NT * E3
        lg, la, lb, lc, ld, top8 = (kpair[:, SCR + n * NT * E3:SCR + (n + 1) * NT * E3] for n in range(6))
        gsc = sb("gsc", [P, NT * G3])
        gsd = sb("gsd", [P, NT * G3])
        rk, rk2 = (kpair[:, at:at + NT * G3 * G3] for at in (SCR + 6 * NT * E3, SCR + 6 * NT * E3 + NT * G3 * G3))
        red = sb("red", [P, NT])
        red2 = sb("red2", [P, NT])
        vm = sb("vm", [P, NT])
        g3 = kpair[:, SCR + 7 * NT * E3:SCR + 9 * NT * E3].bitcast(BF16)[:, 0:NT * 3 * E3]
        cm, piece_own = (kpair[:, at:at + HALF] for at in (7168, 7168 + HALF))
        cm = cm.bitcast(I32)
        ps = stack.enter_context(nc.psum_tensor("ps", [P, 8, 512], F32))

        def E(name):
            a, n = ECOL[name]
            return early[:, a:a + n]

        def L(name):
            a, n = LCOL[name]
            return late[:, a:a + n]

        def R(name):
            a, n = RCOL[name]
            return rows[:, a:a + n]

        def kc(ap):
            return ap.rearrange("p (k n) -> p k n", k=KC)

        ident = E("ident")
        w2h = kpair[:, 0:C2 * D]
        s3 = probs_r[:, :, :].rearrange("p a n -> p (a n)")
        s5 = kpair_r[:, 4096:8192]
        WH, WL, HH = ({l: r[:, a:b].rearrange("p (c n) -> p c n", c=2) for l, r in ((3, s3), (5, s5))}
                      for a, b in ((0, 2 * W1COLS), (2 * W1COLS, 4 * W1COLS), (4 * W1COLS, 4 * W1COLS + 2 * HALF)))
        HL = hid_r
        XH = qT_r
        XL = {3: xn_r[:, :, :].rearrange("p t n -> p (t n)").rearrange("p (c n) -> p c n", c=KC),
              5: kpair_r[:, 0:KC * TOK].rearrange("p (c n) -> p c n", c=KC)}
        W7 = [probs_r[:, n, 0:2 * 512].rearrange("p (c n) -> p c n", c=2) for n in range(2)]
        H7 = [k_[:, 0:4 * HALF].rearrange("p (c n) -> p c n", c=4) for k_ in (kpair, kpair_r)]
        HH7 = kpair_r[:, 4 * HALF:8 * HALF].rearrange("p (c n) -> p c n", c=4)
        yT = qT
        Kp = kpair[:, 0:KC * B * 2 * S].rearrange("p (c b h s) -> p c b h s", c=KC, b=B, h=2)
        Kq = kpair[:, :].bitcast(F16).rearrange("p (i c b m s) -> p i c b m s", i=2, c=KC, b=B, m=4)
        k16 = probs[:, 1, :].bitcast(F16).rearrange("p (i c n) -> p i c n", i=2, c=KC)
        q16 = qT[:, :, :].rearrange("p c n -> p (c n)").bitcast(F16).rearrange("p (i c n) -> p i c n", i=2, c=KC)
        Vp = vpair[:, 0:B * 272].rearrange("p (b j h e) -> p b j h e", b=B, j=8, h=2)
        Vq = vpair[:, 0:B * 288].rearrange("p (b j h e) -> p b j h e", b=B, j=16, h=2)

        def tok(t):
            return slice(t * P, (t + 1) * P)

        s_x, s_first, s_early, s_rows, s_late, s_misc, s_out = map(sem, (
            "x_landed", "first_landed", "early_landed", "rows_landed", "late_landed", "misc_landed", "out_stored"))
        s_dve, s_pool = sem("dve_chain"), sem("pool_chain")
        s_cst = sem("consts_ready")
        s_tanh = sem("tanh_ready")
        ln_var, ln_rstd, ln_xn, ln_Tfull, ln_xT = map(sem, (
            "ln_variance", "ln_rstd", "ln_normed", "ln_transposed", "ln_xT"))
        w2_bf, w2_mm, w2_ev = sem("w2_butterfly"), sem("w2_hadamard"), sem("w2_ready")
        A = {l: Named(sem, f"attention{l}_") for l in (0, 4, 6)}
        a2 = Named(sem, "attention2_")
        Fs = {l: Named(sem, f"ffn{l}_") for l in (1, 3, 5, 7, 8)}
        s_lat, s_latE = sem("lat_full"), sem("lat_ready")
        s_vq = sem("vq_cleared")
        s_piece = sem("piece_step")
        s_sel3 = sem("sel3_landed")

        block = stack.enter_context(nc.Block())
        FF = {1: 8, 3: 2 * C1, 5: 2 * C2, 7: 2 * E3, 8: 2 * C3S}

        def down_weights(l, i, c):
            if l == 3:
                return wring[:, c, W2COLS:W1COLS]
            return L("w2f")[:, bass.ds(i * (2 * D) + c * D, D)]

        def mask_keys(half, multiply, done):
            bs = slice(half * 8, half * 8 + 8)
            for h in range(4):
                for i in range(2):
                    ins = multiply(Kq[:, i, :, bs, h, :],
                                   k16[:, i, :, half * HALF:(half + 1) * HALF].rearrange("p c (b s) -> p c b s", s=S),
                                   E("quad")[:, h:h + 1])
            ins.then_inc(done, 1)

        @block.sync
        def _(sp):
            first = sum(ECOL["wk0"])
            sp.dma_start(early[:, 0:first], early_in[:, 0:first]).then_inc(s_first, 16)
            sp.dma_start(ctxT[:, :, 0:HALF], ctxT_in[:, :, 0:HALF]).then_inc(s_first, 16)
            sp.dma_start(ctxT[:, :, HALF:TOK], ctxT_in[:, :, HALF:TOK]).then_inc(s_early, 16)
            sp.dma_start(early[:, first:EN], early_in[:, first:EN]).then_inc(s_early, 16)
            sp.dma_start(rows[:, :], rows_in.partition_broadcast(P)).then_inc(s_rows, 16)
            sp.dma_start(late[:, :], late_in).then_inc(s_late, 16)
            for dst, src in ((identb[:, :], identb_in), (sel0[:, :], sel0_in), (sel1[:, :], sel1_in),
                             (m8[:, :, :], mask1_in), (mraw[:, :], mask2_in),
                             (ctx[:, :, :], ctx_in)):
                sp.dma_start(dst, src).then_inc(s_misc, 16)
            for l, w, cols, chunks in ((3, w1_in, W1COLS, C1), (5, w2_in, W2COLS, C2), (7, w3_in, 2 * W3COLS, E3 // 2)):
                f = Fs[l]
                if l > 3:
                    before = Fs[l - 2]
                    sp.wait_ge(before["up_lo"], C1 if l == 5 else C2)
                    if l == 5:
                        sp.wait_ge(before["down_lo"], C1)
                        sp.dma_start(sel3, sel3_in).then_inc(s_sel3, 16)
                for c in range(2):
                    sp.dma_start(wring[:, c, 0:cols], w[c]).then_inc(f[f"land{c}"], 16)
                with sp.Fori(1, chunks // 2) as i:
                    for c in range(2):
                        if l == 7:
                            sp.wait_ge(Fs[5]["up_lo"], i * 2 + (C2 + c - 1))
                            sp.wait_ge(Fs[5]["down_lo"], i * 2 + (C2 + c - 1))
                        else:
                            sp.wait_ge(f["up_lo"], i * 2 + (c - 1))
                        if l == 3:
                            sp.wait_ge(f["down_lo"], i * 2 + (c - 1))
                        sp.dma_start(wring[:, c, 0:cols], w[bass.ds(i * 2 + c, 1)].rearrange("o p n -> (o p) n")
                                     ).then_inc(f[f"land{c}"], 16)
            for t in range(NT):
                sp.wait_ge(Fs[8]["resid"], NT + t + 1)
                sp.dma_start(out[:, t, :], x[:, t, :]).then_inc(s_out, 16)
            sp.wait_ge(s_out, 16 * NT)

        @block.gpsimd
        def _(pool):
            ch = Chain(pool, s_pool)
            pool.dma_start(x[:, :, :], x_in).then_inc(s_x, 16)
            pool.memset(mhalf[:, 0:16], -0.5).then_inc(s_cst, 1)
            ones = mhalf[:, 16:17]
            ch.link(pool.memset(mhalf[:, 16:32], 1.0))

            def block_diagonal(v, e, first):
                if first:
                    pool.memset(vpair[:, :], 0.0).then_inc(s_cst, 1)
                else:
                    ch.link(pool.memset(vpair[:, :], 0.0))
                if first:
                    pool.wait_ge(s_cst, 2)
                for h in range(2):
                    pool.memset(v[h * S:(h + 1) * S, :, :, h, e:e + 1].rearrange("p b j e -> p b (j e)"), 1.0).then_inc(
                        s_cst if first else s_vq, 1)
                    pool.wait_ge(*((s_cst, 3 + h) if first else (s_vq, 1 + h)))

            block_diagonal(Vp, 16, True)

            def rsqrt(out_ap, tmp, src, mul, eps, n, done):
                ch.link(pool.tensor_scalar(tmp, src, mul, eps, ALU.mult, ALU.add))
                pool.tensor_tensor(out_ap, tmp, mhalf[:, 0:n], ALU.pow).then_inc(done, 1)

            def ln(l):
                for t in range(NT):
                    pool.wait_ge(ln_var, NT * l + t + 1)
                    rsqrt(rstd[:, t:t + 1], ve[:, t:t + 1], mv[:, t, 1:2], 1.0, 1e-5, 1, ln_rstd)

            def rms_0(first):
                for q in range(2):
                    pool.wait_ge(A[0]["ss"], first + 4 * q + 4)
                    r = slice(4 * q, 4 * q + 4)
                    rsqrt(ssr[:, first // NT, r], ssv[:, first // NT, r], ss[:, first // NT, r], 1.0 / D, 1e-6, 4,
                          A[0]["rms"])

            def split_weights(l, chunks, first=True, others=True):
                f = Fs[l]

                def one(c, at, down):
                    pool.wait_ge(f["up_hi"], at + 1)
                    pool.tensor_tensor(WL[l][:, c, 0:W2COLS], wring[:, c, 0:W2COLS], WH[l][:, c, 0:W2COLS],
                                       ALU.subtract).then_inc(f["up_lo"], 1)
                    pool.wait_ge(f["up_lo"], at + 1)
                    pool.wait_ge(f["down_hi"], at + 1)
                    pool.tensor_tensor(WL[l][:, c, W2COLS:W1COLS], down, WH[l][:, c, W2COLS:W1COLS],
                                       ALU.subtract).then_inc(f["down_lo"], 1)
                    pool.wait_ge(f["down_lo"], at + 1)

                if first:
                    for c in range(2):
                        one(c, c, down_weights(l, 0, c))
                if others:
                    with pool.Fori(1, chunks // 2) as i:
                        for c in range(2):
                            one(c, i * 2 + c, down_weights(l, i, c))

            def squares_6(buf, first):
                for t in range(NT):
                    pool.wait_ge(A[6]["raw"], first + t + 1)
                    if first + t >= 2:
                        pool.wait_ge(A[6]["sum"], first + t - 1)
                    pool.tensor_tensor(junk[:, t % 2, :], buf[:, t, :], buf[:, t, :], ALU.mult).then_inc(A[6]["sq"], 1)

            ln(0)
            rms_0(0)
            rms_0(NT)
            for l in range(1, NL):
                if l == 5:
                    for t in range(NT):
                        pool.wait_ge(A[4]["dvar"], t + 1)
                        rsqrt(rstd[:, t:t + 1], ve[:, t:t + 1], mv[:, t, 1:2], 1.0, 1e-5, 1, A[4]["drstd"])
                        if t >= 1:
                            pool.wait_ge(ln_var, NT * l + t)
                            rsqrt(rstd[:, t - 1:t], ve[:, t - 1:t], mv[:, t - 1, 1:2], 1.0, 1e-5, 1, ln_rstd)
                    pool.wait_ge(ln_var, NT * l + NT)
                    rsqrt(rstd[:, NT - 1:NT], ve[:, NT - 1:NT], mv[:, NT - 1, 1:2], 1.0, 1e-5, 1, ln_rstd)
                    block_diagonal(Vq, 8, False)
                    split_weights(5, C2, first=False)
                else:
                    ln(l)
                if l == 4:
                    split_weights(5, C2, others=False)
                if l == 1:
                    pool.wait_ge(s_late, 16)
                    pool.wait_ge(A[0]["sc_full"], 4 * NT)
                    src, dst = L("w2f"), w2h
                    for stage in range(3):
                        n = (1 << stage) * D
                        u = src.rearrange("p (a two n) -> p a two n", two=2, n=n)
                        v = dst.rearrange("p (a two n) -> p a two n", two=2, n=n)
                        for k, op in enumerate((ALU.add, ALU.subtract)):
                            pool.tensor_tensor(v[:, :, k, :], u[:, :, 0, :], u[:, :, 1, :], op).then_inc(w2_bf, 1)
                        pool.wait_ge(w2_bf, 2 * stage + 2)
                        src, dst = dst, src
                if l == 3:
                    for k in range(4):
                        pool.wait_ge(Fs[3]["x_hi"], k + 1)
                        q = slice(k * D, (k + 1) * D)
                        pool.tensor_tensor(XL[3][:, :, q], xT[:, :, q], XH[:, :, q], ALU.subtract).then_inc(
                            Fs[3]["x_lo"], 1)
                        pool.wait_ge(Fs[3]["x_lo"], k + 1)
                    split_weights(3, C1, others=False)
                    pool.wait_ge(A[4]["v_done"], B)
                    for h in range(2):
                        r = slice(h * S, (h + 1) * S)
                        for j in range(8):
                            bias = R("bv2")[r, h * (D // 2) + 16 * j:h * (D // 2) + 16 * j + 16]
                            o = Vp[r, :, j, h, 0:16]
                            pool.tensor_tensor(o, o, bias.unsqueeze(1).to_broadcast([S, B, 16]), ALU.add).then_inc(
                                A[4]["v_bias"], 1)
                        pool.wait_ge(A[4]["v_bias"], 8 * h + 8)
                    split_weights(3, C1, first=False)
                if l == 6:
                    squares_6(k_tok, 0)
                    squares_6(q_tok, NT)
            f5, f7 = Fs[5], Fs[7]
            pool.wait_ge(A[6]["pv_full"], NT)

            def split_7(c, at, i, low):
                pool.wait_ge(f7[f"land{c}"], i * 16 + 16)
                for n, (read, written) in enumerate((("up", "up_lo"), ("down", "down_lo"))):
                    w = slice(n * 2 * P, (n + 1) * 2 * P)
                    if low >= 2:
                        pool.wait_ge(f7[read], at * 4 - 4)
                    ch.link(pool.tensor_tensor(W7[0][:, c, w], wring[:, c, w], ones.to_broadcast([P, 2 * P]), ALU.mult))
                    pool.tensor_tensor(W7[1][:, c, w], wring[:, c, w], W7[0][:, c, w], ALU.subtract).then_inc(
                        f5[written], 1)
                    pool.wait_ge(f5[written], at + (C2 + 1))

            for c in range(2):
                split_7(c, c, 0, c)
            with ch.loop(1, E3 // 4, 4) as i:
                for c in range(2):
                    split_7(c, i * 2 + c, i, 2)

        @block.tensor
        def _(pe):
            def mm(o, lhsT, rhs, start=True, stop=True):
                return pe.matmul(o, lhsT, rhs, start=start, stop=stop, skip_group_check=True)

            def rows_by_width(bank, actT, t, w):
                for k in range(KC):
                    ins = mm(ps[:, bank, 0:D], actT[:, k, tok(t)], w[:, k, :], k == 0, k == KC - 1)
                return ins

            def layernorm_T(l):
                for k in range(NT // 2):
                    pe.wait_ge(ln_xn, NT * l + 2 * k + 2)
                    for j in range(2):
                        for c in range(KC):
                            ins = pe.transpose(ps[:, k, j * D + c * P:j * D + (c + 1) * P],
                                               xn[:, 2 * k + j, c * P:(c + 1) * P], ident)
                    ins.then_inc(ln_Tfull, 1)

            def xT_ready(l, tiles):
                pe.wait_ge(ln_xT, (NT // 2) * l + (tiles + 1) // 2)

            def project(a, actT, w, first, l):
                for t in range(NT):
                    if first:
                        xT_ready(l, t + 1)
                    if t >= 4:
                        pe.wait_ge(a["raw"], first + t - 3)
                    elif first:
                        pe.wait_ge(a["v_done"], B - 3 + t)
                    if t == 4 and a is A[0]:
                        pe.wait_ge(s_early, 32)
                    rows_by_width(4 + t % 4, actT, t, kc(w)).then_inc(a["pr_full"], 1)

            def transpose_normed(a, buf, first):
                for t in range(NT):
                    pe.wait_ge(a["normed"], first + t + 1)
                    if first or t >= 4:
                        pe.wait_ge(a["T_done"], first + t - 3)
                    else:
                        pe.wait_ge(a["raw"], 2 * NT - 3 + t)
                    for c in range(KC):
                        ins = pe.transpose(ps[:, 4 + t % 4, c * P:(c + 1) * P], buf[:, t, c * P:(c + 1) * P], ident)
                    ins.then_inc(a["T_full"], 1)

            def values(a, w):
                for b in range(B):
                    if b >= 4:
                        pe.wait_ge(a["v_done"], b - 3)
                    elif a is not A[4]:
                        pe.wait_ge(a["raw"], NT - 3 + b)
                    for h in range(2):
                        for k in range(KC):
                            ins = mm(ps[h * S:(h + 1) * S, 4 + b % 4, 0:D // 2], ctxT[:, k, b * S:(b + 1) * S],
                                     kc(w)[:, k, h * (D // 2):(h + 1) * (D // 2)], k == 0, k == KC - 1)
                    ins.then_inc(a["v_full"], 1)

            def pv(a, t, bank, lhs, V, n, width):
                for j in range(n):
                    for b in range(BT):
                        ins = mm(ps[b * S:(b + 1) * S, bank, j * width:(j + 1) * width], lhs(j, b),
                                 V[:, BT * t + b, j, :, :].rearrange("p h e -> p (h e)"))
                ins.then_inc(a["pv_full"], 1)

            def out_T(a, t, bank):
                pe.wait_ge(a["o_norm"], t + 1)
                for c in range(KC):
                    ins = pe.transpose(ps[:, bank, c * P:(c + 1) * P], oN[:, t % 2, c * P:(c + 1) * P], ident)
                ins.then_inc(a["oT_full"], 1)

            def out_projection(a, t, bank, w):
                pe.wait_ge(a["oT_ready"], t + 1)
                for k in range(KC):
                    ins = mm(ps[:, bank, D:2 * D], oT[:, t % 2, k * P:(k + 1) * P], kc(w)[:, k, :], k == 0, k == KC - 1)
                ins.then_inc(a["o_proj"], 1)

            a = A[0]
            pe.wait_ge(s_first, 32)
            project(a, ctxT, E("wk0"), 0, 0)
            values(a, E("wv0"))
            layernorm_T(0)
            project(a, xT, E("wq0"), NT, 0)
            transpose_normed(a, k_tok, 0)
            transpose_normed(a, q_tok, NT)
            pe.wait_ge(a["T_done"], 2 * NT)
            for s in range(NT + 3):
                t = s
                if t < NT:
                    for j in range(4):
                        if t >= 1:
                            pe.wait_ge(a["sc_free"], 4 * (t - 1) + j + 1)
                        g = slice(32 * j, 32 * j + 32)
                        for c in range(KC):
                            for b in range(BT):
                                ins = mm(ps[b * S:(b + 1) * S, j, c * P:(c + 1) * P],
                                         qT[g, c, t * P + b * S:t * P + (b + 1) * S],
                                         Kp[g, c, BT * t + b, :, :].rearrange("p h s -> p (h s)"))
                        ins.then_inc(a["sc_full"], 1)
                t = s - 3
                if 0 <= t:
                    if t >= 1:
                        pe.wait_ge(a["resid"], t)
                    out_T(a, t, 7)
                t = s - 1
                if 0 <= t < NT:
                    pe.wait_ge(a["p_ready"], 4 * t + 4)
                    Pt = probs[:, t % 2, 0:1024].rearrange("p (j n) -> p j n", j=8)
                    if t >= 1:
                        pe.wait_ge(a["pT_act"], t)
                    for n in range(8):
                        if n == 4 and t >= 1:
                            pe.wait_ge(a["pT_dve"], t)
                        ins = pe.transpose(ps[:, 4 + n // 4, (n % 4) * P:(n % 4 + 1) * P], Pt[:, n, :], ident)
                        if n % 4 == 3:
                            ins.then_inc(a["pT_full"], 1)
                t = s - 3
                if 0 <= t:
                    out_projection(a, t, 7, E("wo0"))
                t = s - 2
                if 0 <= t < NT:
                    pe.wait_ge(a["pT_act"], t + 1)
                    pe.wait_ge(a["pT_dve"], t + 1)
                    if t >= 1:
                        pe.wait_ge(a["o_norm"], t)
                    PT = probs[:, t % 2, 1024:2048].rearrange("p (j c n) -> p j c n", j=4, c=KC)
                    pv(a, t, 6, lambda n, b: PT[:, n % 4, n // 4, b * S:(b + 1) * S], Vp, 8, 34)
            def gates_T(l, e):
                f = Fs[l]
                pe.wait_ge(f["gates"], 1)
                gv = g3[:, 0:NT * 3 * e].rearrange("p (t n) -> p t n", t=NT)
                for t in range(NT):
                    ins = pe.transpose(ps[:, 7 if l == 7 else 1, :].bitcast(BF16)[0:3 * e, tok(t)], gv[:, t, :], identb[:, :])
                ins.then_inc(f["gT_full"], 1)
                pe.wait_ge(f["gT_ready"], 1)

            def logits(l, w, e):
                for t in range(NT):
                    xT_ready(l, t + 1)
                    for k in range(KC):
                        ins = mm(ps[:, 0, t * e:(t + 1) * e], xT[:, k, tok(t)], w[:, k, :], k == 0, k == KC - 1)
                ins.then_inc(Fs[l]["logits"], 1)

            def up2(o, w, half):
                for k in range(KC):
                    ins = mm(o, w[:, k, :], xT[:, k, half * HALF:(half + 1) * HALF], k == 0, k == KC - 1)
                return ins

            def down_tokens(hid, half, w, first):
                for q in range(4):
                    t = 4 * half + q
                    ins = mm(ps[:, t // 2, (t % 2) * D:(t % 2 + 1) * D], hid[:, q * P:(q + 1) * P], w,
                             first and t % 2 == 0, True)
                return ins

            def at_least(sm, n, low):
                if low >= 1:
                    pe.wait_ge(sm, n)

            def run_units(units, up, down):
                groups = units // 4

                def group(base, low, last, first):
                    for k in range(4):
                        if not (last and k == 3):
                            up(base + (k + 1), low + k + 1, (k + 1) % 4)
                        down(base + k, low + k, k, first and k < 2)
                up(0, 0, 0)
                group(0, 0, groups == 1, True)
                if groups > 2:
                    with pe.Fori(1, groups - 1) as i:
                        group(i * 4, 4, False, False)
                if groups > 1:
                    group(4 * (groups - 1), 4 * (groups - 1), True, False)

            f = Fs[1]
            pe.wait_ge(s_late, 16)
            pe.wait_ge(s_misc, 16 * 6)
            layernorm_T(1)
            logits(1, kc(L("wr0")), E0)
            gates_T(1, E0)
            a0 = L("A0").rearrange("p (k n) -> p k n", k=KC)
            b0 = L("B0").rearrange("p (k n) -> p k n", n=D)

            def up_1(n, low, k):
                c, half = n // 2, n % 2
                at_least(f["act"], n - 1, low - 1)
                up2(ps[:, 4 + 2 * (n % 2), :], a0[:, :, c * P:(c + 1) * P], half).then_inc(f["up"], 1)
                at_least(f["h"], n - 1, low - 1)
                mm(ps[:, 5 + 2 * (n % 2), :], sel0[:, c * P:(c + 1) * P], gT[0:3 * E0, half * HALF:(half + 1) * HALF]
                   ).then_inc(f["cw"], 1)

            def down_1(n, low, k, first):
                pe.wait_ge(f["h"], n + 1)
                down_tokens(sbuf_h[:, n % 2, :], n % 2, b0[:, n // 2, :], first).then_inc(f["down"], 1)

            up_1(0, 0, 0)
            for n in range(FF[1]):
                if n + 1 < FF[1]:
                    up_1(n + 1, n + 1, 0)
                down_1(n, n, 0, n < 2)
            layernorm_T(2)
            for t in range(NT):
                xT_ready(2, t + 1)
                for b in range(BT):
                    for k in range(KC):
                        q = slice(t * P + b * S, t * P + (b + 1) * S)
                        ins = mm(ps[b * S:(b + 1) * S, 4 + t // 4, (t % 4) * S:(t % 4 + 1) * S], xT[:, k, q],
                                 ctxT[:, k, q], k == 0, k == KC - 1)
                if t % 4 == 3:
                    ins.then_inc(a2["sc_full"], 1)
            pe.wait_ge(a2["shift"], 2)
            for s in range(NT + 1):
                if s < NT:
                    pe.wait_ge(a2["p_ready"], 2 * (s // 4) + 2)
                    if s >= 2:
                        pe.wait_ge(a2["pT_ready"], s - 1)
                    pe.transpose(ps[:, 6 + s % 2, 0:P], probs[:, 0, tok(s)], ident).then_inc(a2["pT_full"], 1)
                t = s - 1
                if t >= 0:
                    pe.wait_ge(a2["pT_ready"], t + 1)
                    if t >= 2:
                        pe.wait_ge(a2["resid"], t - 1)
                    mm(ps[:, 4 + t % 2, 0:D], probs[:, 1, (t % 2) * P:(t % 2 + 1) * P], ctx[:, t, :]
                       ).then_inc(a2["pv_full"], 1)
            f3 = Fs[3]
            layernorm_T(3)
            logits(3, kc(L("gate1")), E1 + 1)
            a = A[4]

            def projection_T(w, actT):
                for half in range(2):
                    for c in range(KC):
                        for k in range(KC):
                            ins = mm(ps[:, 4 + 2 * half + c, :], w[:, k, c * P:(c + 1) * P],
                                     actT[:, k, half * HALF:(half + 1) * HALF], k == 0, k == KC - 1)
                        ins.then_inc(a["kq_full"], 1)

            projection_T(kc(L("wk2")), ctxT)
            pe.wait_ge(a["kq_done"], 4)
            values(a, L("wv2"))
            pe.wait_ge(a["v_done"], B)
            pe.wait_ge(w2_bf, 6)
            for n in range(4):
                mm(ps[:, 4 + n, :], L("had"), w2h[:, n * 512:(n + 1) * 512]).then_inc(w2_mm, 1)
            gates_T(3, EP1)

            def gate_up(l, o, c, g, half):
                w = [W[l][:, c, 0:W2COLS].rearrange("p (k g n) -> p k g n", k=KC, g=2)[:, :, g, :] for W in (WH, WL)]
                for n, (wi, xs) in enumerate(((w[1], XH), (w[0], XL[l]), (w[0], XH))):
                    for k in range(KC):
                        ins = mm(o, wi[:, k, :], xs[:, k, half * HALF:(half + 1) * HALF], n == 0 and k == 0,
                                 n == 2 and k == KC - 1)
                return ins

            def down_T(l, n, k, first):
                f, c, half = Fs[l], k // 2, k % 2
                pe.wait_ge(f["h_lo"], n + 1)
                if half == 0:
                    pe.wait_ge(f["down_lo"], n // 2 + 1)
                for d in range(KC):
                    w = [W[l][:, c, W2COLS + d * P:W2COLS + (d + 1) * P] for W in (WH, WL)]
                    for m, (wi, hs) in enumerate(((w[1], HH[l]), (w[0], HL), (w[0], HH[l]))):
                        ins = mm(ps[:, 2 * half + d, :], wi, hs[:, half, :], first and m == 0, m == 2)
                ins.then_inc(f["down"], 1)

            def back_to_tokens(l):
                for t in range(NT):
                    if t % 4 == 0:
                        pe.wait_ge(Fs[l]["yT"], 2 * (t // 4) + 2)
                    for d in range(KC):
                        ins = pe.transpose(ps[:, t // 2, (t % 2) * D + d * P:(t % 2) * D + (d + 1) * P],
                                           yT[:, d, tok(t)], ident)
                    if t % 2:
                        ins.then_inc(Fs[l]["y"], 1)

            def up_3(n, low, k):
                c, half = k // 2, k % 2
                if half == 0:
                    pe.wait_ge(f3["up_lo"], n // 2 + 1)
                at_least(f3["h"], n - 1, low - 1)
                gate_up(3, ps[:, 4 + (3 * k) % 4, :], c, 0, half)
                at_least(f3["act"], n, low)
                gate_up(3, ps[:, 4 + (3 * k + 1) % 4, :], c, 1, half).then_inc(f3["up"], 1)
                at_least(f3["mid"], n, low)
                if isinstance(n, int):
                    chunk = sel1[:, (n // 2) * P:(n // 2 + 1) * P]
                else:
                    chunk = sel1[:, bass.ds((n - k) * (P // 2) + c * P, P)]
                mm(ps[:, 4 + (3 * k + 2) % 4, :], chunk, gT[0:3 * EP1, half * HALF:(half + 1) * HALF]
                   ).then_inc(f3["cw"], 1)

            def down_3(n, low, k, first):
                down_T(3, n, k, first)

            pe.wait_ge(f3["x_lo"], 4)
            pe.wait_ge(w2_ev, 4)
            run_units(FF[3], up_3, down_3)
            back_to_tokens(3)
            layernorm_T(4)
            xT_ready(4, NT)
            projection_T(kc(L("wq2")), xT)
            for s in range(NT + 2):
                t = s
                if t < NT:
                    pe.wait_ge(a["k_ready"], 8)
                    pe.wait_ge(a["q_ready"], 2 * (t // 4) + 2)
                    if t >= 1:
                        pe.wait_ge(a["sc_free"], t)
                    for c in range(KC):
                        for b in range(BT):
                            for j in range(4):
                                g = slice(32 * j, 32 * j + 32)
                                ins = mm(ps[:, j, c * P + b * S:c * P + (b + 1) * S],
                                         Kp[g, c, BT * t + b, :, :].rearrange("p h s -> p (h s)"),
                                         qT[g, c, t * P + b * S:t * P + (b + 1) * S])
                    ins.then_inc(a["sc_full"], 1)
                t = s - 2
                if t >= 0:
                    if t == 0:
                        pe.wait_ge(a["kq_done"], 8)
                    if t >= 2:
                        pe.wait_ge(a["dvar"], t - 1)
                    out_T(a, t, 6 + t % 2)
                t = s - 1
                if 0 <= t < NT:
                    pe.wait_ge(a["p_ready"], t + 1)
                    if t >= 2:
                        pe.wait_ge(a["o_norm"], t - 1)
                    if t == 0:
                        pe.wait_ge(a["kq_done"], 6)
                    PT = probs[:, t % 2, 0:1024].rearrange("p (j c n) -> p j c n", j=4, c=KC)
                    pv(a, t, 4 + t % 2, lambda n, b: PT[:, n % 4, n // 4, b * S:(b + 1) * S], Vp, 8, 34)
                t = s - 2
                if t >= 0:
                    out_projection(a, t, 6 + t % 2, L("wo2"))
            f5 = Fs[5]
            layernorm_T(5)
            pe.wait_ge(f5["x_lo"], 4)

            def up_5(n, low, k):
                c, half = k // 2, k % 2
                if half == 0:
                    pe.wait_ge(f5["up_lo"], n // 2 + 1)
                at_least(f5["act"], n - 1, low - 1)
                gate_up(5, ps[:, 4 + 2 * (k % 2), :], c, 0, half)
                at_least(f5["h"], n - 1, low - 1)
                gate_up(5, ps[:, 5 + 2 * (k % 2), :], c, 1, half).then_inc(f5["up"], 1)

            def down_5(n, low, k, first):
                down_T(5, n, k, first)

            run_units(FF[5], up_5, down_5)
            back_to_tokens(5)
            a = A[6]
            project(a, ctxT, L("wk3"), 0, 6)
            values(a, L("wv3"))
            layernorm_T(6)
            project(a, xT, L("wq3"), NT, 6)
            transpose_normed(a, k_tok, 0)
            transpose_normed(a, q_tok, NT)
            pe.wait_ge(a["masked"], 1)
            pe.wait_ge(a["T_done"], 2 * NT)
            for s in range(NT + 1):
                t = s
                if t == NT // 2:
                    pe.wait_ge(A[4]["k_ready"], 8 + 1)
                if t < NT:
                    for j in range(4):
                        if t >= 1:
                            pe.wait_ge(a["p_ready"], 4 * (t - 1) + j + 1)
                        g = slice(32 * j, 32 * j + 32)
                        for c in range(KC):
                            for u in range(2):
                                for b in range(BT):
                                    at = (2 * c + u) * P + b * S
                                    for n, (ki, qi) in enumerate(((0, 1), (1, 0), (0, 0))):
                                        ins = mm(ps[:, j, at:at + S],
                                                 Kq[g, ki, c, BT * t + b, 2 * u:2 * u + 2, :].rearrange("p m s -> p (m s)"),
                                                 q16[g, qi, c, t * P + b * S:t * P + (b + 1) * S], n == 0, n == 2)
                        ins.then_inc(a["sc_full"], 1)
                t = s - 1
                if t >= 0:
                    pe.wait_ge(a["p_ready"], 4 * t + 4)
                    if t >= 2:
                        pe.wait_ge(a["o_norm"], t - 1)
                    PT = probs[:, t % 2, :].rearrange("p (j c u n) -> p j c u n", j=4, c=KC, u=2)
                    pv(a, t, 4 + t % 2,
                       lambda n, b: PT[:, (n % 8) // 2, n // 8, n % 2, b * S:(b + 1) * S], Vq, 16, 18)
            f7, f8 = Fs[7], Fs[8]
            layernorm_T(7)
            logits(7, kc(L("gate3")), E3)
            fc1 = kc(L("fc1"))
            for half in range(2):
                for k in range(KC):
                    ins = mm(ps[:, 2 + half, :], fc1[:, k, :], xT[:, k, half * HALF:(half + 1) * HALF],
                             k == 0, k == KC - 1)
                ins.then_inc(s_lat, 1)
            u3 = L("up3").rearrange("p (c k n) -> p c k n", c=C3S, k=KC)
            d3 = L("down3").rearrange("p (c n) -> p c n", c=C3S)

            def up_8(n):
                if n >= 4:
                    pe.wait_ge(f8["act"], n - 3)
                up2(ps[:, 4 + n % 4, :], u3[:, n // 2, :, :], n % 2).then_inc(f8["up"], 1)

            up_8(0)
            up_8(1)
            pe.wait_ge(f7["e"], 1)
            pe.wait_ge(f5["x_lo"], 4 + 2)
            for n in range(FF[8]):
                if n + 2 < FF[8]:
                    up_8(n + 2)
                pe.wait_ge(f8["h"], n + 1)
                down_tokens(sbuf_h[:, n % 2, :], n % 2, d3[:, n // 2, :], n < 2).then_inc(f8["down"], 1)
            pe.wait_ge(f8["act"], FF[8])
            gates_T(7, E3)
            pe.wait_ge(s_sel3, 16)
            pe.wait_ge(f8["resid"], NT)

            def up_7(n, low, k):
                c, e, half = k // 4, k // 2 % 2, k % 2
                if k % 4 == 0:
                    pe.wait_ge(f5["up_lo"], n // 4 + (C2 + 1) if isinstance(n, int) else (n - k) // 4 + (C2 + c + 1))
                at_least(f7["act"], n - 3, low - 3)
                for m, (w, xs) in enumerate(((1, 0), (0, 1), (0, 0))):
                    ins = mm(ps[:, 4 + k % 4, :], W7[w][:, c, e * P:(e + 1) * P],
                             qT_r[:, xs, half * HALF:(half + 1) * HALF], m == 0, m == 2)
                ins.then_inc(f7["up"], 1)
                at_least(f7["h"], n - 1, low - 1)
                if isinstance(n, int):
                    chunk = sel3[:, (n // 2) * P:(n // 2 + 1) * P]
                else:
                    chunk = sel3[:, bass.ds((n - k) * (P // 2) + (k // 2) * P, P)]
                mm(ps[:, 2 + k % 2, :], chunk, gT[0:3 * E3, half * HALF:(half + 1) * HALF]).then_inc(f7["cw"], 1)

            def down_7(n, low, k, first):
                c, e, half = k // 4, k // 2 % 2, k % 2
                if k % 4 == 0:
                    pe.wait_ge(f5["down_lo"], n // 4 + (C2 + 1) if isinstance(n, int) else (n - k) // 4 + (C2 + c + 1))
                pe.wait_ge(f5["h_lo"], n + (FF[5] + 1))
                for m, (w, hs) in enumerate(((1, HH7), (0, H7[1]), (0, HH7))):
                    ins = mm(ps[:, half, :], W7[w][:, c, (2 + e) * P:(3 + e) * P], hs[:, k % 4, :], first and m == 0, m == 2)
                ins.then_inc(f7["down"], 1)

            def group_7(base, low, last, first):
                for k in range(8):
                    if not (last and k >= 5):
                        up_7(base + (k + 3), low + k + 3, (k + 3) % 8)
                    down_7(base + k, low + k, k, first and k < 2)

            for n in range(3):
                up_7(n, n, n)
            group_7(0, 0, False, True)
            with pe.Fori(1, FF[7] // 8 - 1) as i:
                group_7(i * 8, 8, False, False)
            group_7(FF[7] - 8, FF[7] - 8, True, False)
            pe.wait_ge(s_latE, 4)
            for t in range(NT):
                ins = mm(ps[:, t // 2, (t % 2) * D:(t % 2 + 1) * D], qT[:, 1, tok(t)], L("fc2"), t % 2 == 0, True)
                if t % 2:
                    ins.then_inc(f8["down"], 1)

        @block.scalar
        def _(act):
            def copy(o, i):
                return nc.scalar.activation(o, i, ACT.Copy)

            def layernorm_evac(l):
                for k in range(NT // 2):
                    act.wait_ge(ln_Tfull, (NT // 2) * l + k + 1)
                    copy(xT[:, :, 2 * k * P:2 * (k + 1) * P].rearrange("p c (t n) -> p t c n", t=2),
                         ps[:, k, :].rearrange("p (t c n) -> p t c n", t=2, c=KC)).then_inc(ln_xT, 1)

            def squares(a, buf, first):
                for t in range(NT):
                    act.wait_ge(a["raw"], first + t + 1)
                    if first + t >= 2:
                        act.wait_ge(a["ss"], first + t - 1)
                    nc.scalar.activation(junk[:, t % 2, :], buf[:, t, :], ACT.Square,
                                         accum_out=ss[:, first // NT, t:t + 1]).then_inc(a["ss"], 1)

            def by_tokens(a, buf, first):
                for t in range(NT):
                    act.wait_ge(a["pr_full"], first + t + 1)
                    copy(buf[:, t, :], ps[:, 4 + t % 4, 0:D]).then_inc(a["raw"], 1)
                for q in range(2):
                    act.wait_ge(a["ss"], first // 4 + q + 1)
                    nc.scalar.activation(ssr[:, 4 * q:4 * q + 4, :], ssv[:, 4 * q:4 * q + 4, :], ACT.Sqrt
                                         ).then_inc(a["rms"], 1)

            def keys_out(a):
                for t in range(NT):
                    act.wait_ge(a["T_full"], t + 1)
                    src = ps[:, 4 + t % 4, 0:D].rearrange("p (c b s) -> p c b s", c=KC, b=BT)
                    for h in range(2):
                        ins = nc.scalar.activation(Kp[:, :, BT * t:BT * t + BT, h, :], src, ACT.Copy,
                                                   scale=E("pair")[:, h:h + 1])
                    ins.then_inc(a["T_done"], 1)

            def queries_out(a):
                for t in range(NT):
                    act.wait_ge(a["T_full"], NT + t + 1)
                    copy(qT[:, :, tok(t)], ps[:, 4 + t % 4, 0:D].rearrange("p (c n) -> p c n", c=KC)
                         ).then_inc(a["T_done"], 1)

            def out_T_evac(a, t, bank):
                act.wait_ge(a["oT_full"], t + 1)
                copy(oT[:, t % 2, :], ps[:, bank, 0:D]).then_inc(a["oT_ready"], 1)

            a = A[0]
            act.wait_ge(s_rows, 16)
            nc.scalar.activation(tg[:, :], R("gates"), ACT.Tanh).then_inc(s_tanh, 1)
            act.wait_ge(s_early, 32)
            squares(a, k_tok, 0)
            layernorm_evac(0)
            squares(a, q_tok, NT)
            keys_out(a)
            queries_out(a)
            for s in range(NT + 3):
                t = s
                if t < NT:
                    for j in range(4):
                        act.wait_ge(a["sc_free"], 4 * t + j + 1)
                        v = probs[:, t % 2, j * D:(j + 1) * D]
                        nc.scalar.activation(v, v, ACT.Exp, scale=0.25).then_inc(a["p_ready"], 1)
                t = s - 1
                if 0 <= t < NT:
                    act.wait_ge(a["pT_full"], 2 * t + 1)
                    if t >= 2:
                        act.wait_ge(a["pv_full"], t - 1)
                    copy(probs[:, t % 2, 1024:1536], ps[:, 4, :]).then_inc(a["pT_act"], 1)
                t = s - 3
                if t >= 0:
                    out_T_evac(a, t, 7)
            def gates_evac(l, e):
                f = Fs[l]
                act.wait_ge(f["gT_full"], 1)
                copy(gT[0:3 * e, :], ps[:, 7 if l == 7 else 1, :].bitcast(BF16)[0:3 * e, :]).then_inc(f["gT_ready"], 1)

            def up_hi(l, c, slot):
                act.wait_ge(Fs[l][f"land{slot}"], (c - slot) * 8 + 16)
                copy(WH[l][:, slot, 0:W2COLS], wring[:, slot, 0:W2COLS]).then_inc(Fs[l]["up_hi"], 1)

            def down_hi(l, i, slot):
                copy(WH[l][:, slot, W2COLS:W1COLS], down_weights(l, i, slot)).then_inc(Fs[l]["down_hi"], 1)

            def run_split_units(l, units, bank):
                f = Fs[l]

                def group(i, first, last):
                    for k in range(4):
                        n = i * 4 + k
                        act.wait_ge(f["up"], n + 1)
                        if not (first and k < 2):
                            act.wait_ge(f["h"], n - 1)
                        nc.scalar.activation(sbuf_s[:, k % 2, :], ps[:, bank(k), :], ACT.Silu).then_inc(f["act"], 1)
                        if k == 0 and not first:
                            up_hi(l, i * 2 + 1, 1)
                        if k == 2 and not last:
                            up_hi(l, i * 2 + 2, 0)
                        if k == 1 and not first:
                            act.wait_ge(f["down"], n - 1)
                            down_hi(l, i, 1)
                        if k == 3 and not last:
                            act.wait_ge(f["down"], n - 1)
                            down_hi(l, i + 1, 0)
                        act.wait_ge(f["h"], n + 1)
                        copy(HH[l][:, k % 2, :], sbuf_h[:, k % 2, :]).then_inc(f["h_hi"], 1)

                group(0, True, False)
                with act.Fori(1, units // 4 - 1) as i:
                    group(i, False, False)
                group(units // 4 - 1, False, True)
                for half in range(2):
                    act.wait_ge(f["down"], units - 1 + half)
                    for d in range(KC):
                        copy(yT[:, d, half * HALF:(half + 1) * HALF], ps[:, 2 * half + d, :]).then_inc(f["yT"], 1)

            f = Fs[1]
            layernorm_evac(1)
            act.wait_ge(f["lread"], 1)
            nc.scalar.activation(lb[:, 0:NT * E0], la[:, 0:NT * E0], ACT.Exp).then_inc(f["e"], 1)
            gates_evac(1, E0)
            for n in range(FF[1]):
                act.wait_ge(f["up"], n + 1)
                if n >= 2:
                    act.wait_ge(f["h"], n - 1)
                copy(sbuf_s[:, n % 2, :], ps[:, 4 + 2 * (n % 2), :]).then_inc(f["act"], 1)
            layernorm_evac(2)
            pd = probs[:, 0, 0:NT * P].rearrange("p (t n) -> p t n", t=NT)
            sv = cr[:, :].rearrange("p (t n) -> p t n", t=NT)
            for half in range(2):
                act.wait_ge(a2["shift"], half + 1)
                for b in range(BT):
                    r, ts = slice(b * S, (b + 1) * S), slice(4 * half, 4 * half + 4)
                    nc.scalar.activation(pd[r, ts, b * S:(b + 1) * S], sv[r, ts, :], ACT.Exp,
                                         scale=D ** -0.5).then_inc(a2["p_ready"], 1)
            for t in range(NT):
                act.wait_ge(a2["pT_full"], t + 1)
                if t >= 2:
                    act.wait_ge(a2["pv_full"], t - 1)
                copy(probs[:, 1, (t % 2) * P:(t % 2 + 1) * P], ps[:, 6 + t % 2, 0:P]).then_inc(a2["pT_ready"], 1)
            f = Fs[3]
            layernorm_evac(3)
            lg17 = lg[:, 0:NT * (E1 + 1)].rearrange("p (t e) -> p t e", t=NT)
            act.wait_ge(f["lread"], 1)
            nc.scalar.activation(rk[:, 0:NT], lg17[:, :, E1], ACT.Exp, scale=-1.0).then_inc(f["e"], 1)
            act.wait_ge(f["lread"], 2)
            nc.scalar.activation(lb[:, 0:NT * E1], lb[:, 0:NT * E1], ACT.Exp).then_inc(f["e"], 1)
            for k in range(4):
                q = slice(k * D, (k + 1) * D)
                copy(XH[:, :, q], xT[:, :, q]).then_inc(f["x_hi"], 1)
            for c in range(2):
                up_hi(3, c, c)
                down_hi(3, 0, c)
            a = A[4]

            def projection_out(n0, bias, dst):
                for g in range(4):
                    half, c = g // 2, g % 2
                    act.wait_ge(a["kq_full"], n0 + g + 1)
                    nc.scalar.activation(dst[:, c, half * HALF:(half + 1) * HALF], ps[:, 4 + g, :], ACT.Identity,
                                         bias=bias[:, c:c + 1]).then_inc(a["kq_done"], 1)

            act.wait_ge(f["x_lo"], 4)
            projection_out(0, L("bqk2")[:, KC:2 * KC], xT)
            for b in range(B):
                act.wait_ge(a["v_full"], b + 1)
                for h in range(2):
                    r = slice(h * S, (h + 1) * S)
                    ins = copy(Vp[r, b, :, h, 0:16], ps[r, 4 + b % 4, 0:D // 2].rearrange("p (j e) -> p j e", e=16))
                ins.then_inc(a["v_done"], 1)
            for n in range(4):
                act.wait_ge(w2_mm, n + 1)
                nc.scalar.activation(L("w2f")[:, n * 512:(n + 1) * 512], ps[:, 4 + n, :], ACT.Copy,
                                     scale=1.0 / 32).then_inc(w2_ev, 1)
            gates_evac(3, EP1)
            run_split_units(3, FF[3], lambda k: 4 + (3 * k) % 4)
            a = A[4]
            act.wait_ge(s_piece, STEPS * PIECES + 1)
            for g in range(4):
                c, half = g // 2, g % 2
                for h in range(2):
                    nc.scalar.activation(Kp[:, c, half * 8:half * 8 + 8, h, :],
                                         xT[:, c, half * HALF:(half + 1) * HALF].rearrange("p (b s) -> p b s", s=S),
                                         ACT.Copy, scale=E("pair")[:, h:h + 1]).then_inc(a["k_ready"], 1)
            act.wait_ge(a["k_ready"], 8)
            for c in range(2):
                up_hi(5, c, c)
                down_hi(5, 0, c)
            layernorm_evac(4)
            projection_out(4, L("bqk2")[:, 0:KC], qT)
            for s in range(NT + 2):
                t = s
                if t < NT:
                    act.wait_ge(a["sc_free"], t + 1)
                    v = probs[:, t % 2, 0:1024]
                    nc.scalar.activation(v, v, ACT.Exp, scale=0.25).then_inc(a["p_ready"], 1)
                t = s - 2
                if t >= 0:
                    out_T_evac(a, t, 6 + t % 2)
            for k in range(4):
                act.wait_ge(ln_Tfull, (NT // 2) * 5 + k + 1)
                copy(XH[:, :, 2 * k * P:2 * (k + 1) * P].rearrange("p c (t n) -> p t c n", t=2),
                     ps[:, k, :].rearrange("p (t c n) -> p t c n", t=2, c=KC)).then_inc(Fs[5]["x_hi"], 1)
                act.wait_ge(Fs[5]["x_hi"], k + 1)
                act.sem_inc(ln_xT, 1)
            run_split_units(5, FF[5], lambda k: 4 + 2 * (k % 2))
            a = A[6]
            by_tokens(a, k_tok, 0)
            layernorm_evac(6)
            by_tokens(a, q_tok, NT)
            for t in range(2 * NT):
                if t == NT + 4:
                    act.wait_ge(a["T_done"], NT)
                    mask_keys(1, lambda o, i, scale: nc.scalar.activation(o, i, ACT.Copy, scale=scale), A[4]["k_ready"])
                act.wait_ge(a["T_full"], t + 1)
                copy((k16 if t < NT else q16)[:, 0, :, tok(t % NT)],
                     ps[:, 4 + t % 4, 0:D].rearrange("p (c n) -> p c n", c=KC)).then_inc(a["hi"], 1)
            for t in range(NT):
                for j in range(4):
                    act.wait_ge(a["sc_full"], 4 * t + j + 1)
                    if t >= 2:
                        act.wait_ge(a["pv_full"], t - 1)
                    nc.scalar.activation(probs[:, t % 2, j * 512:(j + 1) * 512], ps[:, j, :], ACT.Exp,
                                         scale=8 ** -0.5 / LIFT ** 2).then_inc(a["p_ready"], 1)
            f = Fs[7]
            layernorm_evac(7)
            act.wait_ge(f["logits"], 1)
            nc.scalar.activation(lb[:, :], ps[:, 0, 0:NT * E3], ACT.Exp, scale=-1.0).then_inc(f["e"], 1)
            for half in range(2):
                act.wait_ge(s_lat, half + 1)
                copy(qT_r[:, 0, half * HALF:(half + 1) * HALF], ps[:, 2 + half, :]).then_inc(s_latE, 1)
            f8 = Fs[8]
            for n in range(FF[8]):
                act.wait_ge(f8["up"], n + 1)
                if n >= 2:
                    act.wait_ge(f8["h"], n - 1)
                nc.scalar.activation(sbuf_s[:, n % 2, :], ps[:, 4 + n % 4, :], ACT.Relu).then_inc(f8["act"], 1)
                act.wait_ge(f8["act"], n + 1)
                if n >= 2:
                    act.wait_ge(f8["down"], n - 1)
                nc.scalar.activation(sbuf_h[:, n % 2, :], sbuf_s[:, n % 2, :], ACT.Square).then_inc(f8["h"], 1)
            act.wait_ge(f8["h"], FF[8])
            gates_evac(7, E3)

            def hidden_hi_7(n, k):
                act.wait_ge(f["h"], n + 1)
                copy(HH7[:, k, :], H7[0][:, k, :]).then_inc(Fs[5]["h_hi"], 1)

            def group_7(base, first):
                for k in range(4):
                    n = base + k
                    act.wait_ge(f["up"], n + 1)
                    if not (first and k < 2):
                        act.wait_ge(f["sq"], n - 1)
                    nc.scalar.activation(sbuf_s[:, k % 2, :], ps[:, 4 + k, :], ACT.Relu).then_inc(f["act"], 1)
                    act.wait_ge(f["act"], n + 1)
                    nc.scalar.activation(sbuf_t[:, k % 2, :], sbuf_s[:, k % 2, :], ACT.Square).then_inc(f["sq"], 1)
                    if not (first and k < 1):
                        if not first:
                            act.wait_ge(f["down"], n - 4)
                        hidden_hi_7(base + (k - 1), (k - 1) % 4)

            group_7(0, True)
            with act.Fori(1, FF[7] // 4) as i:
                group_7(i * 4, False)
            hidden_hi_7(FF[7] - 1, 3)
            act.wait_ge(f["down"], FF[7])
            for half in range(2):
                copy(qT[:, 1, half * HALF:(half + 1) * HALF], ps[:, half, :]).then_inc(s_latE, 1)

        @block.vector
        def _(v):
            ch = Chain(v, s_dve)
            link = ch.link

            def ln_stats(l, t):
                link(v.bn_stats(st[:, t, :], x[:, t, :]))
                v.bn_aggr(mv[:, t, :], st[:, t, :]).then_inc(ln_var, 1)

            def ln_norm(l, t):
                v.wait_ge(ln_rstd, NT * l + t + 1)
                v.tensor_scalar(xn[:, t, :], x[:, t, :], mv[:, t, 0:1], rstd[:, t:t + 1], ALU.subtract,
                                ALU.mult).then_inc(ln_xn, 1)

            def biased(a, buf, first, bias):
                for t in range(NT):
                    v.wait_ge(a["pr_full"], first + t + 1)
                    v.tensor_tensor(buf[:, t, :], ps[:, 4 + t % 4, 0:D], bias, ALU.add).then_inc(a["raw"], 1)

            def normalize_0(a, buf, first, gain):
                for t in range(NT):
                    v.wait_ge(a["rms"], first // 4 + t // 4 + 1)
                    v.scalar_tensor_tensor(out=buf[:, t, :], in0=buf[:, t, :], scalar=ssr[:, first // NT, t:t + 1],
                                           in1=gain, op0=ALU.mult, op1=ALU.mult).then_inc(a["normed"], 1)

            def sums_6(a, first):
                for q in range(2):
                    for t in range(4 * q, 4 * q + 4):
                        v.wait_ge(a["sq"], first + t + 1)
                        v.tensor_reduce(ss[:, t, :], junk[:, t % 2, :].rearrange("p (h e) -> p h e", e=8), AX.X,
                                        ALU.add).then_inc(a["sum"], 1)
                    v.wait_ge(a["sum"], first + 4 * q + 4)
                    v.tensor_scalar(ssv[:, 4 * q:4 * q + 4, :], ss[:, 4 * q:4 * q + 4, :], 1.0 / 8, 1e-6, ALU.mult,
                                    ALU.add).then_inc(a["ss"], 1)

            def normalize_6(a, buf, first):
                for q in range(2):
                    r, m, y = (b_[:, 4 * q:4 * q + 4, :] for b_ in (ss, ssv, ssr))
                    v.wait_ge(a["rms"], first // 4 + q + 1)
                    link(v.reciprocal(y, y))
                    link(v.tensor_tensor(r, y, y, ALU.mult))
                    link(v.tensor_tensor(r, r, m, ALU.mult))
                    link(v.tensor_scalar(r, r, -0.5 * LIFT, 1.5 * LIFT, ALU.mult, ALU.add))
                    link(v.tensor_tensor(y, y, r, ALU.mult))
                    for t in range(4 * q, 4 * q + 4):
                        o = buf[:, t, :].rearrange("p (h e) -> p h e", e=8)
                        v.tensor_tensor(o, o, ssr[:, t, :].unsqueeze(2).to_broadcast([P, 32, 8]),
                                        ALU.mult).then_inc(a["normed"], 1)

            def values(a, V, e, bias):
                for b in range(B):
                    v.wait_ge(a["v_full"], b + 1)
                    for h in range(2):
                        r = slice(h * S, (h + 1) * S)
                        src = ps[r, 4 + b % 4, 0:D // 2].rearrange("p (j e) -> p j e", e=e)
                        dst = V[r, b, :, h, 0:e]
                        if bias is None:
                            ins = v.tensor_copy(dst, src)
                        else:
                            ins = v.tensor_tensor(dst, src,
                                                  bias[r, h * (D // 2):(h + 1) * (D // 2)].rearrange("p (j e) -> p j e", e=e),
                                                  ALU.add)
                    ins.then_inc(a["v_done"], 1)

            def gate(l):
                return tg[:, (l // 2 if l % 2 == 0 else 4 + l // 2):][:, 0:1]

            def clean(ap, n):
                c, m = cr[:, 0:n], cm[:, 0:n]
                link(v.tensor_scalar(c, ap, 0.0, 1e4, ALU.max, ALU.min))
                v.tensor_scalar(m, ap, 0.0, 0.0, ALU.mult, ALU.not_equal)
                link(v.scalar_tensor_tensor(out=c, in0=ap, scalar=0.0, in1=c, op0=ALU.min, op1=ALU.add))
                link(v.tensor_scalar(c, c, -1e4, None, ALU.max))
                return v.copy_predicated(ap, m, c)

            def head_norm(a, t, bank, heads, e, eps):
                par = t % 2
                o = ps[:, bank, 0:heads * (e + 1)].rearrange("p (h e) -> p h e", e=e + 1)
                r = rden[:, par, 0:heads]
                if eps:
                    d = den2[:, par, 0:heads]
                    link(v.tensor_copy(d, o[:, :, e]))
                    link(v.scalar_tensor_tensor(out=d, in0=d, scalar=1e-8, in1=d, op0=ALU.mult, op1=ALU.add))
                    link(v.reciprocal(r, d))
                else:
                    link(v.reciprocal(r, o[:, :, e]))
                return v.tensor_tensor(oN[:, par, :].rearrange("p (h e) -> p h e", e=e), o[:, :, 0:e],
                                       r.unsqueeze(2).to_broadcast([P, heads, e]), ALU.mult)

            def residual(l, t, done, src, scalar):
                link(v.scalar_tensor_tensor(out=x[:, t, :], in0=src, scalar=scalar, in1=x[:, t, :], op0=ALU.mult,
                                            op1=ALU.add))
                if l + 1 < NL:
                    link(v.bn_stats(st[:, t, :], x[:, t, :]))
                    v.bn_aggr(mv[:, t, :], st[:, t, :]).then_inc(ln_var, 1)
                if done is not None:
                    v.sem_inc(done, 1)

            a = A[0]
            v.wait_ge(s_x, 16)
            for t in range(NT):
                ln_stats(0, t)
                if t >= 2:
                    ln_norm(0, t - 2)
            for t in range(NT - 2, NT):
                ln_norm(0, t)
            v.wait_ge(s_rows, 16)
            biased(a, k_tok, 0, R("bk0"))
            v.wait_ge(s_cst, 4)
            values(a, Vp, 16, R("bv0"))
            normalize_0(a, k_tok, 0, R("gk0"))
            biased(a, q_tok, NT, R("bq0"))
            normalize_0(a, q_tok, NT, R("gq0"))
            v.wait_ge(s_tanh, 1)
            for s in range(NT + 4):
                t = s
                if t < NT:
                    for j in range(4):
                        v.wait_ge(a["sc_full"], 4 * t + j + 1)
                        if t >= 2 and j == 0:
                            v.wait_ge(a["pT_full"], 2 * (t - 1))
                        sc = ps[:, j, 0:D].rearrange("p (h s) -> p h s", s=S)
                        mj = mx[:, t % 2, 4 * j:4 * j + 4]
                        link(v.tensor_reduce(mj, sc, AX.X, ALU.max))
                        v.tensor_tensor(probs[:, t % 2, j * D:(j + 1) * D].rearrange("p (h s) -> p h s", s=S), sc,
                                        mj.unsqueeze(2).to_broadcast([P, 4, S]), ALU.subtract).then_inc(a["sc_free"], 1)
                t = s - 1
                if 0 <= t < NT:
                    v.wait_ge(a["pT_full"], 2 * t + 2)
                    v.tensor_copy(probs[:, t % 2, 1536:2048], ps[:, 5, :]).then_inc(a["pT_dve"], 1)
                t = s - 2
                if 0 <= t < NT:
                    v.wait_ge(a["pv_full"], t + 1)
                    head_norm(a, t, 6, 16, 16, False).then_inc(a["o_norm"], 1)
                t = s - 3
                if 0 <= t < NT:
                    v.wait_ge(a["o_proj"], t + 1)
                    link(v.tensor_tensor(junk[:, t % 2, :], ps[:, 7, D:2 * D], R("bo0"), ALU.add))
                    residual(0, t, a["resid"], junk[:, t % 2, :], gate(0))
                t = s - 4
                if 0 <= t:
                    ln_norm(1, t)
            def view(buf, e):
                return buf[:, 0:NT * e].rearrange("p (t e) -> p t e", t=NT)

            def over(small, e):
                return small.unsqueeze(2).to_broadcast([P, NT, e])

            def split(g, e, f):
                gv = g3[:, 0:NT * 3 * e].rearrange("p (t k e) -> p t k e", t=NT, k=3)
                r1, r2 = view(lc, e), view(la, e)
                link(v.tensor_copy(gv[:, :, 0, :], g))
                link(v.tensor_tensor(r1, g, gv[:, :, 0, :], ALU.subtract))
                link(v.tensor_copy(gv[:, :, 1, :], r1))
                link(v.tensor_tensor(r2, r1, gv[:, :, 1, :], ALU.subtract))
                v.tensor_copy(gv[:, :, 2, :], r2).then_inc(f["gates"], 1)

            def run_units(units, one):
                for k in range(4):
                    one(k, k, k)
                with v.Fori(1, units // 4) as i:
                    for k in range(4):
                        one(i * 4 + k, 4 + k, k)

            def piece_step(step, ap):
                w = ap.shape[-1]
                c, m, own = cr[:, 0:w], cm[:, 0:w], piece_own[:, 0:w]
                if step == 0:
                    ins = v.tensor_copy(own, ap)
                elif step == 1:
                    ins = v.tensor_scalar(c, own, 0.0, 1e4, ALU.max, ALU.min)
                elif step == 2:
                    ins = v.tensor_scalar(m, own, 0.0, 0.0, ALU.mult, ALU.not_equal)
                elif step == 3:
                    ins = v.scalar_tensor_tensor(out=c, in0=own, scalar=0.0, in1=c, op0=ALU.min, op1=ALU.add)
                elif step == 4:
                    ins = v.tensor_scalar(c, c, -1e4, None, ALU.max)
                elif step == 5:
                    ins = v.copy_predicated(own, m, c)
                else:
                    ins = v.tensor_copy(ap, own)
                ins.then_inc(s_piece, 1)

            def remainder(l, n, k):
                v.wait_ge(Fs[l]["h_hi"], n + 1)
                v.tensor_tensor(HL[:, k % 2, :], sbuf_h[:, k % 2, :], HH[l][:, k % 2, :], ALU.subtract).then_inc(
                    Fs[l]["h_lo"], 1)

            def ffn_residual(l, f, units):
                for t in range(NT + 1):
                    if t < NT:
                        if l in (3, 5):
                            v.wait_ge(f["y"], t // 2 + 1)
                        else:
                            v.wait_ge(f["down"], units - 1 + t // 4)
                        residual(l, t, None, ps[:, t // 2, (t % 2) * D:(t % 2 + 1) * D], gate(l))
                    if t >= 1:
                        ln_norm(l + 1, t - 1)

            f = Fs[1]
            v.wait_ge(f["logits"], 1)
            lgv, lav, lbv, lcv, ldv = (view(b_, E0) for b_ in (lg, la, lb, lc, ld))
            link(v.tensor_tensor(lgv, ps[:, 0, 0:NT * E0].rearrange("p (t e) -> p t e", t=NT),
                                 R("br0").unsqueeze(1).to_broadcast([P, NT, E0]), ALU.add))
            link(v.tensor_reduce(red[:, :], lgv, AX.X, ALU.max))
            v.tensor_tensor(lav, lgv, over(red[:, :], E0), ALU.subtract).then_inc(f["lread"], 1)
            v.wait_ge(f["lread"], 1)
            link(v.tensor_scalar(lcv, lav, 0.0, None, ALU.is_ge))
            link(v.tensor_tensor(ldv, lcv, R("first8").unsqueeze(1).to_broadcast([P, NT, E0]), ALU.mult))
            link(v.tensor_reduce(red2[:, :], ldv, AX.X, ALU.max))
            link(v.tensor_tensor(lcv, ldv, over(red2[:, :], E0), ALU.is_equal))
            v.wait_ge(f["e"], 1)
            link(v.tensor_reduce(vm[:, :], lbv, AX.X, ALU.add))
            link(v.reciprocal(red[:, :], vm[:, :]))
            link(v.tensor_scalar(red[:, :], red[:, :], 1.0 / R0, None, ALU.mult))
            link(v.tensor_tensor(ldv, lcv, over(red[:, :], E0), ALU.mult))
            split(ldv, E0, f)

            def one_1(n, low, k):
                v.wait_ge(f["act"], n + 1)
                v.wait_ge(f["cw"], n + 1)
                if low >= 2:
                    v.wait_ge(f["down"], n - 1)
                v.tensor_tensor(sbuf_h[:, k % 2, :], sbuf_s[:, k % 2, :], ps[:, 5 + 2 * (k % 2), :],
                                ALU.mult).then_inc(f["h"], 1)

            for n in range(FF[1]):
                one_1(n, n, n)
            v.wait_ge(s_misc, 16 * 6)
            link(v.tensor_copy(m32[:, :, :], m8[:, :, :]))
            link(v.tensor_reduce(vm[:, :], m32[:, :, :], AX.X, ALU.max))
            v.memset(cr[:, :], NEG * D ** 0.5)
            link(v.memset(probs[:, 0, 0:NT * P], 0.0))
            ffn_residual(1, f, FF[1])
            sv = cr[:, :].rearrange("p (t n) -> p t n", t=NT)
            for half in range(2):
                ts = slice(4 * half, 4 * half + 4)
                v.wait_ge(a2["sc_full"], half + 1)
                link(v.copy_predicated(sv[:, ts, :], m32[:, ts, :],
                                       ps[:, 4 + half, 0:4 * S].rearrange("p (t n) -> p t n", t=4)))
                link(v.tensor_reduce(red[:, ts], sv[:, ts, :], AX.X, ALU.max))
                v.tensor_tensor(sv[:, ts, :], sv[:, ts, :], red[:, ts].unsqueeze(2).to_broadcast([P, 4, S]),
                                ALU.subtract).then_inc(a2["shift"], 1)
            pd = probs[:, 0, 0:NT * P].rearrange("p (t n) -> p t n", t=NT)
            v.wait_ge(a2["p_ready"], 4)
            link(v.tensor_reduce(red2[:, :], pd, AX.X, ALU.add))
            link(v.reciprocal(red2[:, :], red2[:, :]))
            link(v.tensor_tensor(red2[:, :], red2[:, :], vm[:, :], ALU.mult))
            link(v.tensor_scalar(red2[:, :], red2[:, :], gate(2), None, ALU.mult))
            for t in range(NT + 1):
                if t < NT:
                    v.wait_ge(a2["pv_full"], t + 1)
                    residual(2, t, a2["resid"], ps[:, 4 + t % 2, 0:D], red2[:, t:t + 1])
                if t >= 1:
                    ln_norm(3, t - 1)
            f3 = Fs[3]
            EX = E1 + 8 - TOP1
            lc20, la20 = (b_[:, 0:NT * EX].rearrange("p (t e) -> p t e", t=NT) for b_ in (lc, la))
            lg17, ld24 = view(lg, E1 + 1), view(ld, EP1)
            lbv = view(lb, E1)
            t8 = top8[:, 0:NT * 8].rearrange("p (t e) -> p t e", t=NT)
            link(v.memset(lc20[:, :, E1:EX], BIG))
            v.wait_ge(f3["logits"], 1)
            v.tensor_copy(lg17, ps[:, 0, 0:NT * (E1 + 1)].rearrange("p (t e) -> p t e", t=NT)).then_inc(f3["lread"], 1)
            v.wait_ge(f3["lread"], 1)
            link(v.tensor_copy(lc20[:, :, 0:E1], lg17[:, :, 0:E1]))
            for t in range(NT):
                ins = v.max(t8[:, t, :], lc20[:, t, :])
            link(ins)
            v.tensor_tensor(lbv, lg17[:, :, 0:E1], over(t8[:, :, 8 - TOP1], E1), ALU.subtract).then_inc(f3["lread"], 1)
            for t in range(NT):
                ins = v.match_replace(out=la20[:, t, :], in_to_replace=t8[:, t, :], in_values=lc20[:, t, :],
                                      imm_value=-BIG)
            link(ins)
            link(v.tensor_tensor(la20, la20, lc20, ALU.not_equal))
            v.wait_ge(f3["e"], 2)
            link(v.tensor_tensor(lbv, lbv, la20[:, :, 0:E1], ALU.mult))
            link(v.tensor_reduce(red[:, :], lbv, AX.X, ALU.add))
            link(v.reciprocal(red[:, :], red[:, :]))
            link(v.memset(ld24[:, :, E1 + 1:EP1], 0.0))
            v.tensor_tensor(ld24[:, :, 0:E1], lbv, over(red[:, :], E1), ALU.mult)
            link(v.tensor_scalar(rk[:, 0:NT], rk[:, 0:NT], 1.0, None, ALU.add))
            link(v.reciprocal(ld24[:, :, E1], rk[:, 0:NT]))
            split(ld24, EP1, f3)

            def one_3(n, low, k, between=(), behind=()):
                v.wait_ge(f3["act"], n + 1)
                if low >= 1:
                    v.wait_ge(f3["h"], n)
                v.tensor_tensor(sbuf_t[:, k % 2, :], sbuf_s[:, k % 2, :], ps[:, 4 + (3 * k + 1) % 4, :],
                                ALU.mult).then_inc(f3["mid"], 1)
                v.wait_ge(f3["mid"], n + 1)
                v.wait_ge(f3["cw"], n + 1)
                if low >= 2:
                    v.wait_ge(f3["down"], n - 1)
                if between:
                    v.wait_ge(s_piece, between[0])
                v.tensor_tensor(sbuf_h[:, k % 2, :], sbuf_t[:, k % 2, :], ps[:, 4 + (3 * k + 2) % 4, :],
                                ALU.mult).then_inc(f3["h"], 1)
                if between:
                    piece_step(*between[1:])
                if behind:
                    v.wait_ge(s_piece, behind[0])
                remainder(3, n, k)
                if behind:
                    piece_step(*behind[1:])

            def group_3(i, piece, ap):
                for k in range(4):
                    def steps(w):
                        return (piece * STEPS + (w + 1), w, ap) if ap is not None else ()
                    one_3(i * 4 + k, 4 * i + k if isinstance(i, int) else 4 + k, k, steps(2 * k),
                          steps(2 * k + 1) if k < 3 else ())

            group_3(0, 0, None)
            v.wait_ge(A[4]["v_bias"], 16)
            v.sem_inc(s_piece, 1)
            with v.Fori(1, 9) as i:
                group_3(i, i - 1, vpair[:, bass.ds(i * HALF - HALF, HALF)])
            keys = xT[:, :, :].rearrange("p c n -> p (c n)")
            v.wait_ge(A[4]["kq_done"], 4)
            with v.Fori(9, 13) as i:
                group_3(i, i - 1, keys[:, bass.ds(i * HALF - 9 * HALF, HALF)])
            group_3(FF[3] // 4 - 1, PIECES - 1, vpair[:, 8 * HALF:B * 272])
            ffn_residual(3, f3, FF[3])
            a = A[4]
            link(v.tensor_scalar(hi2[:, :], mraw[:, :], 0.5, 400.0, ALU.is_gt, ALU.mult))
            link(v.tensor_scalar(hi2[:, :], hi2[:, :], -200.0, None, ALU.add))
            link(v.tensor_scalar(rs[:, :], R("rs2"), 0.0, 0.3, ALU.max, ALU.min))

            def clean_queries(g):
                half, c = g // 2, g % 2
                v.wait_ge(a["kq_done"], 4 + g + 1)
                if g >= 1:
                    v.wait_ge(a["q_ready"], g)
                clean(qT[:, c, half * HALF:(half + 1) * HALF], HALF).then_inc(a["q_ready"], 1)

            clean_queries(0)
            clean_queries(1)

            def x_lo_5(k):
                v.wait_ge(Fs[5]["x_hi"], k + 1)
                v.tensor_tensor(XL[5][:, :, 2 * k * P:2 * (k + 1) * P].rearrange("p c (t n) -> p t c n", t=2),
                                ps[:, k, :].rearrange("p (t c n) -> p t c n", t=2, c=KC),
                                XH[:, :, 2 * k * P:2 * (k + 1) * P].rearrange("p c (t n) -> p t c n", t=2),
                                ALU.subtract).then_inc(Fs[5]["x_lo"], 1)

            for s in range(NT + 4):
                t = s
                if t < NT:
                    v.wait_ge(a["sc_full"], t + 1)
                    if t >= 2:
                        v.wait_ge(a["pv_full"], t - 1)
                    for b in range(BT):
                        ins = v.tensor_scalar(
                            probs[:, t % 2, 0:1024].rearrange("p (j c b n) -> p j c b n", j=4, c=KC, b=BT)[:, :, :, b, :],
                            ps[:, 0:4, 0:D].rearrange("p j (c b n) -> p j c b n", c=KC, b=BT)[:, :, :, b, :],
                            hi2[:, BT * t + b:BT * t + b + 1], -200.0, ALU.min, ALU.max)
                    ins.then_inc(a["sc_free"], 1)
                    if t < 2:
                        clean_queries(2 + t)
                t = s - 1
                if 0 <= t < NT:
                    v.wait_ge(a["pv_full"], t + 1)
                    head_norm(a, t, 4 + t % 2, 16, 16, True).then_inc(a["o_norm"], 1)
                t = s - 2
                if 0 <= t < NT:
                    v.wait_ge(a["o_proj"], t + 1)
                    d = junk[:, t % 2, :]
                    link(v.tensor_tensor(d, ps[:, 6 + t % 2, D:2 * D], R("bo2"), ALU.add))
                    link(clean(d, D))
                    link(v.tensor_scalar(d, d, rs[:, 0:1], None, ALU.mult))
                    link(v.bn_stats(st[:, t, :], d))
                    v.bn_aggr(mv[:, t, :], st[:, t, :]).then_inc(a["dvar"], 1)
                t = s - 3
                if 0 <= t < NT:
                    d = junk[:, t % 2, :]
                    v.wait_ge(a["drstd"], t + 1)
                    link(v.tensor_scalar(d, d, mv[:, t, 0:1], rstd[:, t:t + 1], ALU.subtract, ALU.mult))
                    link(v.tensor_tensor(d, d, R("gamma2"), ALU.mult))
                    link(v.tensor_tensor(d, d, R("beta2"), ALU.add))
                    residual(4, t, a["resid"], d, gate(4))
                t = s - 4
                if 0 <= t:
                    ln_norm(5, t)
                if s >= NT + 2:
                    for k in range(2):
                        x_lo_5(2 * (s - NT - 2) + k)
            f5 = Fs[5]

            def one_5(n, low, k):
                v.wait_ge(f5["act"], n + 1)
                if low >= 2:
                    v.wait_ge(f5["down"], n - 1)
                v.tensor_tensor(sbuf_h[:, k % 2, :], sbuf_s[:, k % 2, :], ps[:, 5 + 2 * (k % 2), :],
                                ALU.mult).then_inc(f5["h"], 1)
                remainder(5, n, k)

            run_units(FF[5], one_5)
            ffn_residual(5, f5, FF[5])
            a = A[6]
            v.wait_ge(s_vq, 2)
            sums_6(a, 0)
            values(a, Vq, 8, None)
            normalize_6(a, k_tok, 0)
            sums_6(a, NT)

            def remainders(first, dst, tiles):
                for t in tiles:
                    v.wait_ge(a["hi"], first + t + 1)
                    v.tensor_tensor(dst[:, 1, :, tok(t)], ps[:, 4 + t % 4, 0:D].rearrange("p (c n) -> p c n", c=KC),
                                    dst[:, 0, :, tok(t)], ALU.subtract).then_inc(a["T_done"], 1)

            remainders(0, k16, range(NT))
            normalize_6(a, q_tok, NT)
            remainders(NT, q16, range(4))
            v.wait_ge(a["T_done"], NT)
            mask_keys(0, lambda o, i, scale: v.tensor_scalar(o, i, scale, None, ALU.mult), a["masked"])
            remainders(NT, q16, range(4, NT))
            for t in range(NT + 1):
                if t < NT:
                    v.wait_ge(a["pv_full"], t + 1)
                    link(head_norm(a, t, 4 + t % 2, 32, 8, False))
                    v.sem_inc(a["o_norm"], 1)
                    residual(6, t, None, oN[:, t % 2, :], gate(6))
                if t >= 1:
                    ln_norm(7, t - 1)
            f7, f8 = Fs[7], Fs[8]
            sig, sbv, mk, rep = la, lg, lc, ld
            v.wait_ge(f7["e"], 1)
            link(v.tensor_scalar(lb[:, :], lb[:, :], 1.0, None, ALU.add))
            link(v.reciprocal(sig[:, :], lb[:, :]))
            link(v.tensor_tensor(view(sbv, E3), view(sig, E3), R("bias3").unsqueeze(1).to_broadcast([P, NT, E3]),
                                 ALU.add))
            for g in range(NT * G3):
                ins = v.max(top8[:, g * 8:g * 8 + 8], sbv[:, g * 8:g * 8 + 8])
            link(ins)
            for half in range(2):
                v.wait_ge(s_latE, half + 1)
                r = slice(half * HALF, (half + 1) * HALF)
                v.tensor_tensor(qT_r[:, 1, r], ps[:, 2 + half, :], qT_r[:, 0, r], ALU.subtract).then_inc(Fs[5]["x_lo"], 1)
            tops = top8[:, :].rearrange("p (g e) -> p g e", e=8)
            link(v.tensor_tensor(gsc[:, :], tops[:, :, 0], tops[:, :, 1], ALU.add))
            gs = gsc[:, :].rearrange("p (t g) -> p t g", t=NT)
            other = gs.unsqueeze(2).to_broadcast([P, NT, G3, G3])
            own = gs.unsqueeze(3).to_broadcast([P, NT, G3, G3])
            r4, r4b = (b_[:, :].rearrange("p (t g o) -> p t g o", t=NT, g=G3) for b_ in (rk, rk2))
            v.tensor_tensor(r4, other, own, ALU.is_gt)
            link(v.tensor_tensor(r4b, other, own, ALU.is_equal))
            link(v.tensor_tensor(rk2[:, :].rearrange("p (t n) -> p t n", t=NT), rk2[:, :].rearrange("p (t n) -> p t n", t=NT),
                                 R("lower4").unsqueeze(1).to_broadcast([P, NT, G3 * G3]), ALU.mult))
            link(v.tensor_tensor(rk[:, :], rk[:, :], rk2[:, :], ALU.add))
            link(v.tensor_reduce(gsd[:, :], rk[:, :].rearrange("p (g o) -> p g o", o=G3), AX.X, ALU.add))
            link(v.tensor_scalar(gsd[:, :], gsd[:, :], TOPG3 - 0.5, None, ALU.is_lt))
            link(v.tensor_scalar(gsc[:, :], gsd[:, :], -NEG, NEG, ALU.mult, ALU.add))

            def by_group(buf):
                return buf[:, :].rearrange("p (g e) -> p g e", e=8)

            link(v.tensor_tensor(by_group(mk), by_group(sbv), gsd[:, :].unsqueeze(2).to_broadcast([P, NT * G3, 8]), ALU.mult))
            link(v.tensor_tensor(by_group(mk), by_group(mk), gsc[:, :].unsqueeze(2).to_broadcast([P, NT * G3, 8]), ALU.add))
            for t in range(NT):
                ins = v.max(top8[:, t * 8:t * 8 + 8], mk[:, t * E3:(t + 1) * E3])
            link(ins)
            for t in range(NT):
                ins = v.match_replace(out=rep[:, t * E3:(t + 1) * E3], in_to_replace=top8[:, t * 8:t * 8 + 8],
                                      in_values=mk[:, t * E3:(t + 1) * E3], imm_value=-BIG)
            link(ins)
            link(v.tensor_tensor(rep[:, :], rep[:, :], mk[:, :], ALU.not_equal))
            link(v.tensor_tensor(lb[:, :], sig[:, :], rep[:, :], ALU.mult))
            link(v.tensor_reduce(red[:, :], view(lb, E3), AX.X, ALU.add))
            link(v.reciprocal(red[:, :], red[:, :]))
            link(v.tensor_scalar(red[:, :], red[:, :], SCALE3, None, ALU.mult))
            link(v.tensor_tensor(view(ld, E3), view(lb, E3), over(red[:, :], E3), ALU.mult))
            split(view(ld, E3), E3, f7)

            for t in range(NT):
                v.wait_ge(f8["down"], FF[8] - 1 + t // 4)
                residual(7, t, f8["resid"], ps[:, t // 2, (t % 2) * D:(t % 2 + 1) * D], gate(7))

            def hidden_lo_7(n, k):
                v.wait_ge(Fs[5]["h_hi"], n + (FF[5] + 1))
                v.tensor_tensor(H7[1][:, k, :], H7[0][:, k, :], HH7[:, k, :], ALU.subtract).then_inc(Fs[5]["h_lo"], 1)

            def group_7(base, first):
                for k in range(4):
                    n = base + k
                    v.wait_ge(f7["sq"], n + 1)
                    v.wait_ge(f7["cw"], n + 1)
                    if not first:
                        v.wait_ge(f7["down"], n - 3)
                    v.tensor_tensor(H7[0][:, k, :], sbuf_t[:, k % 2, :], ps[:, 2 + k % 2, :], ALU.mult).then_inc(f7["h"], 1)
                    if not (first and k < 1):
                        hidden_lo_7(base + (k - 1), (k - 1) % 4)

            group_7(0, True)
            with v.Fori(1, FF[7] // 4) as i:
                group_7(i * 4, False)
            hidden_lo_7(FF[7] - 1, 3)
            for t in range(NT):
                v.wait_ge(f8["down"], FF[8] + t // 2 + 1)
                residual(7, t, f8["resid"], ps[:, t // 2, (t % 2) * D:(t % 2 + 1) * D], gate(7))



def kernel(**inputs):
    import ml_dtypes
    import concourse.bacc as _bacc
    from concourse.bass_utils import run_bass_kernel_spmd as _run

    a = {k: np.asarray(v) for k, v in inputs.items()}
    f = np.float32

    def tiles(v):
        return v.reshape(NT, P, D).transpose(1, 0, 2)

    def wT(w):
        return w.T.reshape(-1, P, w.shape[0]).transpose(1, 0, 2).reshape(P, -1)

    def row(v):
        return v.reshape(1, -1)

    def even_odd(v, e):
        return np.moveaxis(v.reshape(*v.shape[:-1], D // 2 // e, 2, e), -2, -3).reshape(v.shape)

    first8 = np.arange(E0, 0, -1, dtype=f)
    lower4 = np.tril(np.ones((G3, G3), f), -1)
    rows_d = dict(bq0=a["L0_xattn_b_q"], bk0=a["L0_xattn_b_k_img"], bv0=even_odd(a["L0_xattn_b_v_img"], 16), bo0=a["L0_xattn_b_o"],
                  gq0=a["L0_xattn_g_q"], gk0=a["L0_xattn_g_k_img"], br0=a["L0_ffn_br"], bv2=even_odd(a["L2_xattn_bv"], 16),
                  bo2=a["L2_xattn_bo"], gamma2=a["L2_xattn_ln_gamma"], beta2=a["L2_xattn_ln_beta"],
                  bias3=a["L3_ffn_gate_bias"], rs2=a["L2_xattn_residual_scale"],
                  gates=np.concatenate([a["g_xattn"], a["g_ffn"]]), first8=first8, lower4=lower4)
    rows = np.concatenate([row(rows_d[n]) for n, _ in ROWS], 1)

    part = np.arange(P)
    pair = (part[:, None] // 16 % 2 == np.arange(2)).astype(f)
    quad = (part[:, None] // 8 % 4 == np.arange(4)).astype(f)
    early_d = dict(wk0=wT(a["L0_xattn_w_k_img"]), wq0=wT(a["L0_xattn_w_q"]), wv0=wT(even_odd(a["L0_xattn_w_v_img"].T, 16).T),
                   wo0=wT(a["L0_xattn_w_o"]), ident=np.eye(P, dtype=f), pair=pair, quad=quad)
    early = np.concatenate([early_d[n] for n, _ in EARLY], 1)

    had = np.ones((1, 1), f)
    while had.shape[0] < P:
        had = np.block([[had, had], [had, -had]])
    kv3 = np.concatenate([a["L3_xattn_Wk"], a["L3_xattn_Wv"]])
    col = lambda b: b.reshape(KC, P).T
    late_d = dict(
        A0=wT(a["L0_ffn_A"].reshape(E0 * R0, D)), B0=wT(a["L0_ffn_B"].transpose(1, 0, 2).reshape(D, E0 * R0)),
        wr0=wT(a["L0_ffn_Wr"]), gate1=wT(np.concatenate([a["L1_ffn_gate_w"], a["L1_ffn_shared_gate_vec"]])),
        wk2=wT(a["L2_xattn_Wk"]), wq2=wT(a["L2_xattn_Wq"]), wv2=wT(even_odd(a["L2_xattn_Wv"].T, 16).T), wo2=wT(a["L2_xattn_Wo"]),
        bqk2=np.concatenate([col(a["L2_xattn_bq"]), col(a["L2_xattn_bk"])], 1),
        had=had, w2f=wT(a["L2_ffn_W2"]), wk3=wT(kv3[0::2]), wq3=wT(a["L3_xattn_Wq"]), wv3=wT(even_odd(kv3[1::2].T, 8).T),
        gate3=wT(a["L3_ffn_gate_w"]), fc1=wT(a["L3_ffn_fc1_w"]), fc2=wT(a["L3_ffn_fc2_w"]),
        up3=a["L3_ffn_shared_up_w"].reshape(C3S, P, KC, P).transpose(3, 0, 2, 1).reshape(P, -1),
        down3=wT(a["L3_ffn_shared_down_w"]))
    late = np.concatenate([late_d[n] for n, _ in LATE], 1)

    gu = a["L1_ffn_expert_gate_up"]
    sgu = a["L1_ffn_shared_gate_up"]
    pad = np.zeros((C1 * P - E1 * I1 - SI1, D), f)
    g_rows = np.concatenate([gu[:, :I1].reshape(-1, D), sgu[:SI1], pad])
    u_rows = np.concatenate([gu[:, I1:].reshape(-1, D), sgu[SI1:], pad])
    d_rows = np.concatenate([a["L1_ffn_expert_down"].transpose(0, 2, 1).reshape(-1, D), a["L1_ffn_shared_down"].T, pad])

    def chunks_up(g, u, n):
        both = np.stack([g.reshape(n, P, KC, P), u.reshape(n, P, KC, P)])
        return both.transpose(1, 4, 3, 0, 2).reshape(n, P, KC * 2 * P)

    w1 = np.concatenate([chunks_up(g_rows, u_rows, C1), d_rows.reshape(C1, P, D)], 2)
    w2 = chunks_up(a["L2_ffn_W1"], a["L2_ffn_W3"], C2)
    w3 = np.stack([a["L3_ffn_w1"].transpose(0, 2, 1), a["L3_ffn_w2"].transpose(0, 2, 1)])
    w3 = w3.reshape(2, E3 // 2, 2, P, P).transpose(1, 3, 0, 2, 4).reshape(E3 // 2, P, 4 * P)

    def selector(expert_of, e):
        one = (expert_of[None, :] == np.arange(e)[:, None])
        return np.concatenate([one] * 3).astype(ml_dtypes.bfloat16)

    h1 = np.arange(C1 * P)
    e1 = np.where(h1 < E1 * I1, h1 // I1, E1)
    mask1 = a["mask_BxS2_bk0"].reshape(NT, BT, 1, S).repeat(S, 2).reshape(NT, P, S).transpose(1, 0, 2)
    mask2 = np.tile(a["mask_BxS2_ik0"].T, (2, 1))
    arrays = dict(
        x_dram=tiles(a["x"]), ctx_dram=tiles(a["ctx_2048"]),
        ctxT_dram=a["ctx_2048"].reshape(TOK, KC, P).transpose(2, 1, 0), rows_dram=rows, early_dram=early,
        late_dram=late, w1_dram=w1, w2_dram=w2, w3_dram=w3, mask1_dram=mask1, mask2_dram=mask2,
        identb_dram=np.eye(P, dtype=ml_dtypes.bfloat16), sel0_dram=selector(np.arange(E0 * R0) // R0, E0),
        sel1_dram=selector(e1, EP1), sel3_dram=selector(np.arange(E3 * P) // P, E3))
    arrays = {k: np.ascontiguousarray(v) for k, v in arrays.items()}

    nc = _bacc.Bacc("TRN2", target_bir_lowering=False, num_devices=1)
    args = [nc.dram_tensor(k, v.shape, U8 if v.dtype == bool else mybir.dt.from_np(v.dtype), kind="ExternalInput").ap() for k, v in arrays.items()]
    args.append(nc.dram_tensor("out_dram", (P, NT, D), F32, kind="ExternalOutput").ap())
    flamingo_kernel(nc, *args)
    r = _run(nc, [arrays], core_ids=[0])
    return r.results[0]["out_dram"].transpose(1, 0, 2).reshape(B, S, D)
```
